# Optimizing a Trainium2 kernel written in Bass

```python
import numpy as np
import jax
import jax.numpy as jnp

def _softmax(x, axis=-1):
    return jax.nn.softmax(x, axis=axis)

def _gelu(x):
    return jax.nn.gelu(x, approximate=True)

def _silu(x):
    return jax.nn.silu(x)

def _sigmoid(x):
    return jax.nn.sigmoid(x)

def _layernorm(x, axis=-1, eps=1e-05):
    m = jnp.mean(x, axis=axis, keepdims=True)
    v = jnp.var(x, axis=axis, keepdims=True)
    return (x - m) / jnp.sqrt(v + eps)

def _scatter_add(tgt, idx, src, axis=0):
    return tgt.at[idx].add(src)

def _segment_sum(src, seg, n):
    return jax.ops.segment_sum(src, seg, n)
kernel_name = 'mk_decoder_preln_d1_seqx_r4_cb4aee'

def setup_inputs(seed: int=0):
    np.random.seed(seed)
    _w = jnp.asarray

    def _rec_inputs():
        import jax
        import jax.numpy as jnp
        _rk = jax.random.key(seed)
        x = -0.0003929 + 0.9999 * jax.random.normal(jax.random.fold_in(_rk, 1), (32, 128, 256), jnp.float32)
        _lenS = 128 - jax.random.randint(jax.random.fold_in(_rk, 7), (32,), 0, max(1, 128 // 4) + 1, jnp.int32)
        _lenS2 = 128 - jax.random.randint(jax.random.fold_in(_rk, 8), (32,), 0, max(1, 128 // 4) + 1, jnp.int32)
        _ctx_512P = jax.random.normal(jax.random.fold_in(_rk, 11), (32, 16, 128), jnp.float32)
        _ctx_512c = jax.random.dirichlet(jax.random.fold_in(_rk, 511), 0.3 * jnp.ones((16,), jnp.float32), (32, 128))
        _ctx_512t = jnp.einsum('bsk,bkd->bsd', _ctx_512c, _ctx_512P)
        _ctx_512t = _ctx_512t * jax.lax.rsqrt(jnp.mean(jnp.square(_ctx_512t)) + 1e-12) * 0.953939
        ctx_512 = 4.13588e-05 + 0.999923 * (_ctx_512t + 0.3 * jax.random.normal(jax.random.fold_in(_rk, 611), (32, 128, 128), jnp.float32))
        return (x, ctx_512)
    x, ctx_512 = _rec_inputs()

    def _L0_attn_setup():
        import jax, jax.numpy as jnp
        import numpy as np
        D_MODEL = 256
        EXPAND = 2
        D_INNER = D_MODEL * EXPAND
        D_STATE = 16
        D_CONV = 4
        B, T = (4, 512)
        key = jax.random.key(seed)
        ks = jax.random.split(key, 8)
        s = 0.02
        return {'x': jax.random.normal(ks[0], (B, T, D_MODEL), jnp.float32), 'in_proj_w': jax.random.normal(ks[1], (2 * D_INNER, D_MODEL), jnp.float32) * s, 'conv_w': jax.random.normal(ks[2], (D_INNER, 1, D_CONV), jnp.float32) * s, 'conv_b': jnp.zeros((D_INNER,), jnp.float32), 'x_proj_w': jax.random.normal(ks[3], (2 * D_STATE, D_INNER), jnp.float32) * s, 'dt_proj_w': jax.random.normal(ks[4], (D_INNER, D_STATE), jnp.float32) * s, 'dt_proj_b': jnp.zeros((D_INNER,), jnp.float32), 'D_param': jnp.ones((D_INNER,), jnp.float32), 'out_proj_w': jax.random.normal(ks[5], (D_MODEL, D_INNER), jnp.float32) * s}
    _L0_attn_all = _L0_attn_setup()
    _L0_attn_in = {k: v for k, v in _L0_attn_all.items() if k in ('in_proj_w', 'conv_w', 'conv_b', 'x_proj_w', 'dt_proj_w', 'dt_proj_b', 'D_param', 'out_proj_w')}
    del _L0_attn_all

    def _L0_xattn_setup():
        import jax, jax.numpy as jnp
        import numpy as np
        B, LQ, LK = (8, 512, 512)
        QD, KD, VD = (256, 128, 128)
        key = jax.random.key(seed)
        ks = jax.random.split(key, 9)
        s = 0.02
        return {'query': jax.random.normal(ks[0], (B, LQ, QD), jnp.float32), 'key': jax.random.normal(ks[1], (B, LK, KD), jnp.float32), 'value': jax.random.normal(ks[2], (B, LK, VD), jnp.float32), 'Wq': jax.random.normal(ks[3], (QD, QD), jnp.float32) * s, 'bq': jnp.zeros((QD,), jnp.float32), 'Wk': jax.random.normal(ks[4], (KD, QD), jnp.float32) * s, 'bk': jnp.zeros((QD,), jnp.float32), 'Wv': jax.random.normal(ks[5], (VD, QD), jnp.float32) * s, 'bv': jnp.zeros((QD,), jnp.float32)}
    _L0_xattn_all = _L0_xattn_setup()
    _L0_xattn_in = {k: v for k, v in _L0_xattn_all.items() if k in ('Wq', 'bq', 'Wk', 'bk', 'Wv', 'bv')}
    del _L0_xattn_all

    def _L0_ffn_setup():
        import jax, jax.numpy as jnp
        import numpy as np
        E, D, F = (8, 256, 1024)
        LN_EPS = 1e-05
        key = jax.random.key(seed)
        k = jax.random.split(key, 8)
        x = jax.random.normal(k[0], (4, 512, D), jnp.float32)
        centroids = jax.random.normal(k[1], (E, D), jnp.float32) * 0.1
        ln_g = jnp.ones((E, D), jnp.float32)
        ln_b = jnp.zeros((E, D), jnp.float32)
        w1 = jax.random.normal(k[2], (E, F, D), jnp.float32) * (1.0 / np.sqrt(D))
        b1 = jnp.zeros((E, F), jnp.float32)
        w2 = jax.random.normal(k[3], (E, D, F), jnp.float32) * (1.0 / np.sqrt(F))
        b2 = jnp.zeros((E, D), jnp.float32)
        return {'input_features': x, 'centroids': centroids, 'ln_g': ln_g, 'ln_b': ln_b, 'w1': w1, 'b1': b1, 'w2': w2, 'b2': b2}
    _L0_ffn_all = _L0_ffn_setup()
    _L0_ffn_in = {k: v for k, v in _L0_ffn_all.items() if k in ('centroids', 'ln_g', 'ln_b', 'w1', 'b1', 'w2', 'b2')}
    del _L0_ffn_all
    return {'x': x, 'ctx_512': ctx_512, 'L0_attn_in_proj_w': _L0_attn_in['in_proj_w'], 'L0_attn_conv_w': _L0_attn_in['conv_w'], 'L0_attn_conv_b': _L0_attn_in['conv_b'], 'L0_attn_x_proj_w': _L0_attn_in['x_proj_w'], 'L0_attn_dt_proj_w': _L0_attn_in['dt_proj_w'], 'L0_attn_dt_proj_b': _L0_attn_in['dt_proj_b'], 'L0_attn_D_param': _L0_attn_in['D_param'], 'L0_attn_out_proj_w': _L0_attn_in['out_proj_w'], 'L0_xattn_Wq': _L0_xattn_in['Wq'], 'L0_xattn_bq': _L0_xattn_in['bq'], 'L0_xattn_Wk': _L0_xattn_in['Wk'], 'L0_xattn_bk': _L0_xattn_in['bk'], 'L0_xattn_Wv': _L0_xattn_in['Wv'], 'L0_xattn_bv': _L0_xattn_in['bv'], 'L0_ffn_centroids': _L0_ffn_in['centroids'], 'L0_ffn_ln_g': _L0_ffn_in['ln_g'], 'L0_ffn_ln_b': _L0_ffn_in['ln_b'], 'L0_ffn_w1': _L0_ffn_in['w1'], 'L0_ffn_b1': _L0_ffn_in['b1'], 'L0_ffn_w2': _L0_ffn_in['w2'], 'L0_ffn_b2': _L0_ffn_in['b2']}

def reference(x, ctx_512, L0_attn_in_proj_w, L0_attn_conv_w, L0_attn_conv_b, L0_attn_x_proj_w, L0_attn_dt_proj_w, L0_attn_dt_proj_b, L0_attn_D_param, L0_attn_out_proj_w, L0_xattn_Wq, L0_xattn_bq, L0_xattn_Wk, L0_xattn_bk, L0_xattn_Wv, L0_xattn_bv, L0_ffn_centroids, L0_ffn_ln_g, L0_ffn_ln_b, L0_ffn_w1, L0_ffn_b1, L0_ffn_w2, L0_ffn_b2):
    import jax
    import jax.numpy as jnp

    def _L0_attn_ref(x, in_proj_w, conv_w, conv_b, x_proj_w, dt_proj_w, dt_proj_b, D_param, out_proj_w):
        import jax, jax.numpy as jnp
        import numpy as np
        D_MODEL = 256
        EXPAND = 2
        D_INNER = D_MODEL * EXPAND
        D_STATE = 16
        D_CONV = 4
        B, T = (4, 512)
        Bsz, Tlen, _ = x.shape
        xz = jnp.einsum('btd,ed->bte', x, in_proj_w)
        x_inner, z = jnp.split(xz, 2, axis=-1)
        xc = jnp.transpose(x_inner, (0, 2, 1))
        xc = jax.lax.conv_general_dilated(xc, conv_w, window_strides=(1,), padding=[(D_CONV - 1, 0)], feature_group_count=D_INNER)
        xc = xc + conv_b[None, :, None]
        x_conv = jax.nn.silu(jnp.transpose(xc, (0, 2, 1)))
        x_ssm = jnp.einsum('btd,ed->bte', x_conv, x_proj_w)
        B_ssm, C_ssm = jnp.split(x_ssm, 2, axis=-1)
        dt = jax.nn.softplus(jnp.einsum('btn,dn->btd', B_ssm, dt_proj_w) + dt_proj_b)
        alpha = jax.nn.sigmoid(jnp.mean(dt, axis=-1, keepdims=True))

        def step(h, inp):
            a, xt = inp
            h = a * h + (1.0 - a) * xt
            return (h, h)
        aT = jnp.transpose(alpha, (1, 0, 2))
        xT = jnp.transpose(x_conv, (1, 0, 2))
        h0 = jnp.zeros((Bsz, D_INNER), x.dtype)
        _, ys = jax.lax.scan(step, h0, (aT, xT))
        y = jnp.transpose(ys, (1, 0, 2))
        y = y * D_param + x_conv
        y = y * jax.nn.silu(z)
        out = jnp.einsum('btd,ed->bte', y, out_proj_w)
        return out

    def _L0_xattn_ref(query, key, value, Wq, bq, Wk, bk, Wv, bv):
        import jax, jax.numpy as jnp
        import numpy as np
        B, LQ, LK = (8, 512, 512)
        QD, KD, VD = (256, 128, 128)
        q = jnp.einsum('bld,de->ble', query, Wq) + bq
        k = jnp.einsum('bld,de->ble', key, Wk) + bk
        v = jnp.einsum('bld,de->ble', value, Wv) + bv
        scores = jnp.einsum('bqe,bke->bqk', q, k)
        attn = jax.nn.softmax(scores, axis=-1)
        out = jnp.einsum('bqk,bke->bqe', attn, v)
        return out

    def _L0_ffn_ref(input_features, centroids, ln_g, ln_b, w1, b1, w2, b2):
        import jax, jax.numpy as jnp
        import numpy as np
        E, D, F = (8, 256, 1024)
        LN_EPS = 1e-05
        x = input_features.reshape(-1, D)
        aff = jax.lax.stop_gradient(x) @ centroids.T
        assign = jnp.argmax(aff, axis=1)
        onehot = jax.nn.one_hot(assign, E, dtype=x.dtype)
        mu = jnp.mean(x, axis=-1, keepdims=True)
        var = jnp.mean((x - mu) ** 2, axis=-1, keepdims=True)
        xhat = (x - mu) * jax.lax.rsqrt(var + LN_EPS)
        xn = xhat[None, :, :] * ln_g[:, None, :] + ln_b[:, None, :]
        h = jax.nn.relu(jnp.einsum('etd,efd->etf', xn, w1) + b1[:, None, :])
        y = x[None, :, :] + jnp.einsum('etf,edf->etd', h, w2) + b2[:, None, :]
        alpha = jax.nn.sigmoid(x @ centroids.T)
        a = alpha.T[:, :, None]
        gated = a * y + (1.0 - a) * x[None, :, :]
        out = jnp.einsum('te,etd->td', onehot, gated)
        return out.reshape(input_features.shape)
    x = x + _L0_attn_ref(_layernorm(x, axis=-1), L0_attn_in_proj_w, L0_attn_conv_w, L0_attn_conv_b, L0_attn_x_proj_w, L0_attn_dt_proj_w, L0_attn_dt_proj_b, L0_attn_D_param, L0_attn_out_proj_w)
    x = x + _L0_xattn_ref(_layernorm(x, axis=-1), ctx_512, ctx_512, L0_xattn_Wq, L0_xattn_bq, L0_xattn_Wk, L0_xattn_bk, L0_xattn_Wv, L0_xattn_bv)
    x = x + _L0_ffn_ref(_layernorm(x, axis=-1), L0_ffn_centroids, L0_ffn_ln_g, L0_ffn_ln_b, L0_ffn_w1, L0_ffn_b1, L0_ffn_w2, L0_ffn_b2)
    return x

_drawn_inputs = setup_inputs


def setup_inputs(seed=0):
    import zlib

    import numpy as np

    out = dict(_drawn_inputs(seed))
    spreads = {'L0_attn_conv_b': (0.0, 0.278),
     'L0_attn_dt_proj_b': (0.0, 2.0),
     'L0_attn_D_param': (1.0, 0.6),
     'L0_xattn_bq': (0.0, 0.1),
     'L0_xattn_bk': (0.0, 2.0),
     'L0_xattn_bv': (0.0, 0.1),
     'L0_ffn_ln_g': (1.0, 0.2),
     'L0_ffn_ln_b': (0.0, 0.274),
     'L0_ffn_b1': (0.0, 0.269),
     'L0_ffn_b2': (0.0, 0.1)}
    factors = {'L0_attn_conv_w': 8.0, 'L0_attn_x_proj_w': 200.0, 'L0_attn_dt_proj_w': 200.0}
    for name, (base, spread) in spreads.items():
        noise = np.random.default_rng([zlib.crc32(name.encode()), seed]).standard_normal(out[name].shape)
        drawn = base * np.exp(spread * noise) if base else spread * noise
        out[name] = jnp.asarray(drawn.astype(out[name].dtype))
    for name, factor in factors.items():
        out[name] = (out[name] * factor).astype(out[name].dtype)
    return out
```

```python
from contextlib import ExitStack

import concourse.bass as bass
from concourse import mybir

F32 = mybir.dt.float32
I32 = mybir.dt.int32
ALU = mybir.AluOpType
ACT = mybir.ActivationFunctionType
X = mybir.AxisListType.X

P = 128
EPS = 1e-5


def decoder_program(nc, x, ctx, ctx_t, in_w_t, dt_w_t, dt_b, out_w_t, wq_t, wk_t, wv, bv, lane_w,
                    w1_t, w2_t, b2, out):
    NB, T, D = x.shape
    C = ctx.shape[2]
    DI = out_w_t.shape[0]
    NS = dt_w_t.shape[0]
    E, _, F = w1_t.shape
    assert T == P and C == P
    KD, KI, KF = D // P, DI // P, F // P
    GB = 4
    G = NB // GB
    GT = GB * T
    TILES = NB
    SLOTS = TILES + E - 1
    RING = 6
    SP_ = 40
    assert SLOTS <= SP_ and G % 2 == 0 and SLOTS % 2 == 1

    rows_dram = nc.dram_tensor("token_rows", (NB * T, 2 * D), F32, kind="Internal").ap()

    with ExitStack() as stack:
        def sb(name, cols, dt=F32):
            return stack.enter_context(nc.sbuf_tensor(name, [P, cols], dt))

        def sem(name):
            return stack.enter_context(nc.semaphore(name))

        def split(ap, n):
            return ap.rearrange("p (n w) -> p n w", n=n)

        bank = [stack.enter_context(nc.psum_tensor(f"bank{i}", [P, 512], F32)) for i in range(8)]

        w1_sb = sb("w1_sb", E * KD * F)
        w2_sb = sb("w2_sb", E * KF * D)
        x_flat = sb("x_flat", NB * D)
        arena = sb("arena", 10240)
        w1v = w1_sb[:, :].rearrange("p (e k f) -> p e k f", e=E, k=KD)
        w2v = w2_sb[:, :].rearrange("p (e k d) -> p e k d", e=E, k=KF)
        x_res = split(x_flat[:, :], NB)

        ident = sb("ident", P)
        ones = sb("ones", P)
        before = sb("before", P)
        small = sb("small", 256)
        cols = [0]

        def piece(n):
            a = cols[0]
            cols[0] += n
            return small[:, a:a + n]

        neg_d = piece(KI)
        q_bias = piece(1)
        bk_proj = piece(KD)
        bq_bk = piece(1)
        shift = piece(GB)
        att_top = piece(GB)
        mhalf = piece(GB)
        relu_sum, ln_sum, sp_sum, exp_a, exp_a1, alpha = (piece(GB) for _ in range(6))
        att_max, att_neg, att_sum, att_rcp = (piece(GB) for _ in range(4))
        ln_tmp = [(split(piece(6 * GB), GB), split(piece(2 * GB), GB), piece(GB), piece(GB)) for _ in range(4)]
        assert cols[0] <= 256
        affs = split(sb("affs", TILES * E)[:, :], TILES)

        def take(ap, spots):
            out_, at = {}, 0
            for name, n in spots:
                out_[name] = ap[:, at:at + n]
                at += n
            assert at <= ap.shape[1], (at, ap.shape)
            return out_

        lane_parts = [("conv_w", 4 * KI), ("conv_b", KI), ("d", KI), ("xp", KI * NS), ("bq", KD), ("bk", KD),
                      ("cent", KD * E), ("ln_g", KD * E), ("ln_b", KD * E), ("b1", E * KF)]
        lane_sb = sb("lane_sb", sum(n for _, n in lane_parts))
        L = take(lane_sb[:, :], lane_parts)
        conv_w_sb, conv_b_sb, d_sb, xpw_sb = split(L["conv_w"], KI), L["conv_b"], L["d"], split(L["xp"], KI)
        bq_sb, bk_sb, cent_sb = L["bq"], L["bk"], split(L["cent"], KD)

        A = take(w2_sb[:, :], [("xn", GB * D), ("xnT", KD * GT), ("xc", KI * GT), ("th", 2048), ("xs", KI * GT),
                               ("gz0", KI * GT), ("gz1", KI * GT), ("u", KI * GT), ("as", GT)])
        A["yv"] = w1_sb[:, 0:KI * GT]
        A["sp"] = w1_sb[:, 2048:4096]
        A["diag"] = w1_sb[:, 4608:5120]
        A["bT"] = w1_sb[:, 5120:5632]
        A["thz"] = w1_sb[:, 5632:7680]
        A["stage"] = w1_sb[:, 7680:7680 + GB * D]
        B = take(arena[:, :], [("row", GB * 2 * D), ("xlT", KD * GT), ("pr", GT), ("xn", GB * D), ("xnT", KD * GT),
                               ("q", GT), ("prT", GT), ("gT", GT), ("cT", GT), ("c", GT), ("xl", GB * D),
                               ("wk", KD * C), ("wqk", KD * C), ("wv", D), ("bv", D)])
        inw_sb = split(B["row"], KD)
        outw_sb = split(B["xlT"], KI)
        dtw_sb = B["pr"]
        Dm = take(arena[:, :], [("rows", RING * 2 * D), ("xT", KD * P), ("h", F), ("hT0", F), ("hT1", F),
                                ("o", 3 * D), ("b2", E * D)])
        b2_sb = split(Dm["b2"], E)
        Cm = take(x_flat[:, :], [("lo_hot", TILES * P), ("hi_hot", TILES * SP_), ("hi_val", TILES * 2 * SP_)])
        Rm = take(arena[:, 3584:5632], [("max", TILES), ("eq", TILES * E), ("cand", TILES * E), ("first", TILES),
                             ("hot", TILES * E), ("tot", TILES * E), ("pos", TILES), ("hi", TILES),
                             ("lo", TILES), ("ealpha", TILES)])
        slot_alpha = sb("slot_alpha", SP_)[:, :]
        routing_tmp = sb("routing_tmp", 3 * E)[:, :]
        iotas = sb("iotas", E + 2 * TILES + P + SP_)
        Im = take(iotas[:, :], [("e8", E), ("k128", TILES), ("lane", P), ("slot", SP_), ("tok", TILES)])
        gather_cols, scatter_cols = sb("gather_cols", RING, I32), sb("scatter_cols", 3, I32)
        gather_col = [gather_cols[:, k:k + 1] for k in range(RING)]
        scatter_col = [scatter_cols[:, k:k + 1] for k in range(3)]
        idx = sb("idx", 4 * TILES + 3 * SP_, I32)
        pos_i, hi_i, lo_i = (idx[:, k * TILES:(k + 1) * TILES] for k in range(3))
        gather_i, scatter_i, expert_i = (idx[:, 4 * TILES + k * SP_:4 * TILES + (k + 1) * SP_] for k in range(3))

        names = """staged_0 staged_1 ld_x01 ld_x ld_wa ld_wb ld_ct ld_c ld_w1 ld_w2 ld_b2
            ident_set consts_set fills_set neg_d_set
            a_transposed a_xnT_ready a_z_done a_tanh_z a_gate_ready a_x_done a_first_tap a_taps a_tanh_x a_xs_ready
            a_xp_done a_bT_ready a_dt_done a_abs a_exp a_ln a_relu a_sp_sum a_exp_a a_exp_a1 a_alpha a_diag
            a_alpha_rows a_alpha_copied a_alpha_zeroed a_u a_scan a_y a_gated a_out_done a_resid
            b_prep b_prep_copied b_transposed b_xnT_ready b_q_done b_q_ready b_scores b_max b_top b_neg b_shift b_probs b_rcp
            b_prT_done b_prT_ready b_g_done b_gT_ready b_v_done b_xbv b_x2 b_xl_transposed b_xlT_ready b_aff_done
            b_aff_copied b_base b_rows_out
            c_step c_ealpha c_prefix c_slots c_map
            d_gather_col d_scatter_col d_xT_done d_xT_ready d_h_done d_h_copied d_hT_done d_hT_act d_hT_dve d_y_done d_yb
            d_o_ready d_scattered_0 d_scattered_1 d_scattered_2""".split()
        S = {n: sem(n) for n in names}
        lns = [{k: sem(f"ln{i}_{k}") for k in ("stats", "aggr", "eps", "rstd", "out")} for i in range(4)]
        gath = [sem(f"d_gathered_{i}") for i in range(RING)]
        scat = [S[f"d_scattered_{i}"] for i in range(3)]

        def ln_stats(dve, which, g, src):
            stats, mv, var, rstd = ln_tmp[which]
            s = lns[which]
            dve.nop(nofuse=True)
            for j in range(GB):
                nc.vector.bn_stats(stats[:, j, :], src(j)).then_inc(s["stats"], 1)
            dve.wait_ge(s["stats"], GB * g + GB)
            dve.nop(nofuse=True)
            for j in range(GB):
                nc.vector.bn_aggr(mv[:, j, :], stats[:, j, :]).then_inc(s["aggr"], 1)
            dve.wait_ge(s["aggr"], GB * g + GB)
            dve.wait_ge(s["rstd"], g)
            nc.vector.tensor_scalar(var, mv[:, :, 1], EPS, None, ALU.add).then_inc(s["eps"], 1)

        def ln_rstd(pool, which, g):
            _, _, var, rstd = ln_tmp[which]
            s = lns[which]
            pool.wait_ge(s["eps"], g + 1)
            pool.wait_ge(s["out"], GB * g)
            nc.gpsimd.tensor_tensor(rstd, var, mhalf, ALU.pow).then_inc(s["rstd"], 1)

        def ln_apply(dve, which, g, src, dst):
            _, mv, _, rstd = ln_tmp[which]
            s = lns[which]
            dve.wait_ge(s["rstd"], g + 1)
            for j in range(GB):
                nc.vector.tensor_scalar(dst(j), src(j), mv[:, j, 0:1], rstd[:, j:j + 1],
                                        ALU.subtract, ALU.mult).then_inc(s["out"], 1)

        stages = [A["stage"], w2_sb[:, (E - 1) * KF * D:(E - 1) * KF * D + GB * D]]
        x2_flat = w2_sb[:, E * KF * D - GB * D:E * KF * D]
        x2_tiles = split(x2_flat, GB)

        def staged(which):
            return lambda j: stages[which][:, j * D:(j + 1) * D]

        def stage_group(act, which, g):
            act.wait_ge(lns[which]["out"], GB * g)
            nc.scalar.activation(stages[which], x_flat[:, bass.ds(g * (GB * D), GB * D)], ACT.Copy) \
                .then_inc(S[f"staged_{which}"], 1)

        xnA = split(A["xn"], GB)
        xnTA = split(A["xnT"], KD)
        xc, th, xs, uu, yv, sp, thz = (split(A[k], KI) for k in ("xc", "th", "xs", "u", "yv", "sp", "thz"))
        gz = [split(A["gz0"], KI), split(A["gz1"], KI)]
        xnB, xlB = split(B["xn"], GB), split(B["xl"], GB)
        xnTB, xlTB = split(B["xnT"], KD), split(B["xlT"], KD)
        row = B["row"].rearrange("p (j h d) -> p j h d", j=GB, h=2)
        pr = split(B["pr"], GB)
        cT_sb, c_sb = B["cT"], split(B["c"], GB)
        wq_sb, wk_sb, wqk = split(B["gT"], KD), split(B["wk"], KD), split(B["wqk"], KD)
        slot_rows = split(Dm["rows"], RING)
        xT_d = split(Dm["xT"], KD)
        hT_d = [split(Dm["hT0"], KF), split(Dm["hT1"], KF)]
        o_d = split(Dm["o"], 3)
        LOOP = (SLOTS - 3) // RING * RING

        block = stack.enter_context(nc.Block())

        @block.sync
        def _(sp_):
            xv = x.rearrange("b t d -> t b d")
            sp_.dma_start(x_res[:, 0:GB, :], xv[:, 0:GB, :]).then_inc(S["ld_x01"], 16)
            sp_.dma_start(x_res[:, GB:2 * GB, :], xv[:, GB:2 * GB, :]).then_inc(S["ld_x01"], 16)
            sp_.dma_start(inw_sb, in_w_t.rearrange("(k p) n -> p k n", p=P)).then_inc(S["ld_wa"], 16)
            sp_.dma_start(lane_sb[:, :], lane_w).then_inc(S["ld_wa"], 16)
            sp_.dma_start(dtw_sb[0:NS, :], dt_w_t).then_inc(S["ld_wa"], 16)
            sp_.dma_start(dtw_sb[NS:NS + 1, :], dt_b.rearrange("(o n) -> o n", o=1)).then_inc(S["ld_wa"], 16)
            sp_.dma_start(outw_sb, out_w_t.rearrange("(c p) n -> p c n", p=P)).then_inc(S["ld_wa"], 16)
            sp_.dma_start(x_res[:, 2 * GB:NB, :], xv[:, 2 * GB:NB, :]).then_inc(S["ld_x"], 16)
            sp_.dma_start(wq_sb, wq_t.rearrange("(k p) n -> p k n", p=P)).then_inc(S["ld_wb"], 16)
            sp_.dma_start(wk_sb, wk_t.rearrange("(k p) n -> p k n", p=P)).then_inc(S["ld_wb"], 16)
            sp_.dma_start(B["wv"], wv).then_inc(S["ld_wb"], 16)
            sp_.dma_start(B["bv"], bv.rearrange("(o n) -> o n", o=1).broadcast_to([P, D])).then_inc(S["ld_wb"], 16)

            ctv = ctx_t.rearrange("b c t -> c b t")
            cv = ctx.rearrange("b t c -> t b c")
            sp_.dma_start(split(cT_sb, GB), ctv[:, 0:GB, :]).then_inc(S["ld_ct"], 16)
            sp_.dma_start(c_sb, cv[:, 0:GB, :]).then_inc(S["ld_c"], 16)

            sp_.wait_ge(S["a_resid"], 2 * G)
            for e in range(E):
                sp_.dma_start(w1v[:, e], w1_t[e].rearrange("(k p) f -> p k f", p=P)).then_inc(S["ld_w1"], 16)
                if e < E - 1:
                    sp_.dma_start(w2v[:, e], w2_t[e].rearrange("(k p) d -> p k d", p=P)).then_inc(S["ld_w2"], 16)

            def rows_out(g):
                sp_.wait_ge(lns[3]["out"], GB * g + GB)
                sp_.wait_ge(S["b_base"], GB * g + GB)
                sp_.dma_start(rows_dram.rearrange("(b t) w -> t b w", t=T)[:, bass.ds(g * GB, GB), :],
                              B["row"].rearrange("p (j w) -> p j w", j=GB)).then_inc(S["b_rows_out"], 16)

            def next_ct(g):
                sp_.wait_ge(S["b_scores"], g + 1)
                sp_.dma_start(split(cT_sb, GB), ctv[:, bass.ds((g + 1) * GB, GB), :]).then_inc(S["ld_ct"], 16)

            def next_c(g):
                sp_.wait_ge(S["b_g_done"], g + 1)
                sp_.dma_start(c_sb, cv[:, bass.ds((g + 1) * GB, GB), :]).then_inc(S["ld_c"], 16)

            next_ct(0)
            with sp_.Fori(0, G - 2) as g:
                next_c(g)
                next_ct(g + 1)
                rows_out(g)
            next_c(G - 2)
            rows_out(G - 2)
            rows_out(G - 1)

            sp_.wait_ge(S["b_rows_out"], 16 * G)
            sp_.wait_ge(S["b_aff_copied"], G + 2)
            sp_.dma_start(w2v[:, E - 1], w2_t[E - 1].rearrange("(k p) d -> p k d", p=P)).then_inc(S["ld_w2"], 16)
            sp_.dma_start(b2_sb, b2.rearrange("(o e) d -> o e d", o=1).broadcast_to([P, E, D])).then_inc(S["ld_b2"], 16)

        @block.gpsimd
        def _(pool):
            nc.gpsimd.memset(ones[:, :], 1.0).then_inc(S["fills_set"], 1)
            nc.gpsimd.memset(mhalf, -0.5).then_inc(S["fills_set"], 1)
            nc.gpsimd.memset(A["bT"][0:NS + 1, :], 1.0).then_inc(S["fills_set"], 1)
            pool.wait_ge(S["fills_set"], 3)
            nc.gpsimd.affine_select(out=ident[:, :], in_=ones[:, :], compare_op=ALU.is_equal, fill=0.0, base=0,
                                    pattern=[[-1, P]], channel_multiplier=1).then_inc(S["ident_set"], 1)
            nc.gpsimd.affine_select(out=before[:, :], in_=ones[:, :], compare_op=ALU.is_gt, fill=0.0, base=0,
                                    pattern=[[1, P]], channel_multiplier=-1).then_inc(S["ident_set"], 1)
            for name, base, step, per_lane in (("e8", -E, 1, 0), ("k128", 0, P, 0), ("lane", 0, 1, 0),
                                               ("slot", 0, 1, 0), ("tok", 1, P, 1)):
                nc.gpsimd.iota(Im[name], pattern=[[step, Im[name].shape[1]]], base=base, channel_multiplier=per_lane,
                               allow_small_or_imprecise_dtypes=True).then_inc(S["consts_set"], 1)

            def gated(g, par):
                for c in range(KI):
                    pool.wait_ge(S["a_y"], KI * g + c + 1)
                    nc.gpsimd.tensor_tensor(yv[:, c, :], yv[:, c, :], gz[par][:, c, :], ALU.mult) \
                        .then_inc(S["a_gated"], 1)

            ln_rstd(pool, 0, 0)
            ln_rstd(pool, 0, 1)
            with pool.Fori(0, (G - 2) // 2) as it:
                for k in range(2):
                    ln_rstd(pool, 0, 2 * it + k + 2)
                    gated(2 * it + k, k)
            gated(G - 2, 0)
            gated(G - 1, 1)

            def add_bv(g):
                pool.wait_ge(S["a_resid"], 2 * G)
                pool.wait_ge(lns[1]["out"], GB * g + GB)
                for j in range(GB):
                    nc.gpsimd.tensor_tensor(x_res[:, g * GB + j, :], x_res[:, g * GB + j, :], B["bv"], ALU.add) \
                        .then_inc(S["b_xbv"], 1)

            def base_rows(g):
                for j in range(GB):
                    pool.wait_ge(lns[2]["out"], GB * g + j + 1)
                    pool.wait_ge(S["b_rows_out"], 16 * g)
                    nc.gpsimd.tensor_tensor(row[:, j, 1, :], x2_tiles[:, j, :], xlB[:, j, :], ALU.add) \
                        .then_inc(S["b_base"], 1)

            pool.wait_ge(S["ld_wb"], 16 * 4)
            ln_rstd(pool, 1, 0)
            ln_rstd(pool, 1, 1)
            add_bv(0)
            with pool.Fori(0, G - 2) as g:
                ln_rstd(pool, 1, g + 2)
                ln_rstd(pool, 2, g)
                ln_rstd(pool, 3, g)
                add_bv(g + 1)
                base_rows(g)
            for g in (G - 2, G - 1):
                ln_rstd(pool, 2, g)
                ln_rstd(pool, 3, g)
                if g < G - 1:
                    add_bv(g + 1)
                base_rows(g)

            def gather(s, k):
                nc.gpsimd.tensor_copy(gather_col[k], gather_i[:, bass.ds(s, 1)]).then_inc(S["d_gather_col"], 1)
                pool.wait_ge(S["d_gather_col"], s + 1)
                pool.nop(nofuse=True)
                nc.gpsimd.indirect_dma_start(
                    out=slot_rows[:, k, :], out_offset=None, in_=rows_dram,
                    in_offset=bass.IndirectOffsetOnAxis(ap=gather_col[k], axis=0)).then_inc(gath[k], 16)

            def scatter(s, k):
                pool.wait_ge(S["d_o_ready"], s + 1)
                pool.nop(nofuse=True)
                nc.gpsimd.tensor_copy(scatter_col[k], scatter_i[:, bass.ds(s, 1)]).then_inc(S["d_scatter_col"], 1)
                pool.wait_ge(S["d_scatter_col"], s + 1)
                pool.nop(nofuse=True)
                nc.gpsimd.indirect_dma_start(
                    out=out.rearrange("b t d -> (b t) d"), in_=o_d[:, k, :], in_offset=None,
                    out_offset=bass.IndirectOffsetOnAxis(ap=scatter_col[k], axis=0),
                    bounds_check=NB * T - 1, oob_is_err=False).then_inc(scat[k], 16)

            pool.wait_ge(S["b_rows_out"], 16 * G)
            pool.wait_ge(S["b_aff_copied"], G + 2)
            pool.wait_ge(S["c_map"], 2)
            for s in range(RING):
                gather(s, s)
            with pool.Fori(0, (SLOTS - RING) // RING) as it:
                for k in range(RING):
                    s = RING * it + k
                    scatter(s, k % 3)
                    gather(s + RING, k)
            for s in range((SLOTS - RING) // RING * RING, SLOTS):
                scatter(s, s % 3)
                if s + RING < SLOTS:
                    gather(s + RING, s % RING)
            for k in range(3):
                pool.wait_ge(scat[k], 16 * (SLOTS // 3))

        @block.tensor
        def _(pe):
            def transpose_xn(g, first=False):
                pe.wait_ge(lns[0]["out"], GB * g + GB)
                pe.wait_ge(S["a_xnT_ready"], KD * g)
                if not first:
                    pe.wait_ge(S["a_resid"], 2 * (g - 1))
                for k in range(KD):
                    for j in range(GB):
                        mm = nc.tensor.transpose(bank[k][:, j * P:(j + 1) * P], xnA[:, j, k * P:(k + 1) * P], ident[:, :])
                    mm.then_inc(S["a_transposed"], 1)

            def in_proj(g, first_col, done, free):
                for c in range(KI):
                    free(g, c)
                    for k in range(KD):
                        mm = nc.tensor.matmul(bank[2 + c][:, :], inw_sb[:, k, first_col + c * P:first_col + (c + 1) * P],
                                              xnTA[:, k, :], start=(k == 0), stop=(k == KD - 1))
                    mm.then_inc(done, 1)

            def z_part(g, first=False):
                pe.wait_ge(S["a_xnT_ready"], KD * g + KD)

                def free(g, c):
                    if not first:
                        pe.wait_ge(S["a_relu"], GB * (g - 1) + c + 1)
                in_proj(g, DI, S["a_z_done"], free)

            def x_part(g):
                def free(g, c):
                    pe.wait_ge(S["a_gate_ready"], KI * g + c + 1)
                in_proj(g, 0, S["a_x_done"], free)

            def x_proj(g):
                pe.wait_ge(S["a_bT_ready"], g)
                for c in range(KI):
                    pe.wait_ge(S["a_xs_ready"], KI * g + c + 1)
                    mm = nc.tensor.matmul(bank[6][0:NS, :], xpw_sb[:, c, :], xs[:, c, :], start=(c == 0), stop=(c == KI - 1))
                mm.then_inc(S["a_xp_done"], 1)

            def dt_proj(g):
                pe.wait_ge(S["a_bT_ready"], g + 1)
                for j in range(GB):
                    pe.wait_ge(S["a_taps"], 3 * KI * g + 2 * KI + j + 1)
                    nc.tensor.matmul(bank[2 + j][:, :], A["bT"][0:NS + 1, j * P:(j + 1) * P], dtw_sb[0:NS + 1, :],
                                     start=True, stop=True).then_inc(S["a_dt_done"], 1)

            def alpha_rows(g):
                pe.wait_ge(S["a_u"], KI * g)
                for j in range(GB):
                    pe.wait_ge(S["a_diag"], GB * g + j + 1)
                    mm = nc.tensor.matmul(bank[7][:, j * P:(j + 1) * P], ones[:, :], A["diag"][:, j * P:(j + 1) * P],
                                          start=True, stop=True)
                mm.then_inc(S["a_alpha_rows"], 1)

            def out_proj(g, last=False):
                pe.wait_ge(S["a_gated"], KI * g + KI)
                pe.wait_ge(S["a_xnT_ready"], KD * g + (KD if last else 2 * KD))
                for j in range(GB):
                    for c in range(KI):
                        mm = nc.tensor.matmul(bank[j // 2][:, (j % 2) * D:(j % 2) * D + D],
                                              yv[:, c, j * P:(j + 1) * P], outw_sb[:, c, :], start=(c == 0), stop=(c == KI - 1))
                    mm.then_inc(S["a_out_done"], 1)

            pe.wait_ge(S["ident_set"], 2)
            transpose_xn(0, first=True)
            pe.wait_ge(S["ld_wa"], 16 * 5)
            z_part(0, first=True)
            x_part(0)

            def pass_a(g):
                x_proj(g)
                dt_proj(g)
                transpose_xn(g + 1)
                z_part(g + 1)
                alpha_rows(g)
                x_part(g + 1)
                out_proj(g)

            with pe.Fori(0, G - 1) as g:
                pass_a(g)
            x_proj(G - 1)
            dt_proj(G - 1)
            alpha_rows(G - 1)
            out_proj(G - 1, last=True)

            pe.wait_ge(S["ld_wb"], 16 * 4)
            pe.wait_ge(S["a_relu"], GB * G)
            for k in range(KD):
                for e in range(KD):
                    nc.tensor.matmul(bank[4][:, k * C:(k + 1) * C], wq_sb[:, e, k * P:(k + 1) * P], wk_sb[:, e, :],
                                     start=(e == 0), stop=(e == KD - 1))
            for e in range(KD):
                nc.tensor.matmul(bank[4][:, 2 * C:2 * C + 1], wk_sb[:, e, :], bq_sb[:, e:e + 1],
                                 start=(e == 0), stop=(e == KD - 1))
            for k in range(KD):
                for e in range(KD):
                    mm = nc.tensor.matmul(bank[4][:, 2 * C + 2 + k:2 * C + 3 + k], wq_sb[:, e, k * P:(k + 1) * P],
                                          bk_sb[:, e:e + 1], start=(e == 0), stop=(e == KD - 1))
            for e in range(KD):
                mm = nc.tensor.matmul(bank[4][:, 2 * C + 4:2 * C + 5], bq_sb[:, e:e + 1].broadcast_to([P, P]),
                                      bk_sb[:, e:e + 1], start=(e == 0), stop=(e == KD - 1))
            mm.then_inc(S["b_prep"], 1)
            pe.wait_ge(S["a_resid"], 2 * G)
            pe.wait_ge(S["a_u"], KI * G)

            def transpose_b(src, wait_for, done, count):
                wait_for()
                for k in range(KD):
                    for j in range(GB):
                        mm = nc.tensor.transpose(bank[k][:, j * P:(j + 1) * P], src[:, j, k * P:(k + 1) * P], ident[:, :])
                    mm.then_inc(done, 1)

            def t2(g, n_xl):
                pe.wait_ge(lns[1]["out"], GB * g + GB)
                pe.wait_ge(S["b_xlT_ready"], KD * n_xl)
                transpose_b(xnB, lambda: None, S["b_transposed"], g)

            def t3(g, n_xn):
                pe.wait_ge(lns[2]["out"], GB * g + GB)
                pe.wait_ge(S["b_xnT_ready"], KD * n_xn)
                transpose_b(xlB, lambda: None, S["b_xl_transposed"], g)

            def q_part(g):
                pe.wait_ge(S["b_xnT_ready"], KD * g + KD)
                pe.wait_ge(S["b_q_ready"], g)
                for k in range(KD):
                    mm = nc.tensor.matmul(bank[4][:, :], wqk[:, k, :], xnTB[:, k, :], start=(k == 0), stop=(k == KD - 1))
                mm.then_inc(S["b_q_done"], 1)

            def scores(g):
                pe.wait_ge(S["b_q_ready"], g + 1)
                pe.wait_ge(S["ld_ct"], 16 * g + 16)
                pe.wait_ge(S["b_probs"], GB * g)
                for j in range(GB):
                    mm = nc.tensor.matmul(bank[5][:, j * P:(j + 1) * P], B["q"][:, j * P:(j + 1) * P],
                                          cT_sb[:, j * P:(j + 1) * P], start=True, stop=True)
                mm.then_inc(S["b_scores"], 1)

            def probs_t(g):
                pe.wait_ge(S["b_probs"], GB * g + GB)
                pe.wait_ge(S["b_prT_ready"], g)
                for j in range(GB):
                    mm = nc.tensor.transpose(bank[6][:, j * P:(j + 1) * P], pr[:, j, :], ident[:, :])
                mm.then_inc(S["b_prT_done"], 1)

            def g_part(g):
                pe.wait_ge(S["b_prT_ready"], g + 1)
                pe.wait_ge(S["ld_c"], 16 * g + 16)
                pe.wait_ge(S["b_aff_copied"], g + 1)
                for j in range(GB):
                    mm = nc.tensor.matmul(bank[7][:, j * P:(j + 1) * P], c_sb[:, j, :], B["prT"][:, j * P:(j + 1) * P],
                                          start=True, stop=True)
                mm.then_inc(S["b_g_done"], 1)

            def v_part(g):
                pe.wait_ge(S["b_gT_ready"], g + 1)
                pe.wait_ge(S["b_x2"], GB * g)
                for j in range(GB):
                    nc.tensor.matmul(bank[2 + j // 2][:, (j % 2) * D:(j % 2) * D + D], B["gT"][:, j * P:(j + 1) * P],
                                     B["wv"], start=True, stop=True).then_inc(S["b_v_done"], 1)

            def aff(n, with_aff=True, with_shift=True):
                pe.wait_ge(S["b_gT_ready"], n if with_shift else G)
                if with_shift:
                    for j in range(GB):
                        for k in range(KD):
                            mm = nc.tensor.matmul(bank[7][:, GB * E + j:GB * E + j + 1], xnTB[:, k, j * P:(j + 1) * P],
                                                  bk_proj[:, k:k + 1], start=(k == 0), stop=(k == KD - 1))
                if with_aff:
                    pe.wait_ge(S["b_xlT_ready"], KD * (n - 1))
                    for j in range(GB):
                        for k in range(KD):
                            mm = nc.tensor.matmul(bank[7][:, j * E:(j + 1) * E], xlTB[:, k, j * P:(j + 1) * P],
                                                  cent_sb[:, k, :], start=(k == 0), stop=(k == KD - 1))
                mm.then_inc(S["b_aff_done"], 1)

            pe.wait_ge(S["b_prep_copied"], 1)
            t2(0, 0)
            q_part(0)
            aff(0, with_aff=False)
            scores(0)
            probs_t(0)
            g_part(0)
            t2(1, 0)
            q_part(1)
            v_part(0)
            aff(1, with_aff=False)
            scores(1)
            with pe.Fori(1, G - 1) as g:
                probs_t(g)
                g_part(g)
                t3(g - 1, g + 1)
                t2(g + 1, g)
                q_part(g + 1)
                v_part(g)
                aff(g + 1)
                scores(g + 1)
            probs_t(G - 1)
            g_part(G - 1)
            t3(G - 2, G)
            v_part(G - 1)
            aff(G, with_shift=False)
            pe.wait_ge(S["b_xlT_ready"], KD * (G - 1))
            t3(G - 1, G)
            pe.wait_ge(S["b_aff_copied"], G + 1)
            aff(G + 1, with_shift=False)

            pe.wait_ge(S["c_step"], 5)
            nc.tensor.matmul(bank[0][:, 0:TILES * E], before[:, :], Rm["hot"], start=True, stop=True)
            nc.tensor.matmul(bank[1][:, 0:TILES * E], ones[:, :], Rm["hot"], start=True, stop=True).then_inc(S["c_prefix"], 1)
            pe.wait_ge(S["c_slots"], 1)
            for j in range(TILES):
                mm = nc.tensor.matmul(bank[2][:, 0:2 * SP_], split(Cm["lo_hot"], TILES)[:, j, :],
                                      split(Cm["hi_val"], TILES)[:, j, :], start=(j == 0), stop=(j == TILES - 1))
            mm.then_inc(S["c_prefix"], 1)

            def xT(s, k, turn):
                pe.wait_ge(gath[k], 16 * turn + 16)
                pe.wait_ge(S["d_xT_ready"], KD * s)
                for d in range(KD):
                    mm = nc.tensor.transpose(bank[0][:, d * P:(d + 1) * P], slot_rows[:, k, d * P:(d + 1) * P], ident[:, :])
                mm.then_inc(S["d_xT_done"], 1)

            def hidden(s):
                e = pe.value_load(expert_i[0:1, bass.ds(s, 1)], min_val=0, max_val=E - 1)
                pe.wait_ge(S["d_xT_ready"], KD * s + KD)
                for half in range(2):
                    pe.wait_ge(S["d_h_copied"], 2 * s)
                    for k in range(KD):
                        mm = nc.tensor.matmul(bank[2 + half][:, :], xT_d[:, k, :],
                                              w1_sb[:, bass.ds(e * (KD * F) + k * F + half * 512, 512)],
                                              start=(k == 0), stop=(k == KD - 1))
                    mm.then_inc(S["d_h_done"], 1)

            def hidden_t(s):
                pe.wait_ge(S["d_h_copied"], 2 * s + 2)
                for half in range(2):
                    pe.wait_ge(S["d_hT_act"] if half == 0 else S["d_hT_dve"], 4 * s)
                    for f in range(4):
                        kf = 4 * half + f
                        mm = nc.tensor.transpose(bank[4 + half][:, f * P:(f + 1) * P], Dm["h"][:, kf * P:(kf + 1) * P], ident[:, :])
                    mm.then_inc(S["d_hT_done"], 1)

            def y_part(s, par):
                e = pe.value_load(expert_i[0:1, bass.ds(s, 1)], min_val=0, max_val=E - 1)
                pe.wait_ge(S["d_yb"], s)
                for f in range(KF):
                    pe.wait_ge(S["d_hT_act"] if f < 4 else S["d_hT_dve"], 4 * s + f % 4 + 1)
                    mm = nc.tensor.matmul(bank[6][:, 0:D], hT_d[par][:, f, :], w2_sb[:, bass.ds(e * (KF * D) + f * D, D)],
                                          start=(f == 0), stop=(f == KF - 1))
                mm.then_inc(S["d_y_done"], 1)

            pe.wait_ge(S["c_map"], 2)
            pe.wait_ge(S["ld_w1"], 16 * E)
            pe.wait_ge(S["ld_w2"], 16 * E)
            xT(0, 0, 0)
            hidden(0)
            xT(1, 1, 0)
            hidden(1)
            hidden_t(0)
            xT(2, 2, 0)
            with pe.Fori(0, LOOP // RING) as it:
                for k in range(RING):
                    s = RING * it + k
                    hidden(s + 2)
                    hidden_t(s + 1)
                    xT(s + 3, (k + 3) % RING, it + (k + 3) // RING)
                    y_part(s, k % 2)
            for s in range(LOOP, SLOTS):
                if s + 2 < SLOTS:
                    hidden(s + 2)
                if s + 1 < SLOTS:
                    hidden_t(s + 1)
                if s + 3 < SLOTS:
                    xT(s + 3, (s + 3) % RING, (s + 3) // RING)
                y_part(s, s % 2)

        @block.scalar
        def _(act):
            act_ = nc.scalar.activation

            def copy_xnT(g):
                act.wait_ge(S["a_x_done"], KI * g)
                for k in range(KD):
                    act.wait_ge(S["a_transposed"], KD * g + k + 1)
                    act_(xnTA[:, k, :], bank[k][:, :], ACT.Copy).then_inc(S["a_xnT_ready"], 1)

            def tanh_z(g):
                act.wait_ge(S["a_gate_ready"], KI * g)
                for c in range(KI):
                    act.wait_ge(S["a_z_done"], KI * g + c + 1)
                    act_(thz[:, c, :], bank[2 + c][:, :], ACT.Tanh, scale=0.5).then_inc(S["a_tanh_z"], 1)

            def first_tap(g):
                act.wait_ge(S["a_xs_ready"], KI * g)
                for c in range(KI):
                    act.wait_ge(S["a_x_done"], KI * g + c + 1)
                    act_(xc[:, c, :], bank[2 + c][:, :], ACT.Identity, bias=conv_b_sb[:, c:c + 1],
                         scale=conv_w_sb[:, c, 3:4]).then_inc(S["a_first_tap"], 1)

            def tanh_x(g):
                for c in range(KI):
                    act.wait_ge(S["a_taps"], 3 * KI * g + 2 * KI + c + 1)
                    act_(th[:, c, :], xc[:, c, :], ACT.Tanh, scale=0.5).then_inc(S["a_tanh_x"], 1)

            def copy_bT(g):
                act.wait_ge(S["a_xp_done"], g + 1)
                act.wait_ge(S["a_dt_done"], GB * g)
                act_(A["bT"][0:NS, :], bank[6][0:NS, :], ACT.Copy, scale=0.5).then_inc(S["a_bT_ready"], 1)

            def softplus(g):
                for j in range(GB):
                    act.wait_ge(S["a_dt_done"], GB * g + j + 1)
                    act_(sp[:, j, :], bank[2 + j][:, :], ACT.Abs).then_inc(S["a_abs"], 1)
                for j in range(GB):
                    act.wait_ge(S["a_abs"], GB * g + j + 1)
                    act_(sp[:, j, :], sp[:, j, :], ACT.Exp, scale=-1.0).then_inc(S["a_exp"], 1)

            def softplus_ln(g):
                act.wait_ge(S["a_sp_sum"], g)
                for j in range(GB):
                    act.wait_ge(S["a_exp"], GB * g + j + 1)
                    act_(sp[:, j, :], sp[:, j, :], ACT.Ln, bias=1.0, accum_out=ln_sum[:, j:j + 1]).then_inc(S["a_ln"], 1)

            def exp_alpha(g):
                act.wait_ge(S["a_sp_sum"], g + 1)
                act_(exp_a, sp_sum, ACT.Exp, scale=-1.0 / DI).then_inc(S["a_exp_a"], 1)

            def copy_alpha(g):
                act.wait_ge(S["a_alpha_rows"], g + 1)
                act.wait_ge(S["a_scan"], KI * g)
                act_(A["as"], bank[7][:, :], ACT.Copy).then_inc(S["a_alpha_copied"], 1)

            act.wait_ge(S["ld_x01"], 32)
            stage_group(act, 0, 0)
            stage_group(act, 0, 1)
            copy_xnT(0)
            tanh_z(0)
            act.wait_ge(S["ld_wa"], 16 * 5)
            first_tap(0)
            tanh_x(0)
            act.wait_ge(S["fills_set"], 3)
            act.wait_ge(S["ld_x"], 16)

            def pass_a(g):
                copy_bT(g)
                softplus(g)
                copy_xnT(g + 1)
                softplus_ln(g)
                exp_alpha(g)
                tanh_z(g + 1)
                copy_alpha(g)
                first_tap(g + 1)
                tanh_x(g + 1)

            with act.Fori(0, G - 2) as g:
                stage_group(act, 0, g + 2)
                pass_a(g)
            pass_a(G - 2)
            copy_bT(G - 1)
            softplus(G - 1)
            softplus_ln(G - 1)
            exp_alpha(G - 1)
            copy_alpha(G - 1)

            def copy_t2(g):
                act.wait_ge(S["b_aff_done"], g)
                for k in range(KD):
                    act.wait_ge(S["b_transposed"], KD * g + k + 1)
                    act_(xnTB[:, k, :], bank[k][:, :], ACT.Copy).then_inc(S["b_xnT_ready"], 1)

            def copy_t3(g):
                act.wait_ge(S["b_aff_done"], g + 2)
                for k in range(KD):
                    act.wait_ge(S["b_xl_transposed"], KD * g + k + 1)
                    act_(xlTB[:, k, :], bank[k][:, :], ACT.Copy).then_inc(S["b_xlT_ready"], 1)

            def copy_q(g):
                act.wait_ge(S["b_q_done"], g + 1)
                act.wait_ge(S["b_scores"], g)
                act_(B["q"], bank[4][:, :], ACT.Identity, bias=q_bias).then_inc(S["b_q_ready"], 1)

            def exp_scores(g):
                act.wait_ge(S["b_neg"], g + 1)
                act.wait_ge(S["b_prT_done"], g)
                act.wait_ge(S["b_rcp"], g)
                for j in range(GB):
                    act_(pr[:, j, :], bank[5][:, j * P:(j + 1) * P], ACT.Exp, bias=att_neg[:, j:j + 1],
                         accum_out=att_sum[:, j:j + 1]).then_inc(S["b_probs"], 1)

            def copy_prT(g):
                act.wait_ge(S["b_prT_done"], g + 1)
                act.wait_ge(S["b_g_done"], g)
                act_(B["prT"], bank[6][:, :], ACT.Copy).then_inc(S["b_prT_ready"], 1)

            def copy_gT(g):
                act.wait_ge(S["b_g_done"], g + 1)
                act.wait_ge(S["b_v_done"], GB * g)
                act_(B["gT"], bank[7][:, :], ACT.Copy).then_inc(S["b_gT_ready"], 1)

            act.wait_ge(S["a_resid"], 2 * G)
            stage_group(act, 1, 0)
            stage_group(act, 1, 1)
            act.wait_ge(S["b_prep_copied"], 1)
            copy_t2(0)
            copy_q(0)
            exp_scores(0)
            stage_group(act, 1, 2)
            copy_prT(0)
            copy_gT(0)
            copy_t2(1)
            copy_q(1)
            exp_scores(1)

            def pass_b(g):
                copy_prT(g)
                copy_gT(g)
                copy_t3(g - 1)
                copy_t2(g + 1)
                copy_q(g + 1)
                exp_scores(g + 1)

            with act.Fori(1, G - 2) as g:
                stage_group(act, 1, g + 2)
                pass_b(g)
            pass_b(G - 2)
            copy_prT(G - 1)
            copy_gT(G - 1)
            copy_t3(G - 2)
            copy_t3(G - 1)

            act.wait_ge(S["c_step"], 1)
            act_(Rm["ealpha"], Rm["max"], ACT.Exp, scale=-1.0).then_inc(S["c_ealpha"], 1)

            def copy_h(s):
                act.wait_ge(S["d_hT_done"], 2 * s)
                for half in range(2):
                    act.wait_ge(S["d_h_done"], 2 * s + half + 1)
                    act_(Dm["h"][:, half * 512:(half + 1) * 512], bank[2 + half][:, :], ACT.Copy).then_inc(S["d_h_copied"], 1)

            def relu_lo(s, par):
                e = act.value_load(expert_i[0:1, bass.ds(s, 1)], min_val=0, max_val=E - 1)
                act.wait_ge(S["d_hT_done"], 2 * s + 1)
                if not isinstance(s, int) or s > 0:
                    act.wait_ge(S["d_y_done"], s - 1)
                for f in range(4):
                    act_(hT_d[par][:, f, :], bank[4][:, f * P:(f + 1) * P], ACT.Relu,
                         bias=L["b1"][:, bass.ds(e * KF + f, 1)]) \
                        .then_inc(S["d_hT_act"], 1)

            act.wait_ge(S["c_map"], 2)
            copy_h(0)
            relu_lo(0, 0)
            copy_h(1)
            with act.Fori(0, LOOP // 2) as it:
                for k in range(2):
                    s = 2 * it + k
                    copy_h(s + 2)
                    relu_lo(s + 1, (k + 1) % 2)
            for s in range(LOOP, SLOTS - 1):
                if s + 2 < SLOTS:
                    copy_h(s + 2)
                relu_lo(s + 1, (s + 1) % 2)

        @block.vector
        def _(dve):
            stt = nc.vector.scalar_tensor_tensor

            def ln_out(g):
                dve.wait_ge(S["a_transposed"], KD * g)
                ln_apply(dve, 0, g, staged(0), lambda j: xnA[:, j, :])

            def gate(g, par):
                if not isinstance(g, int) or g > 0:
                    dve.wait_ge(S["a_gated"], KI * (g - 1))
                for c in range(KI):
                    dve.wait_ge(S["a_tanh_z"], KI * g + c + 1)
                    stt(gz[par][:, c, :], thz[:, c, :], 1.0, bank[2 + c][:, :], ALU.add, ALU.mult) \
                        .then_inc(S["a_gate_ready"], 1)

            def conv(g):
                for tap in (1, 2, 3):
                    for c in range(KI):
                        if tap == 1:
                            dve.wait_ge(S["a_first_tap"], KI * g + c + 1)
                        else:
                            dve.wait_ge(S["a_taps"], 3 * KI * g + KI * (tap - 2) + c + 1)
                        late = split(xc[:, c, :], GB)[:, :, tap:T]
                        stt(late, split(bank[2 + c][:, :], GB)[:, :, 0:T - tap], conv_w_sb[:, c, 3 - tap:4 - tap], late,
                            ALU.mult, ALU.add).then_inc(S["a_taps"], 1)

            def silu_x(g):
                dve.wait_ge(S["a_xp_done"], g)
                for c in range(KI):
                    dve.wait_ge(S["a_tanh_x"], KI * g + c + 1)
                    stt(xs[:, c, :], th[:, c, :], 1.0, xc[:, c, :], ALU.add, ALU.mult).then_inc(S["a_xs_ready"], 1)

            def relu_part(g):
                for j in range(GB):
                    dve.wait_ge(S["a_abs"], GB * g + j + 1)
                    nc.vector.tensor_scalar(bank[2 + j][:, :], bank[2 + j][:, :], 0.0, None, ALU.max, ALU.add,
                                            accum_out=relu_sum[:, j:j + 1]).then_inc(S["a_relu"], 1)

            def alphas(g):
                dve.wait_ge(S["a_ln"], GB * g + GB)
                dve.wait_ge(S["a_relu"], GB * g + GB)
                nc.vector.tensor_tensor(sp_sum, relu_sum, ln_sum, ALU.add).then_inc(S["a_sp_sum"], 1)
                dve.wait_ge(S["a_exp_a"], g + 1)
                nc.vector.tensor_scalar(exp_a1, exp_a, 1.0, None, ALU.add).then_inc(S["a_exp_a1"], 1)
                dve.wait_ge(S["a_exp_a1"], g + 1)
                nc.vector.reciprocal(alpha, exp_a1).then_inc(S["a_alpha"], 1)
                dve.wait_ge(S["a_alpha"], g + 1)
                dve.wait_ge(S["a_alpha_rows"], g)
                for j in range(GB):
                    nc.vector.tensor_scalar(A["diag"][:, j * P:(j + 1) * P], ident[:, :], alpha[:, j:j + 1], None,
                                            ALU.mult).then_inc(S["a_diag"], 1)

            def recurrence(g):
                dve.wait_ge(S["a_alpha_copied"], g + 1)
                nc.vector.memset(split(A["as"], GB)[:, :, 0:1], 0.0).then_inc(S["a_alpha_zeroed"], 1)
                for c in range(KI):
                    stt(uu[:, c, :], bank[7][:, :], 1.0, xs[:, c, :], ALU.subtract, ALU.mult).then_inc(S["a_u"], 1)
                dve.wait_ge(S["a_alpha_zeroed"], g + 1)
                for c in range(KI):
                    dve.wait_ge(S["a_u"], KI * g + c + 1)
                    nc.vector.tensor_tensor_scan(uu[:, c, :], A["as"], uu[:, c, :], 0.0, ALU.mult, ALU.add) \
                        .then_inc(S["a_scan"], 1)
                    if c:
                        y_chunk(g, c - 1)
                y_chunk(g, KI - 1)

            def y_chunk(g, c):
                dve.wait_ge(S["a_scan"], KI * g + c + 1)
                if c == 0:
                    dve.wait_ge(S["a_out_done"], GB * g)
                stt(yv[:, c, :], uu[:, c, :], neg_d[:, c:c + 1], xs[:, c, :], ALU.mult, ALU.add).then_inc(S["a_y"], 1)

            def resid(g):
                for half in range(2):
                    dve.wait_ge(S["a_out_done"], GB * g + 2 * half + 2)
                    dst = x_flat[:, bass.ds(g * (GB * D) + half * 2 * D, 2 * D)]
                    stt(dst, bank[half][:, :], 0.25, dst, ALU.mult, ALU.add).then_inc(S["a_resid"], 1)

            dve.wait_ge(S["ld_x01"], 32)
            dve.wait_ge(S["staged_0"], 1)
            ln_stats(dve, 0, 0, staged(0))
            ln_out(0)
            dve.wait_ge(S["staged_0"], 2)
            ln_stats(dve, 0, 1, staged(0))
            dve.wait_ge(S["ld_wa"], 16 * 5)
            nc.vector.tensor_scalar(neg_d, d_sb, -1.0, None, ALU.mult).then_inc(S["neg_d_set"], 1)
            ln_out(1)
            gate(0, 0)
            conv(0)
            silu_x(0)
            dve.wait_ge(S["ld_x"], 16)
            dve.wait_ge(S["ident_set"], 2)
            dve.wait_ge(S["neg_d_set"], 1)

            def pass_a(g, par, has_next, has_stats):
                relu_part(g)
                if has_stats:
                    dve.wait_ge(S["staged_0"], g + 3)
                    ln_stats(dve, 0, g + 2, staged(0))
                alphas(g)
                if has_next:
                    gate(g + 1, 1 - par)
                if has_stats:
                    ln_out(g + 2)
                recurrence(g)
                if has_next:
                    conv(g + 1)
                    silu_x(g + 1)
                resid(g)

            with dve.Fori(0, (G - 2) // 2) as it:
                pass_a(2 * it, 0, True, True)
                pass_a(2 * it + 1, 1, True, True)
            pass_a(G - 2, 0, True, False)
            pass_a(G - 1, 1, False, False)

            dve.wait_ge(S["b_prep"], 1)
            nc.vector.tensor_copy(B["wqk"], bank[4][:, 0:KD * C])
            nc.vector.tensor_copy(bk_proj, bank[4][:, 2 * C + 2:2 * C + 2 + KD])
            nc.vector.tensor_copy(bq_bk, bank[4][:, 2 * C + 4:2 * C + 5])
            nc.vector.tensor_copy(q_bias, bank[4][:, 2 * C:2 * C + 1]).then_inc(S["b_prep_copied"], 1)

            def ln1_out(g):
                dve.wait_ge(S["b_transposed"], KD * g)
                ln_apply(dve, 1, g, staged(1), lambda j: xnB[:, j, :])

            def ln2_out(g):
                dve.wait_ge(S["b_xl_transposed"], KD * g)
                dve.wait_ge(S["b_base"], GB * g)
                ln_apply(dve, 2, g, lambda j: x2_tiles[:, j, :], lambda j: xlB[:, j, :])

            def ln3_out(g):
                dve.wait_ge(S["b_rows_out"], 16 * g)
                ln_apply(dve, 3, g, lambda j: xlB[:, j, :], lambda j: row[:, j, 0, :])

            def score_max(g):
                dve.wait_ge(S["b_aff_copied"], g + 1)
                dve.wait_ge(S["b_scores"], g + 1)
                nc.vector.tensor_reduce(att_max, split(bank[5][:, :], GB), X, ALU.max).then_inc(S["b_max"], 1)
                dve.wait_ge(S["b_max"], g + 1)
                nc.vector.tensor_tensor(att_top, att_max, shift, ALU.add).then_inc(S["b_top"], 1)
                dve.wait_ge(S["b_top"], g + 1)
                nc.vector.tensor_tensor(att_neg, shift, att_top, ALU.subtract).then_inc(S["b_neg"], 1)

            def add_attn(g):
                dve.wait_ge(S["b_probs"], GB * g + GB)
                nc.vector.reciprocal(att_rcp, att_sum).then_inc(S["b_rcp"], 1)
                dve.wait_ge(S["b_rcp"], g + 1)
                dve.wait_ge(S["b_xbv"], GB * g + GB)
                dve.wait_ge(S["b_base"], GB * g)
                for j in range(GB):
                    dve.wait_ge(S["b_v_done"], GB * g + 2 * (j // 2) + 2)
                    stt(x2_tiles[:, j, :], bank[2 + j // 2][:, (j % 2) * D:(j % 2) * D + D], att_rcp[:, j:j + 1],
                        x_res[:, g * GB + j, :],
                        ALU.mult, ALU.add).then_inc(S["b_x2"], 1)

            def copy_aff(n, with_aff=True, with_shift=True):
                dve.wait_ge(S["b_aff_done"], n + 1)
                if with_shift:
                    ins = nc.vector.tensor_scalar(shift, bank[7][:, GB * E:GB * E + GB], bq_bk, None, ALU.add)
                if with_aff:
                    ins = nc.vector.tensor_copy(affs[:, bass.ds((n - 2) * GB, GB), :], split(bank[7][:, 0:GB * E], GB))
                ins.then_inc(S["b_aff_copied"], 1)

            def pass_b(g, has_prev, has_next, has_stats):
                if has_stats:
                    dve.wait_ge(S["staged_1"], g + 3)
                    ln_stats(dve, 1, g + 2, staged(1))
                add_attn(g)
                dve.wait_ge(S["b_x2"], GB * g + GB)
                ln_stats(dve, 2, g, lambda j: x2_tiles[:, j, :])
                if has_stats:
                    ln1_out(g + 2)
                copy_aff(g + 1, with_aff=has_prev, with_shift=has_next)
                ln2_out(g)
                if has_next:
                    score_max(g + 1)
                dve.wait_ge(lns[2]["out"], GB * g + GB)
                ln_stats(dve, 3, g, lambda j: xlB[:, j, :])
                ln3_out(g)

            dve.wait_ge(S["a_resid"], 2 * G)
            dve.wait_ge(S["staged_1"], 1)
            ln_stats(dve, 1, 0, staged(1))
            ln1_out(0)
            dve.wait_ge(S["staged_1"], 2)
            ln_stats(dve, 1, 1, staged(1))
            ln1_out(1)
            copy_aff(0, with_aff=False)
            score_max(0)
            pass_b(0, False, True, True)
            with dve.Fori(1, G - 2) as g:
                pass_b(g, True, True, True)
            pass_b(G - 2, True, True, False)
            pass_b(G - 1, True, False, False)
            copy_aff(G + 1, with_shift=False)

            steps = [0]

            def step(ins):
                ins.then_inc(S["c_step"], 1)
                steps[0] += 1
                dve.wait_ge(S["c_step"], steps[0])

            v = nc.vector
            hot, tot = split(Rm["hot"], TILES), split(Rm["tot"], TILES)

            def over_e(ap):
                return ap.rearrange("p (t o) -> p t o", o=1).broadcast_to([P, TILES, E])

            def over_t(ap, n=TILES):
                return ap.rearrange("p (o e) -> p o e", o=1).broadcast_to([P, n, ap.shape[1]])

            dve.wait_ge(S["b_aff_copied"], G + 2)
            dve.wait_ge(S["consts_set"], 5)
            step(v.tensor_reduce(Rm["max"], affs, X, ALU.max))
            step(v.tensor_tensor(split(Rm["eq"], TILES), affs, over_e(Rm["max"]), ALU.is_ge))
            step(v.tensor_tensor(split(Rm["cand"], TILES), split(Rm["eq"], TILES), over_t(Im["e8"]), ALU.mult))
            step(v.tensor_reduce(Rm["first"], split(Rm["cand"], TILES), X, ALU.min))
            step(v.tensor_tensor(hot, over_t(Im["e8"]), over_e(Rm["first"]), ALU.is_equal))
            dve.wait_ge(S["c_ealpha"], 1)
            step(v.tensor_scalar(Rm["ealpha"], Rm["ealpha"], 1.0, None, ALU.add))
            step(v.reciprocal(Rm["max"], Rm["ealpha"]))
            dve.wait_ge(S["c_prefix"], 1)
            step(v.tensor_copy(Rm["tot"], bank[1][:, 0:TILES * E]))
            cum = split(Rm["eq"], TILES)
            for e in range(E):
                ins = v.tensor_tensor_scan(cum[:, :, e], ones[:, 0:TILES], tot[:, :, e], 0.0, ALU.mult, ALU.add)
            step(ins)
            count = cum[:, TILES - 1, :]
            per_e = Rm["cand"].rearrange("p (e k) -> p e k", e=E)
            step(v.tensor_tensor(per_e, count.rearrange("p (e o) -> p e o", o=1).broadcast_to([P, E, TILES]),
                                 over_t(Im["k128"], E), ALU.is_gt))
            n_slots, ends, starts = (routing_tmp[:, k * E:(k + 1) * E] for k in range(3))
            step(v.tensor_reduce(n_slots, per_e, X, ALU.add))
            step(v.tensor_tensor_scan(ends, ones[:, 0:E], n_slots, 0.0, ALU.mult, ALU.add))
            step(v.tensor_tensor(starts, ends, n_slots, ALU.subtract))
            ge = Cm["lo_hot"][:, 0:SP_ * E]
            step(v.tensor_tensor(split(ge, SP_), Im["slot"].rearrange("p (s o) -> p s o", o=1).broadcast_to([P, SP_, E]),
                                 over_t(ends, SP_), ALU.is_ge))
            slot_e = Cm["hi_hot"][:, 0:SP_]
            step(v.tensor_reduce(slot_e, split(ge, SP_), X, ALU.add))
            step(v.tensor_scalar(expert_i, slot_e, float(E - 1), None, ALU.min))
            step(v.tensor_tensor(cum, cum, tot, ALU.subtract))
            step(v.tensor_tensor(Rm["eq"], Rm["eq"], bank[0][:, 0:TILES * E], ALU.add))
            step(stt(cum, over_t(starts), float(P), cum, ALU.mult, ALU.add))
            step(v.tensor_tensor(cum, cum, hot, ALU.mult))
            step(v.tensor_reduce(Rm["pos"], cum, X, ALU.add))
            step(v.tensor_copy(pos_i, Rm["pos"]))
            step(v.tensor_scalar(hi_i, pos_i, 7, None, ALU.logical_shift_right))
            step(v.tensor_scalar(lo_i, pos_i, P - 1, None, ALU.bitwise_and))
            step(v.tensor_copy(Rm["hi"], hi_i))
            step(v.tensor_copy(Rm["lo"], lo_i))
            lo_hot, hi_hot = split(Cm["lo_hot"], TILES), split(Cm["hi_hot"], TILES)
            hi_val = split(Cm["hi_val"], TILES)

            def wide(ap, n):
                return ap.rearrange("p (t o) -> p t o", o=1).broadcast_to([P, TILES, n])

            step(v.tensor_tensor(hi_hot, wide(Rm["hi"], SP_), over_t(Im["slot"]), ALU.is_equal))
            step(v.tensor_tensor(hi_val[:, :, 0:SP_], hi_hot, wide(Im["tok"], SP_), ALU.mult))
            step(v.tensor_tensor(hi_val[:, :, SP_:2 * SP_], hi_hot, wide(Rm["max"], SP_), ALU.mult))
            step(v.tensor_tensor(lo_hot, wide(Rm["lo"], P), over_t(Im["lane"]), ALU.is_equal))
            v.tensor_copy(Rm["pos"], Rm["hi"]).then_inc(S["c_slots"], 1)
            dve.wait_ge(S["c_prefix"], 2)
            vmap = Rm["cand"][:, 0:SP_]
            step(v.tensor_copy(vmap, bank[2][:, 0:SP_]))
            step(v.tensor_copy(slot_alpha, bank[2][:, SP_:2 * SP_]))
            v.tensor_scalar(gather_i, vmap, -1.0, 0.0, ALU.add, ALU.max).then_inc(S["c_map"], 1)
            none = Rm["cand"][:, SP_:2 * SP_]
            step(v.tensor_scalar(none, vmap, 0.0, float(2 * NB * T), ALU.is_equal, ALU.mult))
            step(stt(none, vmap, -1.0, none, ALU.add, ALU.add))
            v.tensor_copy(scatter_i, none).then_inc(S["c_map"], 1)

            def load_e(s):
                return dve.value_load(expert_i[0:1, bass.ds(s, 1)], min_val=0, max_val=E - 1)

            lng_f, lnb_f, b1_f = L["ln_g"], L["ln_b"], L["b1"]

            def affine(s):
                e = load_e(s)
                dve.wait_ge(S["d_xT_done"], s + 1)
                dve.wait_ge(S["d_h_done"], 2 * s)
                for k in range(KD):
                    v.tensor_scalar(xT_d[:, k, :], bank[0][:, k * P:(k + 1) * P], lng_f[:, bass.ds(e + k * E, 1)],
                                    lnb_f[:, bass.ds(e + k * E, 1)], ALU.mult, ALU.add).then_inc(S["d_xT_ready"], 1)

            def relu_hi(s, par):
                e = load_e(s)
                dve.wait_ge(S["d_hT_done"], 2 * s + 2)
                if not isinstance(s, int) or s > 0:
                    dve.wait_ge(S["d_y_done"], s - 1)
                for f in range(4, 8):
                    v.tensor_scalar(hT_d[par][:, f, :], bank[5][:, (f - 4) * P:(f - 3) * P],
                                    b1_f[:, bass.ds(e * KF + f, 1)], 0.0, ALU.add, ALU.max).then_inc(S["d_hT_dve"], 1)

            def finish(s, place, k, turn):
                e = load_e(s)
                dve.wait_ge(S["d_y_done"], s + 1)
                dve.wait_ge(scat[k], 16 * turn)
                v.tensor_tensor(o_d[:, k, :], bank[6][:, 0:D], Dm["b2"][:, bass.ds(e * D, D)], ALU.add).then_inc(S["d_yb"], 1)
                dve.wait_ge(S["d_yb"], s + 1)
                stt(o_d[:, k, :], o_d[:, k, :], slot_alpha[:, bass.ds(s, 1)], slot_rows[:, place, D:2 * D],
                    ALU.mult, ALU.add).then_inc(S["d_o_ready"], 1)

            dve.wait_ge(S["c_map"], 2)
            dve.wait_ge(S["c_step"], steps[0])
            dve.wait_ge(S["ld_b2"], 16)
            affine(0)
            affine(1)
            relu_hi(0, 0)
            affine(2)
            with dve.Fori(0, LOOP // RING) as it:
                for k in range(RING):
                    s = RING * it + k
                    relu_hi(s + 1, (k + 1) % 2)
                    affine(s + 3)
                    finish(s, k % RING, k % 3, 2 * it + k // 3)
            for s in range(LOOP, SLOTS):
                if s + 1 < SLOTS:
                    relu_hi(s + 1, (s + 1) % 2)
                if s + 3 < SLOTS:
                    affine(s + 3)
                finish(s, s % RING, s % 3, s // 3)


def kernel(**inputs):
    import numpy as np
    import concourse.bacc as bacc
    from concourse.bass_utils import run_bass_kernel_spmd

    def t(name, axes=None):
        a = np.asarray(inputs[name])
        return np.ascontiguousarray(a if axes is None else np.transpose(a, axes))

    def lanes(a):
        return a.reshape(a.shape[0] // P, P, -1).transpose(1, 0, 2).reshape(P, -1)

    b1 = t("L0_ffn_b1")
    lane_w = np.concatenate([
        lanes(t("L0_attn_conv_w")), lanes(t("L0_attn_conv_b")), lanes(t("L0_attn_D_param")),
        lanes(t("L0_attn_x_proj_w", (1, 0))[:, :t("L0_attn_dt_proj_w").shape[1]]),
        lanes(t("L0_xattn_bq")), lanes(t("L0_xattn_bk")), lanes(t("L0_ffn_centroids", (1, 0))),
        lanes(t("L0_ffn_ln_g", (1, 0))), lanes(t("L0_ffn_ln_b", (1, 0))),
        b1.reshape(b1.shape[0], -1, P).transpose(2, 0, 1).reshape(P, -1)], axis=1)
    arrays = [
        ("x", t("x")), ("ctx", t("ctx_512")), ("ctx_t", t("ctx_512", (0, 2, 1))),
        ("in_w_t", t("L0_attn_in_proj_w", (1, 0))), ("dt_w_t", t("L0_attn_dt_proj_w", (1, 0))),
        ("dt_b", t("L0_attn_dt_proj_b")), ("out_w_t", t("L0_attn_out_proj_w", (1, 0))),
        ("wq_t", t("L0_xattn_Wq", (1, 0))), ("wk_t", t("L0_xattn_Wk", (1, 0))),
        ("wv", t("L0_xattn_Wv")), ("bv", t("L0_xattn_bv")), ("lane_w", lane_w),
        ("w1_t", t("L0_ffn_w1", (0, 2, 1))), ("w2_t", t("L0_ffn_w2", (0, 2, 1))), ("b2", t("L0_ffn_b2")),
    ]
    nc = bacc.Bacc("TRN2", target_bir_lowering=False, num_devices=1)
    feeds, args = {}, []
    for name, a in arrays:
        feeds[f"in_{name}"] = a
        args.append(nc.dram_tensor(f"in_{name}", a.shape, mybir.dt.from_np(a.dtype), kind="ExternalInput").ap())
    shape = inputs["x"].shape
    args.append(nc.dram_tensor("layer_out", shape, F32, kind="ExternalOutput").ap())
    decoder_program(nc, *args)
    got = run_bass_kernel_spmd(nc, [feeds], core_ids=[0])
    return got.results[0]["layer_out"]
```

```python
from contextlib import ExitStack

import concourse.bass as bass
from concourse import mybir

F32 = mybir.dt.float32
F32R = mybir.dt.float32r
I32 = mybir.dt.int32
ALU = mybir.AluOpType
ACT = mybir.ActivationFunctionType
X = mybir.AxisListType.X

P = 128
EPS = 1e-5


def decoder_program(nc, x, ctx, ctx_t, in_w_t, dt_w_t, dt_b, out_w_t, wq_t, wk_t, wv, bv, lane_w,
                    w1_t, w2_t, b2, out):
    NB, T, D = x.shape
    C = ctx.shape[2]
    DI = out_w_t.shape[0]
    NS = dt_w_t.shape[0]
    E, _, F = w1_t.shape
    assert T == P and C == P and NS <= 31
    KD, KI, KF = D // P, DI // P, F // P
    GB = 4
    G = NB // GB
    GT = GB * T
    TILES = NB
    SLOTS = TILES + E - 1
    RING = 4
    SP_ = 40
    assert SLOTS <= SP_ and G == 8 and E == G and KI == GB and SLOTS % RING == 3

    rows_dram = nc.dram_tensor("token_rows", (NB * T, 2 * D), F32, kind="Internal").ap()

    with ExitStack() as stack:
        def sb(name, cols, dt=F32):
            return stack.enter_context(nc.sbuf_tensor(name, [P, cols], dt))

        def sem(name):
            return stack.enter_context(nc.semaphore(name))

        def split(ap, n):
            return ap.rearrange("p (n w) -> p n w", n=n)

        bank = [stack.enter_context(nc.psum_tensor(f"bank{i}", [P, 512], F32)) for i in range(8)]

        x_flat = sb("x_flat", NB * D)
        arena = sb("arena", 10240)
        x_res = split(x_flat[:, :], NB)

        ident = sb("ident", P)
        ones = sb("ones", P)
        before = sb("before", P)
        small = sb("small", 256)
        cols = [0]

        def piece(n):
            a = cols[0]
            cols[0] += n
            return small[:, a:a + n]

        neg_d = piece(KI)
        q_bias = piece(1)
        bk_proj = piece(KD)
        bq_bk = piece(1)
        shift = piece(GB)
        att_top = piece(GB)
        mhalf = piece(2 * GB)
        abs_sum, twice_relu, ln_sum, sp_sum, exp_a, exp_a1, alpha = (piece(GB) for _ in range(7))
        att_max, att_neg, att_sum, att_rcp = (piece(GB) for _ in range(4))
        att_nbias = piece(GB)
        xhat_nbias = piece(GB)
        ln_tmp = [(split(piece(6 * GB), GB), split(piece(2 * GB), GB), piece(n), piece(n)) for n in (GB, GB, 2 * GB)]
        assert cols[0] <= 256
        affs = split(sb("affs", TILES * E)[:, :], TILES)

        def take(ap, spots):
            out_, at = {}, 0
            for name, n in spots:
                out_[name] = ap[:, at:at + n]
                at += n
            assert at <= ap.shape[1], (at, ap.shape)
            return out_

        lane_parts = [("conv_w", 4 * KI), ("conv_b", KI), ("d", KI), ("xp", KI * NS), ("bq", KD), ("bk", KD),
                      ("cent", KD * E), ("ln_g", KD * E), ("ln_b", KD * E), ("b1", E * KF)]
        lane_sb = sb("lane_sb", sum(n for _, n in lane_parts))
        L = take(lane_sb[:, :], lane_parts)
        conv_w_sb, conv_b_sb, d_sb, xpw_sb = split(L["conv_w"], KI), L["conv_b"], L["d"], split(L["xp"], KI)
        bq_sb, bk_sb, cent_sb = L["bq"], L["bk"], split(L["cent"], KD)

        WEIGHTS_AT = 98272

        class Placed:
            def __init__(self, at):
                self.at = at

            def __call__(self, name, n, dt=F32):
                t = nc.alloc_sbuf_tensor_at(name, [P, n], dt, offset=self.at)
                self.at += 4 * ((n + 7) // 8 * 8)
                return t[:, :]

        put = Placed(WEIGHTS_AT)
        w1_sb = put("w1_sb", E * KD * F)
        w2_sb = put("w2_sb", E * KF * D)
        weights_end = put.at
        put = Placed(WEIGHTS_AT)
        inw_hi, inw_lo = split(put("inw_hi", KD * 2 * DI, F32R), KD), split(put("inw_lo", KD * 2 * DI, F32R), KD)
        xnT_hi, xnT_lo = split(put("xnT_hi", KD * GT, F32R), KD), split(put("xnT_lo", KD * GT, F32R), KD)
        b_stack = put("b_stack", GT, F32R)
        dtw_stack, dtw_round = put("dtw_stack", DI + 2, F32R), put("dtw_round", DI + 2, F32R)
        dtw_raw = put("dtw_raw", DI + 2)
        xnA = split(put("xnA", GB * D), GB)
        xc = split(put("xc", KI * GT), KI)
        xs = [split(put(f"xs{k}", KI * GT), KI) for k in range(2)]
        gz = [split(put(f"gz{k}", KI * GT), KI) for k in range(2)]
        uu_flat = put("uu", KI * GT)
        uu, inw_raw = split(uu_flat, KI), split(uu_flat, KD)
        yv = split(put("yv", KI * GT), KI)
        sp = split(put("sp", GB * DI), GB)
        alpha_all = put("alpha_all", GT)
        outw_sb = split(put("outw", KI * D), KI)
        assert put.at <= weights_end

        B = take(arena[:, :], [("row", GB * 2 * D), ("xlT", KD * GT), ("pr", GT), ("xn", GB * D), ("xnT", KD * GT),
                               ("q", GT), ("prT", GT), ("gT", GT), ("cT", GT), ("c", GT), ("xl", GB * D),
                               ("wk", KD * C), ("wqk", KD * C), ("wv", D), ("bv", D)])
        xnB, xlB = split(B["xn"], GB), split(B["xl"], GB)
        xnTB, xlTB = split(B["xnT"], KD), split(B["xlT"], KD)
        row = B["row"].rearrange("p (j h d) -> p j h d", j=GB, h=2)
        pr = split(B["pr"], GB)
        cT_sb, c_sb = B["cT"], split(B["c"], GB)
        wq_sb, wk_sb, wqk = split(B["gT"], KD), split(B["wk"], KD), split(B["wqk"], KD)
        Dm = take(arena[:, :], [("xT", KD * P), ("hT0", F), ("hT1", F), ("w1_0", KD * F), ("w1_1", KD * F),
                                ("o", 2 * D), ("b2", E * D)])
        b2_sb = split(Dm["b2"], E)
        slot_rows = split(x_flat[:, 0:RING * 2 * D], RING)
        w1_now = [Dm["w1_0"], Dm["w1_1"]]
        xT_d = split(Dm["xT"], KD)
        hT_d = [split(Dm["hT0"], KF), split(Dm["hT1"], KF)]
        o_d = split(Dm["o"], 2)
        Cm = take(x_flat[:, :], [("lo_hot", TILES * P), ("hi_hot", TILES * SP_), ("hi_val", TILES * 2 * SP_)])
        Rm = take(arena[:, 8960:10240], [("max", TILES), ("eq", TILES * E), ("cand", TILES * E), ("first", TILES),
                             ("hot", TILES * E), ("tot", TILES * E), ("pos", TILES), ("hi", TILES),
                             ("lo", TILES), ("ealpha", TILES)])
        slot_alpha = sb("slot_alpha", SP_)[:, :]
        routing_tmp = sb("routing_tmp", 3 * E)[:, :]
        iotas = sb("iotas", E + 2 * TILES + P + SP_)
        Im = take(iotas[:, :], [("e8", E), ("k128", TILES), ("lane", P), ("slot", SP_), ("tok", TILES)])
        gather_cols, scatter_cols = sb("gather_cols", RING, I32), sb("scatter_cols", 2, I32)
        gather_col = [gather_cols[:, k:k + 1] for k in range(RING)]
        scatter_col = [scatter_cols[:, k:k + 1] for k in range(2)]
        idx = sb("idx", 4 * TILES + 3 * SP_, I32)
        pos_i, hi_i, lo_i = (idx[:, k * TILES:(k + 1) * TILES] for k in range(3))
        gather_i, scatter_i, expert_i = (idx[:, 4 * TILES + k * SP_:4 * TILES + (k + 1) * SP_] for k in range(3))

        names = """ld_x0 ld_x1 ld_x ld_inw ld_lane ld_dt ld_outw ld_wb ld_ct ld_c ld_w1 ld_w2 ld_b2
            fills_set dt_zeroed ident_set consts_set neg_d_set dt_rowsum dt_rounded dt_split inw_hi_set inw_lo_set
            a_transposed a_xnT_hi a_xnT_lo a_x_done a_z_done a_first_tap a_taps a_xs a_gz
            a_xp_done a_b_hi a_b_lo a_dt_done a_abs a_exp a_ln a_twice_relu a_sp_sum a_exp_a a_exp_a1 a_alpha
            a_alpha_rows a_alpha_copied a_alpha_zeroed a_u a_scan a_y a_gated a_out_done a_resid
            b_prep b_prep_copied b_transposed b_xnT_ready b_q_done b_q_ready b_scores b_max b_top b_neg b_probs b_rcp
            b_prT_done b_prT_ready b_g_done b_gT_ready b_v_done b_xbv b_x2 b_nbias b_xhat_nbias b_xhat b_xl_transposed b_xlT_ready
            b_stage_done b_stage_copied b_base b_rows_out
            c_step c_ealpha c_prefix c_hi_hot c_slots c_experts c_map
            d_gather_col d_scatter_col d_xT_done d_xT_ready d_w1_copied d_h_done d_hT_act d_hT_dve d_y_done d_yb
            d_o_ready d_scattered_0 d_scattered_1""".split()
        S = {n: sem(n) for n in names}
        lns = [{k: sem(f"ln{i}_{k}") for k in ("stats", "aggr", "eps", "rstd", "out")} for i in range(3)]
        gath = [sem(f"d_gathered_{i}") for i in range(RING)]
        scat = [S[f"d_scattered_{i}"] for i in range(2)]

        def ln_stats(dve, which, g):
            stats, mv, var, _ = ln_tmp[which]
            s = lns[which]
            dve.nop(nofuse=True)
            for j in range(GB):
                nc.vector.bn_stats(stats[:, j, :], x_flat[:, bass.ds(g * (GB * D) + j * D, D)]).then_inc(s["stats"], 1)
            for j in range(GB):
                dve.wait_ge(s["stats"], GB * g + j + 1)
                dve.nop(nofuse=True)
                nc.vector.bn_aggr(mv[:, j, :], stats[:, j, :]).then_inc(s["aggr"], 1)
            dve.wait_ge(s["aggr"], GB * g + GB)
            if which == 2:
                nc.vector.tensor_scalar(var[:, GB:2 * GB], mv[:, :, 1], 1 + EPS, EPS * EPS, ALU.mult, ALU.add)
            nc.vector.tensor_scalar(var[:, 0:GB], mv[:, :, 1], EPS, None, ALU.add).then_inc(s["eps"], 1)

        def ln_rstd(pool, which, g):
            _, _, var, rstd = ln_tmp[which]
            s = lns[which]
            pool.wait_ge(s["eps"], g + 1)
            nc.gpsimd.tensor_tensor(rstd, var, mhalf[:, 0:var.shape[1]], ALU.pow).then_inc(s["rstd"], 1)

        def ln_apply(dve, which, g, rstd, src, dst, done):
            mv = ln_tmp[which][1]
            for j in range(GB):
                nc.vector.tensor_scalar(dst(j), src(j), mv[:, j, 0:1], rstd[:, j:j + 1],
                                        ALU.subtract, ALU.mult).then_inc(done, 1)

        def x_tile(g, j):
            return x_flat[:, bass.ds(g * (GB * D) + j * D, D)]

        PEEL = 4
        LOOP = SLOTS // RING * RING

        block = stack.enter_context(nc.Block())

        @block.sync
        def _(sp_):
            xv = x.rearrange("b t d -> t b d")
            sp_.dma_start(x_res[:, 0:GB, :], xv[:, 0:GB, :]).then_inc(S["ld_x0"], 16)
            sp_.dma_start(lane_sb[:, :], lane_w).then_inc(S["ld_lane"], 16)
            sp_.wait_ge(S["dt_zeroed"], 1)
            for at in (0, 32, 64):
                sp_.dma_start(dtw_raw[at:at + NS, 0:DI], dt_w_t).then_inc(S["ld_dt"], 16)
                sp_.dma_start(dtw_raw[at + NS:at + NS + 1, 0:DI], dt_b.rearrange("(o n) -> o n", o=1)) \
                    .then_inc(S["ld_dt"], 16)
            sp_.dma_start(x_res[:, GB:2 * GB, :], xv[:, GB:2 * GB, :]).then_inc(S["ld_x1"], 16)
            sp_.dma_start(outw_sb, out_w_t.rearrange("(c p) n -> p c n", p=P)).then_inc(S["ld_outw"], 16)
            sp_.dma_start(x_res[:, 2 * GB:NB, :], xv[:, 2 * GB:NB, :]).then_inc(S["ld_x"], 16)
            sp_.dma_start(wq_sb, wq_t.rearrange("(k p) n -> p k n", p=P)).then_inc(S["ld_wb"], 16)
            sp_.dma_start(wk_sb, wk_t.rearrange("(k p) n -> p k n", p=P)).then_inc(S["ld_wb"], 16)
            sp_.dma_start(B["wv"], wv).then_inc(S["ld_wb"], 16)
            sp_.dma_start(B["bv"], bv.rearrange("(o n) -> o n", o=1).broadcast_to([P, D])).then_inc(S["ld_wb"], 16)

            ctv = ctx_t.rearrange("b c t -> c b t")
            cv = ctx.rearrange("b t c -> t b c")
            sp_.dma_start(split(cT_sb, GB), ctv[:, 0:GB, :]).then_inc(S["ld_ct"], 16)
            sp_.dma_start(c_sb, cv[:, 0:GB, :]).then_inc(S["ld_c"], 16)

            def expert_weights(e):
                sp_.dma_start(split(w1_sb[:, bass.ds(e * (KD * F), KD * F)], KD),
                              w1_t[bass.ds(e, 1)].rearrange("o (k p) f -> p (o k) f", p=P)).then_inc(S["ld_w1"], 16)
                sp_.dma_start(split(w2_sb[:, bass.ds(e * (KF * D), KF * D)], KF),
                              w2_t[bass.ds(e, 1)].rearrange("o (k p) d -> p (o k) d", p=P)).then_inc(S["ld_w2"], 16)

            def next_ct(g):
                sp_.wait_ge(S["b_scores"], g + 1)
                sp_.dma_start(split(cT_sb, GB), ctv[:, bass.ds((g + 1) * GB, GB), :]).then_inc(S["ld_ct"], 16)

            def next_c(g):
                sp_.wait_ge(S["b_g_done"], g + 1)
                sp_.dma_start(c_sb, cv[:, bass.ds((g + 1) * GB, GB), :]).then_inc(S["ld_c"], 16)

            def rows_out(g):
                sp_.wait_ge(S["b_xhat"], GB * g + GB)
                sp_.wait_ge(S["b_base"], GB * g + GB)
                sp_.dma_start(rows_dram.rearrange("(b t) w -> t b w", t=T)[:, bass.ds(g * GB, GB), :],
                              B["row"].rearrange("p (j w) -> p j w", j=GB)).then_inc(S["b_rows_out"], 16)

            next_ct(0)
            sp_.wait_ge(S["a_resid"], 2 * G)
            next_ct(1)
            next_c(0)
            expert_weights(0)
            with sp_.Fori(1, G - 2) as g:
                next_ct(g + 1)
                next_c(g)
                rows_out(g - 1)
                expert_weights(g)
            next_c(G - 2)
            rows_out(G - 3)
            expert_weights(G - 2)
            rows_out(G - 2)
            expert_weights(G - 1)
            rows_out(G - 1)

            sp_.wait_ge(S["b_rows_out"], 16 * G)
            sp_.wait_ge(S["b_xl_transposed"], KD * G)
            sp_.dma_start(b2_sb, b2.rearrange("(o e) d -> o e d", o=1).broadcast_to([P, E, D])).then_inc(S["ld_b2"], 16)

        @block.gpsimd
        def _(pool):
            nc.gpsimd.memset(dtw_raw, 0.0).then_inc(S["dt_zeroed"], 1)
            nc.gpsimd.memset(mhalf, -0.5).then_inc(S["fills_set"], 1)
            nc.gpsimd.memset(ones[:, :], 1.0).then_inc(S["fills_set"], 1)
            nc.gpsimd.memset(b_stack.bitcast(F32), 0.0).then_inc(S["fills_set"], 1)
            pool.wait_ge(S["fills_set"], 3)
            nc.gpsimd.affine_select(out=ident[:, :], in_=ones[:, :], compare_op=ALU.is_equal, fill=0.0, base=0,
                                    pattern=[[-1, P]], channel_multiplier=1).then_inc(S["ident_set"], 1)
            nc.gpsimd.affine_select(out=before[:, :], in_=ones[:, :], compare_op=ALU.is_gt, fill=0.0, base=0,
                                    pattern=[[1, P]], channel_multiplier=-1).then_inc(S["ident_set"], 1)
            nc.gpsimd.memset(b_stack[0:NS + 1, :].bitcast(F32), 1.0).then_inc(S["fills_set"], 1)
            pool.wait_ge(S["ident_set"], 2)
            pool.wait_ge(S["fills_set"], 4)
            nc.gpsimd.memset(b_stack[64:64 + NS + 1, :].bitcast(F32), 1.0).then_inc(S["fills_set"], 1)

            pool.wait_ge(S["fills_set"], 5)

            def gated(g, par):
                for c in range(KI):
                    pool.wait_ge(S["a_y"], KI * g + c + 1)
                    nc.gpsimd.tensor_tensor(yv[:, c, :], yv[:, c, :], gz[par][:, c, :], ALU.mult) \
                        .then_inc(S["a_gated"], 1)

            ln_rstd(pool, 0, 0)
            ln_rstd(pool, 0, 1)
            for name, base, step, per_lane in (("e8", -E, 1, 0), ("k128", 0, P, 0), ("lane", 0, 1, 0),
                                               ("slot", 0, 1, 0), ("tok", 1, P, 1)):
                nc.gpsimd.iota(Im[name], pattern=[[step, Im[name].shape[1]]], base=base, channel_multiplier=per_lane,
                               allow_small_or_imprecise_dtypes=True).then_inc(S["consts_set"], 1)
            ln_rstd(pool, 0, 2)
            gated(0, 0)
            with pool.Fori(0, (G - 4) // 2) as it:
                for k in range(2):
                    ln_rstd(pool, 0, 2 * it + k + 3)
                    gated(2 * it + k + 1, (k + 1) % 2)
            ln_rstd(pool, 0, G - 1)
            gated(G - 3, 1)
            gated(G - 2, 0)
            ln_rstd(pool, 1, 0)
            gated(G - 1, 1)

            def add_bv(g):
                pool.wait_ge(lns[1]["out"], GB * g + GB)
                pool.nop(nofuse=True)
                for j in range(GB):
                    nc.gpsimd.tensor_tensor(x_tile(g, j), x_tile(g, j), B["bv"], ALU.add).then_inc(S["b_xbv"], 1)

            def base_rows(g):
                if not isinstance(g, int) or g > 0:
                    pool.wait_ge(S["b_rows_out"], 16 * g)
                for j in range(GB):
                    pool.wait_ge(lns[2]["out"], GB * g + j + 1)
                    pool.nop(nofuse=True)
                    nc.gpsimd.tensor_tensor(row[:, j, 1, :], x_tile(g, j), xlB[:, j, :], ALU.add) \
                        .then_inc(S["b_base"], 1)

            def rstd_b(g):
                pool.wait_ge(lns[1]["out"], GB * g)
                ln_rstd(pool, 1, g)

            rstd_b(1)
            pool.wait_ge(S["ld_wb"], 16 * 4)
            add_bv(0)
            rstd_b(2)

            def step_b(i, has_next, has_stats):
                if has_stats:
                    rstd_b(i + 3)
                if has_next:
                    add_bv(i + 1)
                if not isinstance(i, int) or i > 0:
                    pool.wait_ge(S["b_xhat"], GB * i)
                ln_rstd(pool, 2, i)
                base_rows(i)

            step_b(0, True, True)
            with pool.Fori(1, G - 3) as i:
                step_b(i, True, True)
            step_b(G - 3, True, False)
            step_b(G - 2, True, False)
            step_b(G - 1, False, False)

            def gather(s, k, after=None):
                if after is not None:
                    pool.wait_ge(S["d_xT_done"], after + 1)
                    pool.nop(nofuse=True)
                nc.gpsimd.tensor_copy(gather_col[k], gather_i[:, bass.ds(s, 1)]).then_inc(S["d_gather_col"], 1)
                if after is not None:
                    pool.wait_ge(S["d_o_ready"], after + 1)
                pool.wait_ge(S["d_gather_col"], s + 1)
                pool.nop(nofuse=True)
                nc.gpsimd.indirect_dma_start(
                    out=slot_rows[:, k, :], out_offset=None, in_=rows_dram,
                    in_offset=bass.IndirectOffsetOnAxis(ap=gather_col[k], axis=0)).then_inc(gath[k], 16)

            def scatter(s, k):
                pool.wait_ge(S["d_o_ready"], s + 1)
                pool.nop(nofuse=True)
                nc.gpsimd.tensor_copy(scatter_col[k], scatter_i[:, bass.ds(s, 1)]).then_inc(S["d_scatter_col"], 1)
                pool.wait_ge(S["d_scatter_col"], s + 1)
                pool.nop(nofuse=True)
                nc.gpsimd.indirect_dma_start(
                    out=out.rearrange("b t d -> (b t) d"), in_=o_d[:, k, :], in_offset=None,
                    out_offset=bass.IndirectOffsetOnAxis(ap=scatter_col[k], axis=0),
                    bounds_check=NB * T - 1, oob_is_err=False).then_inc(scat[k], 16)

            pool.wait_ge(S["b_rows_out"], 16 * G)
            pool.wait_ge(S["b_stage_copied"], G + 3)
            pool.wait_ge(S["c_map"], 1)
            for s in range(RING):
                gather(s, s)
            pool.wait_ge(S["c_map"], 2)

            def serve(s, k, more=True):
                if more:
                    gather(s + RING, k, after=s)
                scatter(s, k % 2)

            with pool.Fori(0, LOOP // RING - 1) as it:
                for k in range(RING):
                    serve(RING * it + k, k)
            for s in range(LOOP - RING, SLOTS):
                serve(s, s % RING, s + RING < SLOTS)
            pool.wait_ge(scat[0], 16 * ((SLOTS + 1) // 2))
            pool.wait_ge(scat[1], 16 * (SLOTS // 2))

        @block.tensor
        def _(pe):
            matmul = nc.tensor.matmul

            def transpose_xn(g):
                pe.wait_ge(lns[0]["out"], GB * g + GB)
                for k in range(KD):
                    if not isinstance(g, int) or g > 0:
                        pe.wait_ge(S["a_gz"], KI * (g - 1) + k + 1)
                    for j in range(GB):
                        mm = nc.tensor.transpose(bank[k][:, j * P:(j + 1) * P], xnA[:, j, k * P:(k + 1) * P], ident[:, :])
                    mm.then_inc(S["a_transposed"], 1)

            def in_proj(g, c, first_col, to, done):
                lhs = [w[:, k, first_col + c * P:first_col + (c + 1) * P] for w in (inw_hi, inw_lo) for k in range(KD)]
                for k in range(2 * KD):
                    pe.wait_ge(S["a_xnT_hi"], KD * g + k % KD + 1)
                    matmul(to, lhs[k], xnT_hi[:, k % KD, :], start=(k == 0), stop=False)
                for k in range(KD):
                    pe.wait_ge(S["a_xnT_lo"], KD * g + k + 1)
                    mm = matmul(to, lhs[k], xnT_lo[:, k, :], start=False, stop=(k == KD - 1))
                mm.then_inc(done, 1)

            def x_part(g):
                for c in range(KI):
                    if not isinstance(g, int) or g > 0:
                        pe.wait_ge(S["a_abs"], GB * (g - 1) + c + 1)
                    in_proj(g, c, 0, bank[2 + c][:, :], S["a_x_done"])

            def z_part(g, resid_before=True):
                for c in range(KI):
                    if c >= 2:
                        pe.wait_ge(S["a_taps"], 3 * KI * g + 2 * KI + c - 1)
                    elif resid_before:
                        pe.wait_ge(S["a_resid"], 2 * (g - 2) + c + 1)
                    in_proj(g, c, DI, bank[c][:, :], S["a_z_done"])

            def x_proj(g, par):
                for c in range(KI):
                    pe.wait_ge(S["a_xs"], KI * g + c + 1)
                    mm = matmul(bank[6][0:NS, :], xpw_sb[:, c, :], xs[par][:, c, :], start=(c == 0), stop=(c == KI - 1))
                mm.then_inc(S["a_xp_done"], 1)

            def dt_proj(g):
                pe.wait_ge(S["a_b_hi"], 2 * g + 2)
                pe.wait_ge(S["a_b_lo"], g + 1)
                for j in range(GB):
                    if j < 2:
                        pe.wait_ge(S["a_gz"], KI * g + j + 3)
                    tokens = b_stack[:, j * P:(j + 1) * P]
                    matmul(bank[2 + j][:, :], tokens, dtw_stack[:, 0:DI], start=True, stop=True).then_inc(S["a_dt_done"], 1)
                for j in range(GB):
                    mm = matmul(bank[6][:, 2 * j:2 * j + 2], b_stack[:, j * P:(j + 1) * P], dtw_stack[:, DI:DI + 2],
                                start=True, stop=True)
                mm.then_inc(S["a_dt_done"], 1)

            def alpha_rows(g):
                pe.wait_ge(S["a_alpha"], g + 1)
                for j in range(GB):
                    mm = matmul(bank[7][:, j * P:(j + 1) * P], alpha[:, j:j + 1].broadcast_to([P, P]), ident[:, :],
                                start=True, stop=True)
                mm.then_inc(S["a_alpha_rows"], 1)

            def out_proj(g):
                pe.wait_ge(S["a_gated"], KI * g + KI)
                for j in range(GB):
                    for c in range(KI):
                        mm = matmul(bank[j // 2][:, (j % 2) * D:(j % 2) * D + D],
                                    yv[:, c, j * P:(j + 1) * P], outw_sb[:, c, :], start=(c == 0), stop=(c == KI - 1))
                    mm.then_inc(S["a_out_done"], 1)

            def step_a(g, par, has_prev=True, has_next=True):
                x_proj(g, par)
                if has_next:
                    transpose_xn(g + 1)
                dt_proj(g)
                if has_next:
                    x_part(g + 1)
                if has_prev:
                    out_proj(g - 1)
                alpha_rows(g)
                if has_next:
                    z_part(g + 1, has_prev)

            pe.wait_ge(S["ident_set"], 2)
            transpose_xn(0)
            pe.wait_ge(S["inw_hi_set"], 1)
            pe.wait_ge(S["inw_lo_set"], 1)
            x_part(0)
            z_part(0, False)
            pe.wait_ge(S["dt_split"], 1)
            pe.wait_ge(S["ld_outw"], 16)
            step_a(0, 0, has_prev=False)
            with pe.Fori(0, (G - 4) // 2) as it:
                for k in range(2):
                    step_a(2 * it + k + 1, (k + 1) % 2)
            step_a(G - 3, 1)
            step_a(G - 2, 0)
            step_a(G - 1, 1, has_next=False)

            pe.wait_ge(S["ld_wb"], 16 * 4)
            pe.wait_ge(S["a_abs"], GB * G)
            for k in range(KD):
                for e in range(KD):
                    matmul(bank[4][:, k * C:(k + 1) * C], wq_sb[:, e, k * P:(k + 1) * P], wk_sb[:, e, :],
                           start=(e == 0), stop=(e == KD - 1))
            for e in range(KD):
                matmul(bank[4][:, 2 * C:2 * C + 1], wk_sb[:, e, :], bq_sb[:, e:e + 1],
                       start=(e == 0), stop=(e == KD - 1))
            for k in range(KD):
                for e in range(KD):
                    matmul(bank[4][:, 2 * C + 2 + k:2 * C + 3 + k], wq_sb[:, e, k * P:(k + 1) * P],
                           bk_sb[:, e:e + 1], start=(e == 0), stop=(e == KD - 1))
            for e in range(KD):
                mm = matmul(bank[4][:, 2 * C + 4:2 * C + 5], bq_sb[:, e:e + 1].broadcast_to([P, P]),
                            bk_sb[:, e:e + 1], start=(e == 0), stop=(e == KD - 1))
            mm.then_inc(S["b_prep"], 1)

            def transpose_b(src, done):
                for k in range(KD):
                    for j in range(GB):
                        mm = nc.tensor.transpose(bank[k][:, j * P:(j + 1) * P], src[:, j, k * P:(k + 1) * P], ident[:, :])
                    mm.then_inc(done, 1)

            def xn_t(n):
                pe.wait_ge(lns[1]["out"], GB * n + GB)
                transpose_b(xnB, S["b_transposed"])

            def xl_t(n, n_xn):
                pe.wait_ge(lns[2]["out"], GB * n + GB)
                pe.wait_ge(S["b_xnT_ready"], KD * n_xn)
                transpose_b(xlB, S["b_xl_transposed"])

            def q_part(n):
                pe.wait_ge(S["b_xnT_ready"], KD * n + KD)
                for k in range(KD):
                    mm = matmul(bank[4][:, :], wqk[:, k, :], xnTB[:, k, :], start=(k == 0), stop=(k == KD - 1))
                mm.then_inc(S["b_q_done"], 1)

            def scores(n):
                pe.wait_ge(S["b_q_ready"], n + 1)
                pe.wait_ge(S["ld_ct"], 16 * n + 16)
                for j in range(GB):
                    mm = matmul(bank[5][:, j * P:(j + 1) * P], B["q"][:, j * P:(j + 1) * P],
                                cT_sb[:, j * P:(j + 1) * P], start=True, stop=True)
                mm.then_inc(S["b_scores"], 1)

            def probs_t(i):
                pe.wait_ge(S["b_probs"], GB * i + GB)
                for j in range(GB):
                    mm = nc.tensor.transpose(bank[6][:, j * P:(j + 1) * P], pr[:, j, :], ident[:, :])
                mm.then_inc(S["b_prT_done"], 1)

            def g_part(i, stages):
                pe.wait_ge(S["b_prT_ready"], i + 1)
                pe.wait_ge(S["ld_c"], 16 * i + 16)
                pe.wait_ge(S["b_stage_copied"], stages)
                for j in range(GB):
                    mm = matmul(bank[7][:, j * P:(j + 1) * P], c_sb[:, j, :], B["prT"][:, j * P:(j + 1) * P],
                                start=True, stop=True)
                mm.then_inc(S["b_g_done"], 1)

            def v_part(i):
                pe.wait_ge(S["b_gT_ready"], i + 1)
                for j in range(GB):
                    if j % 2 == 0 and (not isinstance(i, int) or i > 0):
                        pe.wait_ge(S["b_x2"], GB * (i - 1) + j + 2)
                    matmul(bank[2 + j // 2][:, (j % 2) * D:(j % 2) * D + D], B["gT"][:, j * P:(j + 1) * P],
                           B["wv"], start=True, stop=True).then_inc(S["b_v_done"], 1)

            def stage(n, with_shift=True, with_aff=True):
                if with_shift:
                    pe.wait_ge(S["b_xnT_ready"], KD * n + KD)
                    for j in range(GB):
                        for k in range(KD):
                            mm = matmul(bank[7][:, GB * E + j:GB * E + j + 1], xnTB[:, k, j * P:(j + 1) * P],
                                        bk_proj[:, k:k + 1], start=(k == 0), stop=(k == KD - 1))
                if with_aff:
                    pe.wait_ge(S["b_xlT_ready"], KD * (n - 3) + KD)
                    for j in range(GB):
                        for k in range(KD):
                            mm = matmul(bank[7][:, j * E:(j + 1) * E], xlTB[:, k, j * P:(j + 1) * P],
                                        cent_sb[:, k, :], start=(k == 0), stop=(k == KD - 1))
                mm.then_inc(S["b_stage_done"], 1)

            pe.wait_ge(S["b_prep_copied"], 1)
            pe.wait_ge(S["a_resid"], 2 * (G - 1))
            xn_t(0)
            q_part(0)
            out_proj(G - 1)
            stage(0, with_aff=False)
            scores(0)
            pe.wait_ge(S["a_resid"], 2 * G)
            xn_t(1)
            q_part(1)
            pe.wait_ge(S["b_stage_copied"], 1)
            stage(1, with_aff=False)

            def step_b(i, has_prev=True, has_next=True, has_stage=True, has_xn=True):
                probs_t(i)
                if has_next:
                    scores(i + 1)
                if has_xn:
                    xn_t(i + 2)
                g_part(i, i + 2)
                if has_prev:
                    xl_t(i - 1, i + 3 if has_xn else G)
                v_part(i)
                if has_stage:
                    stage(i + 2, with_shift=has_xn, with_aff=has_prev)
                if has_xn:
                    q_part(i + 2)

            step_b(0, has_prev=False)
            with pe.Fori(1, G - 3) as i:
                step_b(i)
            step_b(G - 3)
            step_b(G - 2, has_xn=False)
            step_b(G - 1, has_next=False, has_xn=False)
            pe.wait_ge(S["b_xlT_ready"], KD * (G - 1))
            xl_t(G - 1, G)
            pe.wait_ge(S["b_stage_copied"], G + 2)
            stage(G + 2, with_shift=False)

            pe.wait_ge(S["c_step"], 5)
            matmul(bank[0][:, 0:TILES * E], before[:, :], Rm["hot"], start=True, stop=True)
            matmul(bank[1][:, 0:TILES * E], ones[:, :], Rm["hot"], start=True, stop=True).then_inc(S["c_prefix"], 1)
            for j in range(TILES):
                pe.wait_ge(S["c_slots"], j // GB + 1)
                mm = matmul(bank[2][:, 0:2 * SP_], split(Cm["lo_hot"], TILES)[:, j, :],
                            split(Cm["hi_val"], TILES)[:, j, :], start=(j == 0), stop=(j == TILES - 1))
            mm.then_inc(S["c_prefix"], 1)

            def xT(s, k, turn):
                pe.wait_ge(gath[k], 16 * turn + 16)
                for d in range(KD):
                    mm = nc.tensor.transpose(bank[0][:, d * P:(d + 1) * P], slot_rows[:, k, d * P:(d + 1) * P], ident[:, :])
                mm.then_inc(S["d_xT_done"], 1)

            def hidden(s, par):
                pe.wait_ge(S["d_w1_copied"], s + 1)
                pe.wait_ge(S["d_xT_ready"], KD * s + KD)
                for half in range(2):
                    for f in range(KF // 2):
                        at = (half * KF // 2 + f) * P
                        for k in range(KD):
                            mm = matmul(bank[2 + 2 * par + half][:, f * P:(f + 1) * P],
                                        w1_now[par][:, k * F + at:k * F + at + P], xT_d[:, k, :],
                                        start=(k == 0), stop=(k == KD - 1))
                    mm.then_inc(S["d_h_done"], 1)

            def y_part(s, par):
                e = pe.value_load(expert_i[0:1, bass.ds(s, 1)], min_val=0, max_val=E - 1)
                if not isinstance(s, int) or s > 0:
                    pe.wait_ge(S["d_yb"], s)
                for f in range(KF):
                    pe.wait_ge(S["d_hT_act"] if f < 4 else S["d_hT_dve"], 4 * s + f % 4 + 1)
                    mm = matmul(bank[6][:, 0:D], hT_d[par][:, f, :], w2_sb[:, bass.ds(e * (KF * D) + f * D, D)],
                                start=(f == 0), stop=(f == KF - 1))
                mm.then_inc(S["d_y_done"], 1)

            def slot(s, k, turn, ahead=2):
                if ahead > 0:
                    hidden(s + 1, (k + 1) % 2)
                if ahead > 1:
                    xT(s + 2, (k + 2) % RING, turn)
                y_part(s, k % 2)

            pe.wait_ge(S["c_map"], 2)
            xT(0, 0, 0)
            hidden(0, 0)
            xT(1, 1, 0)
            pe.wait_ge(S["ld_w2"], 16 * E)
            for s in range(PEEL):
                slot(s, s, (s + 2) // RING)
            with pe.Fori(0, (LOOP - PEEL) // RING) as it:
                for k in range(RING):
                    slot(RING * it + k + PEEL, k, it + 1 + (k + 2) // RING)
            for s in range(LOOP, SLOTS):
                slot(s, s % RING, (s + 2) // RING, ahead=min(2, SLOTS - 1 - s))

        @block.scalar
        def _(act):
            act_ = nc.scalar.activation
            act.dma_start(inw_raw, in_w_t.rearrange("(k p) n -> p k n", p=P)).then_inc(S["ld_inw"], 16)

            def copy_xnT(g):
                for k in range(KD):
                    act.wait_ge(S["a_transposed"], KD * g + k + 1)
                    act_(xnT_hi[:, k, :], bank[k][:, :], ACT.Copy).then_inc(S["a_xnT_hi"], 1)

            def first_tap(g):
                for c in range(KI):
                    act.wait_ge(S["a_x_done"], KI * g + c + 1)
                    act_(xc[:, c, :], bank[2 + c][:, :], ACT.Identity, bias=conv_b_sb[:, c:c + 1],
                         scale=conv_w_sb[:, c, 3:4]).then_inc(S["a_first_tap"], 1)

            def silu_x(g, par):
                for c in range(KI):
                    act.wait_ge(S["a_taps"], 3 * KI * g + 2 * KI + c + 1)
                    act_(xs[par][:, c, :], xc[:, c, :], ACT.Silu).then_inc(S["a_xs"], 1)

            def silu_z(g, par):
                for c in range(KI):
                    act.wait_ge(S["a_z_done"], KI * g + c + 1)
                    act_(gz[par][:, c, :], bank[c][:, :], ACT.Silu).then_inc(S["a_gz"], 1)

            def copy_b(g):
                act.wait_ge(S["a_xp_done"], g + 1)
                act_(b_stack[0:NS, :], bank[6][0:NS, :], ACT.Copy).then_inc(S["a_b_hi"], 1)
                act.wait_ge(S["a_b_hi"], 2 * g + 1)
                act_(b_stack[64:64 + NS, :], b_stack[0:NS, :], ACT.Copy).then_inc(S["a_b_hi"], 1)

            def softplus_exp(g):
                for j in range(GB):
                    act.wait_ge(S["a_dt_done"], (GB + 1) * g + j + 1)
                    act_(sp[:, j, :], bank[2 + j][:, :], ACT.Abs, accum_out=abs_sum[:, j:j + 1]).then_inc(S["a_abs"], 1)
                for j in range(GB):
                    act.wait_ge(S["a_abs"], GB * g + j + 1)
                    act_(sp[:, j, :], sp[:, j, :], ACT.Exp, scale=-1.0).then_inc(S["a_exp"], 1)

            def softplus_ln(g):
                for j in range(GB):
                    act.wait_ge(S["a_exp"], GB * g + j + 1)
                    act_(sp[:, j, :], sp[:, j, :], ACT.Ln, bias=1.0, accum_out=ln_sum[:, j:j + 1]).then_inc(S["a_ln"], 1)

            def exp_alpha(g):
                act.wait_ge(S["a_sp_sum"], g + 1)
                act_(exp_a, sp_sum, ACT.Exp, scale=-1.0 / DI).then_inc(S["a_exp_a"], 1)

            def copy_alpha(g):
                act.wait_ge(S["a_alpha_rows"], g + 1)
                act_(alpha_all, bank[7][:, :], ACT.Copy).then_inc(S["a_alpha_copied"], 1)

            act.wait_ge(S["ld_inw"], 16)
            act_(inw_hi, inw_raw, ACT.Copy).then_inc(S["inw_hi_set"], 1)
            copy_xnT(0)
            act.wait_ge(S["ld_lane"], 16)
            first_tap(0)
            silu_x(0, 0)
            silu_z(0, 0)
            act.wait_ge(S["fills_set"], 5)

            def step_a(g, par, has_next=True):
                copy_b(g)
                if has_next:
                    copy_xnT(g + 1)
                softplus_exp(g)
                if has_next:
                    first_tap(g + 1)
                softplus_ln(g)
                exp_alpha(g)
                copy_alpha(g)
                if has_next:
                    silu_x(g + 1, 1 - par)
                    silu_z(g + 1, 1 - par)

            step_a(0, 0)
            with act.Fori(0, (G - 4) // 2) as it:
                for k in range(2):
                    step_a(2 * it + k + 1, (k + 1) % 2)
            step_a(G - 3, 1)
            step_a(G - 2, 0)
            step_a(G - 1, 1, has_next=False)

            def normalise(n):
                act.wait_ge(S["b_nbias"], n + 1)
                if not isinstance(n, int) or n > 0:
                    act.wait_ge(S["b_transposed"], KD * n)
                for j in range(GB):
                    act_(xnB[:, j, :], x_tile(n, j), ACT.Identity, bias=att_nbias[:, j:j + 1],
                         scale=ln_tmp[1][3][:, j:j + 1]).then_inc(lns[1]["out"], 1)

            def copy_xn_t(n):
                for k in range(KD):
                    act.wait_ge(S["b_transposed"], KD * n + k + 1)
                    act_(xnTB[:, k, :], bank[k][:, :], ACT.Copy).then_inc(S["b_xnT_ready"], 1)

            def copy_xl_t(n):
                for k in range(KD):
                    act.wait_ge(S["b_xl_transposed"], KD * n + k + 1)
                    act_(xlTB[:, k, :], bank[k][:, :], ACT.Copy).then_inc(S["b_xlT_ready"], 1)

            def copy_q(n):
                act.wait_ge(S["b_q_done"], n + 1)
                act_(B["q"], bank[4][:, :], ACT.Identity, bias=q_bias).then_inc(S["b_q_ready"], 1)

            def exp_scores(n):
                act.wait_ge(S["b_neg"], n + 1)
                for j in range(GB):
                    act_(pr[:, j, :], bank[5][:, j * P:(j + 1) * P], ACT.Exp, bias=att_neg[:, j:j + 1],
                         accum_out=att_sum[:, j:j + 1]).then_inc(S["b_probs"], 1)

            def xhat(i):
                act.wait_ge(S["b_xhat_nbias"], i + 1)
                if not isinstance(i, int) or i > 0:
                    act.wait_ge(S["b_rows_out"], 16 * i)
                for j in range(GB):
                    act_(row[:, j, 0, :], x_tile(i, j), ACT.Identity, bias=xhat_nbias[:, j:j + 1],
                         scale=ln_tmp[2][3][:, GB + j:GB + j + 1]).then_inc(S["b_xhat"], 1)

            def copy_prT(i):
                act.wait_ge(S["b_prT_done"], i + 1)
                act_(B["prT"], bank[6][:, :], ACT.Copy).then_inc(S["b_prT_ready"], 1)

            def copy_gT(i):
                act.wait_ge(S["b_g_done"], i + 1)
                act_(B["gT"], bank[7][:, :], ACT.Copy).then_inc(S["b_gT_ready"], 1)

            act.wait_ge(S["b_prep"], 1)
            act_(B["wqk"], bank[4][:, 0:KD * C], ACT.Copy)
            act_(bk_proj, bank[4][:, 2 * C + 2:2 * C + 2 + KD], ACT.Copy)
            act_(bq_bk, bank[4][:, 2 * C + 4:2 * C + 5], ACT.Copy)
            act_(q_bias, bank[4][:, 2 * C:2 * C + 1], ACT.Copy).then_inc(S["b_prep_copied"], 1)
            normalise(0)
            copy_xn_t(0)
            act.wait_ge(S["b_prep_copied"], 1)
            copy_q(0)
            normalise(1)
            exp_scores(0)
            copy_xn_t(1)
            copy_q(1)
            normalise(2)

            def step_b(i, has_prev=True, has_next=True, has_xn=True, has_stats=True):
                copy_prT(i)
                if has_xn:
                    copy_xn_t(i + 2)
                copy_gT(i)
                if has_next:
                    exp_scores(i + 1)
                if has_prev:
                    copy_xl_t(i - 1)
                    xhat(i - 1)
                if has_stats:
                    normalise(i + 3)
                if has_xn:
                    copy_q(i + 2)

            step_b(0, has_prev=False)
            with act.Fori(1, G - 3) as i:
                step_b(i)
            step_b(G - 3, has_stats=False)
            step_b(G - 2, has_xn=False, has_stats=False)
            step_b(G - 1, has_next=False, has_xn=False, has_stats=False)
            copy_xl_t(G - 1)
            xhat(G - 1)

            act.wait_ge(S["c_step"], 1)
            act_(Rm["ealpha"], Rm["max"], ACT.Exp, scale=-1.0).then_inc(S["c_ealpha"], 1)

            def copy_w1(s, par):
                e = act.value_load(expert_i[0:1, bass.ds(s, 1)], min_val=0, max_val=E - 1)
                if not isinstance(s, int) or s > 1:
                    act.wait_ge(S["d_h_done"], 2 * (s - 2) + 2)
                act_(w1_now[par], w1_sb[:, bass.ds(e * (KD * F), KD * F)], ACT.Copy).then_inc(S["d_w1_copied"], 1)

            def relu_lo(s, par):
                e = act.value_load(expert_i[0:1, bass.ds(s, 1)], min_val=0, max_val=E - 1)
                act.wait_ge(S["d_h_done"], 2 * s + 1)
                for f in range(4):
                    act_(hT_d[par][:, f, :], bank[2 + 2 * par][:, f * P:(f + 1) * P], ACT.Relu,
                         bias=L["b1"][:, bass.ds(e * KF + f, 1)]).then_inc(S["d_hT_act"], 1)

            act.wait_ge(S["ld_w1"], 16 * E)
            act.wait_ge(S["c_experts"], 1)
            copy_w1(0, 0)
            copy_w1(1, 1)
            relu_lo(0, 0)
            for s in range(PEEL):
                copy_w1(s + 2, s % 2)
                relu_lo(s + 1, (s + 1) % 2)
            with act.Fori(0, (LOOP - PEEL) // 2) as it:
                for k in range(2):
                    copy_w1(2 * it + k + PEEL + 2, k)
                    relu_lo(2 * it + k + PEEL + 1, (k + 1) % 2)
            for s in range(LOOP, SLOTS - 1):
                if s + 2 < SLOTS:
                    copy_w1(s + 2, s % 2)
                relu_lo(s + 1, (s + 1) % 2)

        @block.vector
        def _(dve):
            v = nc.vector
            stt = nc.vector.scalar_tensor_tensor

            def ln_out(g):
                dve.wait_ge(lns[0]["rstd"], g + 1)
                ln_apply(dve, 0, g, ln_tmp[0][3], lambda j: x_tile(g, j), lambda j: xnA[:, j, :], lns[0]["out"])

            def xnT_rest(g):
                for k in range(KD):
                    dve.wait_ge(S["a_xnT_hi"], KD * g + k + 1)
                    v.tensor_tensor(xnT_lo[:, k, :], bank[k][:, :], xnT_hi[:, k, :], ALU.subtract) \
                        .then_inc(S["a_xnT_lo"], 1)

            def b_rest(g):
                dve.wait_ge(S["a_b_hi"], 2 * g + 1)
                v.tensor_tensor(b_stack[32:32 + NS, :], bank[6][0:NS, :], b_stack[0:NS, :], ALU.subtract) \
                    .then_inc(S["a_b_lo"], 1)

            def conv(g, tap):
                for c in range(KI):
                    if tap == 1:
                        dve.wait_ge(S["a_first_tap"], KI * g + c + 1)
                    else:
                        dve.wait_ge(S["a_taps"], 3 * KI * g + KI * (tap - 2) + c + 1)
                    late = split(xc[:, c, :], GB)[:, :, tap:T]
                    stt(late, split(bank[2 + c][:, :], GB)[:, :, 0:T - tap], conv_w_sb[:, c, 3 - tap:4 - tap], late,
                        ALU.mult, ALU.add).then_inc(S["a_taps"], 1)

            def relu_sums(g):
                dve.wait_ge(S["a_dt_done"], (GB + 1) * g + GB + 1)
                dve.wait_ge(S["a_abs"], GB * g + GB)
                v.tensor_tensor(twice_relu, abs_sum, bank[6][:, 0:2 * GB:2], ALU.add).then_inc(S["a_twice_relu"], 1)

            def alphas(g):
                dve.wait_ge(S["a_twice_relu"], g + 1)
                dve.wait_ge(S["a_ln"], GB * g + GB)
                stt(sp_sum, twice_relu, 0.5, ln_sum, ALU.mult, ALU.add).then_inc(S["a_sp_sum"], 1)
                dve.wait_ge(S["a_exp_a"], g + 1)
                v.tensor_scalar(exp_a1, exp_a, 1.0, None, ALU.add).then_inc(S["a_exp_a1"], 1)
                dve.wait_ge(S["a_exp_a1"], g + 1)
                v.reciprocal(alpha, exp_a1).then_inc(S["a_alpha"], 1)

            def scan_chunk(g, c):
                dve.wait_ge(S["a_u"], KI * g + c + 1)
                v.tensor_tensor_scan(uu[:, c, :], alpha_all, uu[:, c, :], 0.0, ALU.mult, ALU.add).then_inc(S["a_scan"], 1)

            def y_chunk(g, par, c):
                dve.wait_ge(S["a_scan"], KI * g + c + 1)
                stt(yv[:, c, :], uu[:, c, :], neg_d[:, c:c + 1], xs[par][:, c, :], ALU.mult, ALU.add) \
                    .then_inc(S["a_y"], 1)

            def recurrence(g, par):
                dve.wait_ge(S["a_alpha_copied"], g + 1)
                v.memset(split(alpha_all, GB)[:, :, 0:1], 0.0).then_inc(S["a_alpha_zeroed"], 1)
                for c in range(KI):
                    stt(uu[:, c, :], bank[7][:, :], 1.0, xs[par][:, c, :], ALU.subtract, ALU.mult).then_inc(S["a_u"], 1)
                dve.wait_ge(S["a_alpha_zeroed"], g + 1)
                scan_chunk(g, 0)
                scan_chunk(g, 1)
                y_chunk(g, par, 0)
                scan_chunk(g, 2)
                y_chunk(g, par, 1)
                scan_chunk(g, 3)

            def resid(g):
                for half in range(2):
                    dve.wait_ge(S["a_out_done"], GB * g + 2 * half + 2)
                    dst = x_flat[:, bass.ds(g * (GB * D) + half * 2 * D, 2 * D)]
                    v.tensor_tensor(dst, bank[half][:, :], dst, ALU.add).then_inc(S["a_resid"], 1)

            def scale_and_bias(n):
                dve.wait_ge(lns[1]["rstd"], n + 1)
                stt(att_nbias, ln_tmp[1][1][:, :, 0], -1.0, ln_tmp[1][3], ALU.mult, ALU.mult).then_inc(S["b_nbias"], 1)

            dve.wait_ge(S["ld_x0"], 16)
            ln_stats(dve, 0, 0)
            ln_out(0)
            dve.wait_ge(S["inw_hi_set"], 1)
            v.tensor_tensor(inw_lo, inw_raw, inw_hi, ALU.subtract).then_inc(S["inw_lo_set"], 1)
            xnT_rest(0)
            dve.wait_ge(S["ld_x1"], 16)
            ln_stats(dve, 0, 1)
            dve.wait_ge(S["ld_lane"], 16)
            v.tensor_scalar(neg_d, d_sb, -1.0, None, ALU.mult).then_inc(S["neg_d_set"], 1)
            conv(0, 1)
            conv(0, 2)
            conv(0, 3)
            ln_out(1)
            dve.wait_ge(S["ld_dt"], 16 * 6)
            v.tensor_reduce(dtw_raw[:, DI:DI + 1], dtw_raw[:, 0:DI], X, ALU.add).then_inc(S["dt_rowsum"], 1)
            dve.wait_ge(S["dt_rowsum"], 1)
            v.tensor_copy(dtw_raw[:, DI + 1:DI + 2], dtw_raw[:, DI:DI + 1]).then_inc(S["dt_rowsum"], 1)
            dve.wait_ge(S["dt_rowsum"], 2)
            v.tensor_copy(dtw_round, dtw_raw).then_inc(S["dt_rounded"], 1)
            dve.wait_ge(S["dt_rounded"], 1)
            v.tensor_copy(dtw_stack[0:64, :], dtw_raw[0:64, :])
            v.tensor_tensor(dtw_stack[64:P, :], dtw_raw[64:P, :], dtw_round[64:P, :], ALU.subtract) \
                .then_inc(S["dt_split"], 1)
            dve.wait_ge(S["ld_x"], 16)
            dve.wait_ge(S["ident_set"], 2)
            dve.wait_ge(S["neg_d_set"], 1)

            def step_a(g, par, has_prev=True, has_next=True, stats=0):
                b_rest(g)
                if has_prev:
                    y_chunk(g - 1, 1 - par, 2)
                    y_chunk(g - 1, 1 - par, 3)
                if has_next:
                    xnT_rest(g + 1)
                if stats is not None:
                    ln_stats(dve, stats, g + 2 if stats == 0 else 0)
                if stats == 0:
                    ln_out(g + 2)
                relu_sums(g)
                if has_next:
                    conv(g + 1, 1)
                    conv(g + 1, 2)
                alphas(g)
                if stats == 1:
                    scale_and_bias(0)
                if has_prev:
                    resid(g - 1)
                if has_next:
                    conv(g + 1, 3)
                recurrence(g, par)

            step_a(0, 0, has_prev=False)
            with dve.Fori(0, (G - 4) // 2) as it:
                for k in range(2):
                    step_a(2 * it + k + 1, (k + 1) % 2)
            step_a(G - 3, 1)
            step_a(G - 2, 0, stats=None)
            dve.wait_ge(S["a_resid"], 2)
            step_a(G - 1, 1, has_next=False, stats=1)
            y_chunk(G - 1, 1, 2)
            y_chunk(G - 1, 1, 3)

            def sums_rcp(i):
                dve.wait_ge(S["b_probs"], GB * i + GB)
                v.reciprocal(att_rcp, att_sum).then_inc(S["b_rcp"], 1)

            def score_max(n):
                dve.wait_ge(S["b_stage_copied"], n + 1)
                dve.wait_ge(S["b_scores"], n + 1)
                v.tensor_reduce(att_max, split(bank[5][:, :], GB), X, ALU.max).then_inc(S["b_max"], 1)
                dve.wait_ge(S["b_max"], n + 1)
                v.tensor_tensor(att_top, att_max, shift, ALU.add).then_inc(S["b_top"], 1)
                dve.wait_ge(S["b_top"], n + 1)
                v.tensor_tensor(att_neg, shift, att_top, ALU.subtract).then_inc(S["b_neg"], 1)

            def add_attn(i):
                dve.wait_ge(S["b_rcp"], i + 1)
                dve.wait_ge(S["b_xbv"], GB * i + GB)
                for j in range(GB):
                    dve.wait_ge(S["b_v_done"], GB * i + 2 * (j // 2) + 2)
                    stt(x_tile(i, j), bank[2 + j // 2][:, (j % 2) * D:(j % 2) * D + D], att_rcp[:, j:j + 1],
                        x_tile(i, j), ALU.mult, ALU.add).then_inc(S["b_x2"], 1)

            def copy_stage(n, with_shift=True, with_aff=True):
                dve.wait_ge(S["b_stage_done"], n + 1)
                if with_shift:
                    if not isinstance(n, int) or n > 0:
                        dve.wait_ge(S["b_neg"], n)
                    ins = v.tensor_scalar(shift, bank[7][:, GB * E:GB * E + GB], bq_bk, None, ALU.add)
                if with_aff:
                    ins = v.tensor_copy(affs[:, bass.ds((n - 3) * GB, GB), :], split(bank[7][:, 0:GB * E], GB))
                ins.then_inc(S["b_stage_copied"], 1)

            def normalised_twice(i):
                rstd = ln_tmp[2][3]
                if not isinstance(i, int) or i > 0:
                    dve.wait_ge(S["b_xl_transposed"], KD * i)
                    dve.wait_ge(S["b_base"], GB * i)
                dve.wait_ge(lns[2]["rstd"], i + 1)
                ln_apply(dve, 2, i, rstd[:, 0:GB], lambda j: x_tile(i, j), lambda j: xlB[:, j, :], lns[2]["out"])
                stt(xhat_nbias, ln_tmp[2][1][:, :, 0], -1.0, rstd[:, GB:2 * GB], ALU.mult, ALU.mult) \
                    .then_inc(S["b_xhat_nbias"], 1)

            dve.wait_ge(S["a_resid"], 2 * 2)
            ln_stats(dve, 1, 1)
            scale_and_bias(1)
            dve.wait_ge(S["a_resid"], 2 * 3)
            ln_stats(dve, 1, 2)
            resid(G - 1)
            dve.wait_ge(S["a_resid"], 2 * G)
            copy_stage(0, with_aff=False)
            score_max(0)
            copy_stage(1, with_aff=False)
            scale_and_bias(2)

            def step_b(i, has_prev=True, has_next=True, has_stage=True, has_xn=True, has_stats=True):
                sums_rcp(i)
                if has_next:
                    score_max(i + 1)
                if has_stats:
                    ln_stats(dve, 1, i + 3)
                add_attn(i)
                if has_stats:
                    scale_and_bias(i + 3)
                dve.wait_ge(S["b_x2"], GB * i + GB)
                ln_stats(dve, 2, i)
                if has_stage:
                    copy_stage(i + 2, with_shift=has_xn, with_aff=has_prev)
                normalised_twice(i)

            step_b(0, has_prev=False)
            with dve.Fori(1, G - 3) as i:
                step_b(i)
            step_b(G - 3, has_stats=False)
            step_b(G - 2, has_xn=False, has_stats=False)
            step_b(G - 1, has_next=False, has_xn=False, has_stats=False)
            copy_stage(G + 2, with_shift=False)

            steps = [0]

            def step(ins):
                ins.then_inc(S["c_step"], 1)
                steps[0] += 1
                dve.wait_ge(S["c_step"], steps[0])

            hot, tot = split(Rm["hot"], TILES), split(bank[1][:, 0:TILES * E], TILES)

            def over_e(ap):
                return ap.rearrange("p (t o) -> p t o", o=1).broadcast_to([P, TILES, E])

            def over_t(ap, n=TILES):
                return ap.rearrange("p (o e) -> p o e", o=1).broadcast_to([P, n, ap.shape[1]])

            dve.wait_ge(S["b_stage_copied"], G + 3)
            dve.wait_ge(S["b_base"], GB * G)
            dve.wait_ge(S["consts_set"], 5)
            step(v.tensor_reduce(Rm["max"], affs, X, ALU.max))
            step(v.tensor_tensor(split(Rm["eq"], TILES), affs, over_e(Rm["max"]), ALU.is_ge))
            step(v.tensor_tensor(split(Rm["cand"], TILES), split(Rm["eq"], TILES), over_t(Im["e8"]), ALU.mult))
            step(v.tensor_reduce(Rm["first"], split(Rm["cand"], TILES), X, ALU.min))
            step(v.tensor_tensor(hot, over_t(Im["e8"]), over_e(Rm["first"]), ALU.is_equal))
            dve.wait_ge(S["c_ealpha"], 1)
            step(v.tensor_scalar(Rm["ealpha"], Rm["ealpha"], 1.0, None, ALU.add))
            step(v.reciprocal(Rm["max"], Rm["ealpha"]))
            dve.wait_ge(S["c_prefix"], 1)
            cum = split(Rm["eq"], TILES)
            for e in range(E):
                ins = v.tensor_tensor_scan(cum[:, :, e], ones[:, 0:TILES], tot[:, :, e], 0.0, ALU.mult, ALU.add)
            step(ins)
            count = cum[:, TILES - 1, :]
            per_e = Rm["cand"].rearrange("p (e k) -> p e k", e=E)
            step(v.tensor_tensor(per_e, count.rearrange("p (e o) -> p e o", o=1).broadcast_to([P, E, TILES]),
                                 over_t(Im["k128"], E), ALU.is_gt))
            n_slots, ends, starts = (routing_tmp[:, k * E:(k + 1) * E] for k in range(3))
            step(v.tensor_reduce(n_slots, per_e, X, ALU.add))
            step(v.tensor_tensor_scan(ends, ones[:, 0:E], n_slots, 0.0, ALU.mult, ALU.add))
            step(v.tensor_tensor(starts, ends, n_slots, ALU.subtract))
            step(v.tensor_tensor(cum, cum, tot, ALU.subtract))
            step(v.tensor_tensor(Rm["eq"], Rm["eq"], bank[0][:, 0:TILES * E], ALU.add))
            step(stt(cum, over_t(starts), float(P), cum, ALU.mult, ALU.add))
            step(v.tensor_tensor(cum, cum, hot, ALU.mult))
            step(v.tensor_reduce(Rm["pos"], cum, X, ALU.add))
            step(v.tensor_copy(pos_i, Rm["pos"]))
            step(v.tensor_scalar(hi_i, pos_i, 7, None, ALU.logical_shift_right))
            step(v.tensor_copy(Rm["hi"], hi_i))
            step(stt(Rm["lo"], Rm["hi"], -float(P), Rm["pos"], ALU.mult, ALU.add))
            lo_hot, hi_hot = split(Cm["lo_hot"], TILES), split(Cm["hi_hot"], TILES)
            hi_val = split(Cm["hi_val"], TILES)

            def wide(ap, n):
                m = ap.shape[1]
                return ap.rearrange("p (t o) -> p t o", o=1).broadcast_to([P, m, n])

            dve.wait_ge(S["b_xhat"], GB * G)
            for g in range(G):
                tiles = slice(g * GB, (g + 1) * GB)
                v.tensor_tensor(hi_hot[:, tiles], wide(Rm["hi"][:, tiles], SP_), over_t(Im["slot"], GB), ALU.is_equal) \
                    .then_inc(S["c_hi_hot"], 1)
                v.tensor_tensor(lo_hot[:, tiles], wide(Rm["lo"][:, tiles], P), over_t(Im["lane"], GB), ALU.is_equal)
                dve.wait_ge(S["c_hi_hot"], g + 1)
                v.tensor_tensor(hi_val[:, tiles, 0:SP_], hi_hot[:, tiles], wide(Im["tok"][:, tiles], SP_), ALU.mult)
                v.tensor_tensor(hi_val[:, tiles, SP_:2 * SP_], hi_hot[:, tiles], wide(Rm["max"][:, tiles], SP_),
                                ALU.mult).then_inc(S["c_slots"], 1)
            ge = Rm["hot"].rearrange("p (s e) -> p s e", e=E)
            slot_e = Rm["tot"]
            for half, n in ((0, TILES), (TILES, SP_ - TILES)):
                step(v.tensor_tensor(ge[:, 0:n], Im["slot"][:, half:half + n].rearrange("p (s o) -> p s o", o=1)
                                     .broadcast_to([P, n, E]), over_t(ends, n), ALU.is_ge))
                step(v.tensor_reduce(slot_e[:, half:half + n], ge[:, 0:n], X, ALU.add))
            v.tensor_scalar(expert_i, slot_e[:, 0:SP_], float(E - 1), None, ALU.min).then_inc(S["c_experts"], 1)
            dve.wait_ge(S["c_prefix"], 2)
            vmap = Rm["cand"][:, 0:SP_]
            v.tensor_scalar(gather_i, bank[2][:, 0:SP_], -1.0, 0.0, ALU.add, ALU.max).then_inc(S["c_map"], 1)
            none = Rm["cand"][:, SP_:2 * SP_]
            step(v.tensor_copy(vmap, bank[2][:, 0:SP_]))
            step(v.tensor_copy(slot_alpha, bank[2][:, SP_:2 * SP_]))
            step(v.tensor_scalar(none, vmap, 0.0, float(2 * NB * T), ALU.is_equal, ALU.mult))
            step(stt(none, vmap, -1.0, none, ALU.add, ALU.add))
            v.tensor_copy(scatter_i, none).then_inc(S["c_map"], 1)
            dve.wait_ge(S["c_map"], 2)
            dve.wait_ge(S["c_experts"], 1)

            def load_e(s):
                return dve.value_load(expert_i[0:1, bass.ds(s, 1)], min_val=0, max_val=E - 1)

            lng_f, lnb_f, b1_f = L["ln_g"], L["ln_b"], L["b1"]

            def affine(s):
                e = load_e(s)
                dve.wait_ge(S["d_xT_done"], s + 1)
                if not isinstance(s, int) or s > 0:
                    dve.wait_ge(S["d_h_done"], 2 * s)
                for k in range(KD):
                    v.tensor_scalar(xT_d[:, k, :], bank[0][:, k * P:(k + 1) * P], lng_f[:, bass.ds(e + k * E, 1)],
                                    lnb_f[:, bass.ds(e + k * E, 1)], ALU.mult, ALU.add).then_inc(S["d_xT_ready"], 1)

            def relu_hi(s, par):
                e = load_e(s)
                dve.wait_ge(S["d_h_done"], 2 * s + 2)
                for f in range(4, 8):
                    v.tensor_scalar(hT_d[par][:, f, :], bank[3 + 2 * par][:, (f - 4) * P:(f - 3) * P],
                                    b1_f[:, bass.ds(e * KF + f, 1)], 0.0, ALU.add, ALU.max).then_inc(S["d_hT_dve"], 1)

            def finish(s, place, k, turn):
                e = load_e(s)
                dve.wait_ge(S["d_y_done"], s + 1)
                if not isinstance(s, int) or s > 1:
                    dve.wait_ge(scat[k], 16 * turn)
                v.tensor_tensor(o_d[:, k, :], bank[6][:, 0:D], Dm["b2"][:, bass.ds(e * D, D)], ALU.add).then_inc(S["d_yb"], 1)
                dve.wait_ge(S["d_yb"], s + 1)
                stt(o_d[:, k, :], o_d[:, k, :], slot_alpha[:, bass.ds(s, 1)], slot_rows[:, place, D:2 * D],
                    ALU.mult, ALU.add).then_inc(S["d_o_ready"], 1)

            def slot(s, k, turn, ahead=2):
                if ahead > 0:
                    relu_hi(s + 1, (k + 1) % 2)
                if ahead > 1:
                    affine(s + 2)
                finish(s, k, k % 2, turn)

            dve.wait_ge(S["ld_b2"], 16)
            affine(0)
            affine(1)
            relu_hi(0, 0)
            for s in range(PEEL):
                slot(s, s, s // 2)
            with dve.Fori(0, (LOOP - PEEL) // RING) as it:
                for k in range(RING):
                    slot(RING * it + k + PEEL, k, 2 * it + 2 + k // 2)
            for s in range(LOOP, SLOTS):
                slot(s, s % RING, s // 2, ahead=min(2, SLOTS - 1 - s))


def kernel(**inputs):
    import numpy as np
    import concourse.bacc as bacc
    from concourse.bass_utils import run_bass_kernel_spmd

    def t(name, axes=None):
        a = np.asarray(inputs[name])
        return np.ascontiguousarray(a if axes is None else np.transpose(a, axes))

    def lanes(a):
        return a.reshape(a.shape[0] // P, P, -1).transpose(1, 0, 2).reshape(P, -1)

    b1 = t("L0_ffn_b1")
    lane_w = np.concatenate([
        lanes(t("L0_attn_conv_w")), lanes(t("L0_attn_conv_b")), lanes(t("L0_attn_D_param")),
        lanes(t("L0_attn_x_proj_w", (1, 0))[:, :t("L0_attn_dt_proj_w").shape[1]]),
        lanes(t("L0_xattn_bq")), lanes(t("L0_xattn_bk")), lanes(t("L0_ffn_centroids", (1, 0))),
        lanes(t("L0_ffn_ln_g", (1, 0))), lanes(t("L0_ffn_ln_b", (1, 0))),
        b1.reshape(b1.shape[0], -1, P).transpose(2, 0, 1).reshape(P, -1)], axis=1)
    arrays = [
        ("x", t("x")), ("ctx", t("ctx_512")), ("ctx_t", t("ctx_512", (0, 2, 1))),
        ("in_w_t", t("L0_attn_in_proj_w", (1, 0))), ("dt_w_t", t("L0_attn_dt_proj_w", (1, 0))),
        ("dt_b", t("L0_attn_dt_proj_b")), ("out_w_t", t("L0_attn_out_proj_w", (1, 0))),
        ("wq_t", t("L0_xattn_Wq", (1, 0))), ("wk_t", t("L0_xattn_Wk", (1, 0))),
        ("wv", t("L0_xattn_Wv")), ("bv", t("L0_xattn_bv")), ("lane_w", lane_w),
        ("w1_t", t("L0_ffn_w1", (0, 2, 1))), ("w2_t", t("L0_ffn_w2", (0, 2, 1))), ("b2", t("L0_ffn_b2")),
    ]
    nc = bacc.Bacc("TRN2", target_bir_lowering=False, num_devices=1)
    feeds, args = {}, []
    for name, a in arrays:
        feeds[f"in_{name}"] = a
        args.append(nc.dram_tensor(f"in_{name}", a.shape, mybir.dt.from_np(a.dtype), kind="ExternalInput").ap())
    shape = inputs["x"].shape
    args.append(nc.dram_tensor("layer_out", shape, F32, kind="ExternalOutput").ap())
    decoder_program(nc, *args)
    got = run_bass_kernel_spmd(nc, [feeds], core_ids=[0])
    return got.results[0]["layer_out"]
```

```python
from contextlib import ExitStack

import concourse.bass as bass
from concourse import mybir

F32 = mybir.dt.float32
F32R = mybir.dt.float32r
I32 = mybir.dt.int32
ALU = mybir.AluOpType
ACT = mybir.ActivationFunctionType
X = mybir.AxisListType.X

P = 128
EPS = 1e-5


def decoder_program(nc, x, ctx, ctx_t, in_w_t, dt_w_t, dt_b, out_w_t, wq_t, wk_t, wv, bv, lane_w,
                    w1_t, w2_t, b2, out):
    NB, T, D = x.shape
    C = ctx.shape[2]
    DI = out_w_t.shape[0]
    NS = dt_w_t.shape[0]
    E, _, F = w1_t.shape
    assert T == P and C == P and NS <= 31
    KD, KI, KF = D // P, DI // P, F // P
    GB = 4
    G = NB // GB
    GT = GB * T
    TILES = NB
    SLOTS = TILES + E - 1
    RING = 4
    SP_ = 40
    assert SLOTS <= SP_ and G == 8 and E == G and KI == GB and SLOTS % RING == 3

    rows_dram = nc.dram_tensor("token_rows", (NB * T, 2 * D), F32, kind="Internal").ap()

    with ExitStack() as stack:
        def sb(name, cols, dt=F32):
            return stack.enter_context(nc.sbuf_tensor(name, [P, cols], dt))

        def sem(name):
            return stack.enter_context(nc.semaphore(name))

        def split(ap, n):
            return ap.rearrange("p (n w) -> p n w", n=n)

        bank = [stack.enter_context(nc.psum_tensor(f"bank{i}", [P, 512], F32)) for i in range(8)]

        x_flat = sb("x_flat", NB * D)
        x_res = split(x_flat[:, :], NB)

        ident = sb("ident", P)
        ones = sb("ones", P)
        before = sb("before", P)
        small = sb("small", 256)
        cols = [0]

        def piece(n):
            a = cols[0]
            cols[0] += n
            return small[:, a:a + n]

        neg_d = piece(KI)
        q_bias = piece(1)
        bk_proj = piece(KD)
        bq_bk = piece(1)
        shift = piece(GB)
        att_top = piece(GB)
        mhalf = piece(2 * GB)
        abs_sum, twice_relu, ln_sum, sp_sum, exp_a, exp_a1, alpha = (piece(GB) for _ in range(7))
        att_max, att_neg, att_sum, att_rcp = (piece(GB) for _ in range(4))
        att_nbias = piece(GB)
        xhat_nbias = piece(GB)
        ln_tmp = [(split(piece(6 * GB), GB), split(piece(2 * GB), GB), piece(n), piece(n)) for n in (GB, GB, 2 * GB)]
        assert cols[0] <= 256
        affs = split(sb("affs", TILES * E)[:, :], TILES)

        def take(ap, spots):
            out_, at = {}, 0
            for name, n in spots:
                out_[name] = ap[:, at:at + n]
                at += n
            assert at <= ap.shape[1], (at, ap.shape)
            return out_

        lane_parts = [("conv_w", 4 * KI), ("conv_b", KI), ("d", KI), ("xp", KI * NS), ("bq", KD), ("bk", KD),
                      ("cent", KD * E), ("ln_g", KD * E), ("ln_b", KD * E), ("b1", E * KF)]
        lane_sb = sb("lane_sb", sum(n for _, n in lane_parts))
        L = take(lane_sb[:, :], lane_parts)
        conv_w_sb, conv_b_sb, d_sb, xpw_sb = split(L["conv_w"], KI), L["conv_b"], L["d"], split(L["xp"], KI)
        bq_sb, bk_sb, cent_sb = L["bq"], L["bk"], split(L["cent"], KD)

        ARENA = 10240
        WEIGHTS_AT = 98272

        class Placed:
            def __init__(self, at):
                self.at = at

            def __call__(self, name, n, dt=F32):
                t = nc.alloc_sbuf_tensor_at(name, [P, n], dt, offset=self.at)
                self.at += 4 * ((n + 7) // 8 * 8)
                return t[:, :]

        put = Placed(WEIGHTS_AT - 4 * ARENA)
        arena = put("arena", ARENA)
        w1_sb = put("w1_sb", E * KD * F)
        w2_sb = put("w2_sb", E * KF * D)
        weights_end = put.at
        put = Placed(WEIGHTS_AT)
        inw_hi, inw_lo = split(put("inw_hi", KD * 2 * DI, F32R), KD), split(put("inw_lo", KD * 2 * DI, F32R), KD)
        xnT_hi, xnT_lo = split(put("xnT_hi", KD * GT, F32R), KD), split(put("xnT_lo", KD * GT, F32R), KD)
        b_stack = put("b_stack", GT, F32R)
        dtw_stack, dtw_round = put("dtw_stack", DI + 2, F32R), put("dtw_round", DI + 2, F32R)
        dtw_raw = put("dtw_raw", DI + 2)
        xnA = split(put("xnA", GB * D), GB)
        xc = split(put("xc", KI * GT), KI)
        xs = [split(put(f"xs{k}", KI * GT), KI) for k in range(2)]
        gz = [split(put(f"gz{k}", KI * GT), KI) for k in range(2)]
        uu_flat = put("uu", KI * GT)
        uu, inw_raw = split(uu_flat, KI), split(uu_flat, KD)
        yv = split(put("yv", KI * GT), KI)
        sp = split(put("sp", GB * DI), GB)
        alpha_all = put("alpha_all", GT)
        outw_sb = split(put("outw", KI * D), KI)
        assert put.at <= weights_end

        B = take(arena[:, :], [("row", GB * 2 * D), ("xlT", KD * GT), ("pr", GT), ("xn", GB * D), ("xnT", KD * GT),
                               ("q", GT), ("prT", GT), ("gT", GT), ("cT", GT), ("c", GT), ("xl", GB * D),
                               ("wk", KD * C), ("wqk", KD * C), ("wv", D), ("bv", D)])
        xnB, xlB = split(B["xn"], GB), split(B["xl"], GB)
        xnTB, xlTB = split(B["xnT"], KD), split(B["xlT"], KD)
        row = B["row"].rearrange("p (j h d) -> p j h d", j=GB, h=2)
        pr = split(B["pr"], GB)
        cT_sb, c_sb = B["cT"], split(B["c"], GB)
        wq_sb, wk_sb, wqk = split(B["gT"], KD), split(B["wk"], KD), split(B["wqk"], KD)
        put = Placed(WEIGHTS_AT - 4 * ARENA)
        w2_hi, w2_lo = (split(put(name, KF * D, F32R), KF) for name in ("w2_hi", "w2_lo"))
        hT_hi = [split(put(f"hT_hi{k}", F, F32R), KF) for k in range(2)]
        hT_lo = [split(put(f"hT_lo{k}", F, F32R), KF) for k in range(2)]
        xT_d, hT_d, o_d = split(put("slot_xT", KD * P), KD), split(put("slot_hT", F), KF), split(put("slot_o", 2 * D), 2)
        assert put.at <= WEIGHTS_AT
        Dm = take(x_flat[:, :], [("rows", RING * 2 * D), ("w1_0", KD * F), ("w1_1", KD * F), ("b2", E * D)])
        b2_sb = split(Dm["b2"], E)
        slot_rows = split(Dm["rows"], RING)
        w1_now = [Dm["w1_0"], Dm["w1_1"]]
        Cm = take(x_flat[:, :], [("lo_hot", TILES * P), ("hi_hot", TILES * SP_), ("hi_val", TILES * 2 * SP_)])
        Rm = take(arena[:, 8960:10240], [("max", TILES), ("eq", TILES * E), ("cand", TILES * E), ("first", TILES),
                             ("hot", TILES * E), ("slot_e", 2 * TILES), ("pos", TILES), ("hi", TILES),
                             ("lo", TILES), ("ealpha", TILES)])
        slot_alpha = sb("slot_alpha", SP_)[:, :]
        routing_tmp = sb("routing_tmp", 3 * E)[:, :]
        iotas = sb("iotas", E + 2 * TILES + P + SP_)
        Im = take(iotas[:, :], [("e8", E), ("k128", TILES), ("lane", P), ("slot", SP_), ("tok", TILES)])
        gather_cols, scatter_cols = sb("gather_cols", RING, I32), sb("scatter_cols", 2, I32)
        gather_col = [gather_cols[:, k:k + 1] for k in range(RING)]
        scatter_col = [scatter_cols[:, k:k + 1] for k in range(2)]
        idx = sb("idx", 2 * TILES + 3 * SP_, I32)
        pos_i, hi_i = (idx[:, k * TILES:(k + 1) * TILES] for k in range(2))
        gather_i, scatter_i, expert_i = (idx[:, 2 * TILES + k * SP_:2 * TILES + (k + 1) * SP_] for k in range(3))

        names = """ld_x0 ld_x1 ld_x ld_inw ld_lane ld_dt ld_outw ld_wb ld_ct ld_c ld_w1 ld_w2 ld_b2
            fills_set dt_zeroed ident_set consts_set neg_d_set dt_rowsum dt_rounded dt_split inw_hi_set inw_lo_set
            a_transposed a_xnT_hi a_xnT_lo a_x_done a_z_done a_first_tap a_taps a_xs a_gz
            a_xp_done a_b_hi a_b_lo a_dt_done a_abs a_exp a_ln a_twice_relu a_sp_sum a_exp_a a_exp_a1 a_alpha
            a_alpha_rows a_alpha_copied a_alpha_zeroed a_u a_scan a_y a_gated a_out_done a_resid
            b_prep b_prep_copied b_transposed b_xnT_ready b_q_done b_q_ready b_scores b_max b_top b_neg b_probs b_rcp
            b_prT_done b_prT_ready b_g_done b_gT_ready b_v_done b_xbv b_x2 b_nbias b_xhat_nbias b_xhat b_xl_transposed b_xlT_ready
            b_stage_done b_stage_copied b_base b_rows_out
            c_step c_ealpha c_prefix c_hi_hot c_hi_alpha c_slots c_experts c_map
            d_gather_col d_scatter_col d_xT_done d_xT_ready d_w1_copied d_h_done d_hT_act d_hT_dve d_hT_hi d_hT_lo d_w2_hi d_w2_lo d_y_half d_y_done d_yb
            d_o_ready d_scattered_0 d_scattered_1""".split()
        S = {n: sem(n) for n in names}
        lns = [{k: sem(f"ln{i}_{k}") for k in ("stats", "aggr", "eps", "rstd", "out")} for i in range(3)]
        gath = [sem(f"d_gathered_{i}") for i in range(RING)]
        scat = [S[f"d_scattered_{i}"] for i in range(2)]

        def ln_stats(dve, which, g):
            stats, mv, var, _ = ln_tmp[which]
            s = lns[which]
            dve.nop(nofuse=True)
            for j in range(GB):
                nc.vector.bn_stats(stats[:, j, :], x_flat[:, bass.ds(g * (GB * D) + j * D, D)]).then_inc(s["stats"], 1)
            for j in range(GB):
                dve.wait_ge(s["stats"], GB * g + j + 1)
                dve.nop(nofuse=True)
                nc.vector.bn_aggr(mv[:, j, :], stats[:, j, :]).then_inc(s["aggr"], 1)
            dve.wait_ge(s["aggr"], GB * g + GB)
            if which == 2:
                nc.vector.tensor_scalar(var[:, GB:2 * GB], mv[:, :, 1], 1 + EPS, EPS * EPS, ALU.mult, ALU.add)
            nc.vector.tensor_scalar(var[:, 0:GB], mv[:, :, 1], EPS, None, ALU.add).then_inc(s["eps"], 1)

        def ln_rstd(pool, which, g):
            _, _, var, rstd = ln_tmp[which]
            s = lns[which]
            pool.wait_ge(s["eps"], g + 1)
            nc.gpsimd.tensor_tensor(rstd, var, mhalf[:, 0:var.shape[1]], ALU.pow).then_inc(s["rstd"], 1)

        def ln_apply(dve, which, g, rstd, src, dst, done):
            mv = ln_tmp[which][1]
            for j in range(GB):
                nc.vector.tensor_scalar(dst(j), src(j), mv[:, j, 0:1], rstd[:, j:j + 1],
                                        ALU.subtract, ALU.mult).then_inc(done, 1)

        def x_tile(g, j):
            return x_flat[:, bass.ds(g * (GB * D) + j * D, D)]

        def taps_done(g, c, tap=3):
            return 3 * KI * g + 6 * (c // 2) + 2 * (tap - 1) + c % 2 + 1

        def z_bank(g, c):
            return bank[(0, 1, 7, 6)[c] if isinstance(g, int) and g == 0 else c]

        class Experts:
            def __init__(self, engine, first):
                self.engine, self.first, self.loaded = engine, first, {}

            def __call__(self, k):
                if k not in self.loaded:
                    self.loaded[k] = self.engine.value_load(expert_i[0:1, bass.ds(self.first + k, 1)],
                                                            min_val=0, max_val=E - 1)
                return self.loaded[k]

        PEEL = 4
        LOOP = SLOTS // RING * RING

        block = stack.enter_context(nc.Block())

        @block.sync
        def _(sp_):
            xv = x.rearrange("b t d -> t b d")
            sp_.dma_start(x_res[:, 0:GB, :], xv[:, 0:GB, :]).then_inc(S["ld_x0"], 16)
            sp_.dma_start(lane_sb[:, :], lane_w).then_inc(S["ld_lane"], 16)
            sp_.wait_ge(S["dt_zeroed"], 1)
            for at in (0, 32, 64):
                sp_.dma_start(dtw_raw[at:at + NS, 0:DI], dt_w_t).then_inc(S["ld_dt"], 16)
                sp_.dma_start(dtw_raw[at + NS:at + NS + 1, 0:DI], dt_b.rearrange("(o n) -> o n", o=1)) \
                    .then_inc(S["ld_dt"], 16)
            sp_.dma_start(x_res[:, GB:2 * GB, :], xv[:, GB:2 * GB, :]).then_inc(S["ld_x1"], 16)
            sp_.dma_start(outw_sb, out_w_t.rearrange("(c p) n -> p c n", p=P)).then_inc(S["ld_outw"], 16)
            sp_.dma_start(x_res[:, 2 * GB:NB, :], xv[:, 2 * GB:NB, :]).then_inc(S["ld_x"], 16)
            sp_.dma_start(wq_sb, wq_t.rearrange("(k p) n -> p k n", p=P)).then_inc(S["ld_wb"], 16)
            sp_.dma_start(wk_sb, wk_t.rearrange("(k p) n -> p k n", p=P)).then_inc(S["ld_wb"], 16)
            sp_.dma_start(B["wv"], wv).then_inc(S["ld_wb"], 16)
            sp_.dma_start(B["bv"], bv.rearrange("(o n) -> o n", o=1).broadcast_to([P, D])).then_inc(S["ld_wb"], 16)

            ctv = ctx_t.rearrange("b c t -> c b t")
            cv = ctx.rearrange("b t c -> t b c")
            sp_.dma_start(split(cT_sb, GB), ctv[:, 0:GB, :]).then_inc(S["ld_ct"], 16)
            sp_.dma_start(c_sb, cv[:, 0:GB, :]).then_inc(S["ld_c"], 16)

            def expert_weights(e):
                sp_.dma_start(split(w1_sb[:, bass.ds(e * (KD * F), KD * F)], KD),
                              w1_t[bass.ds(e, 1)].rearrange("o (k p) f -> p (o k) f", p=P)).then_inc(S["ld_w1"], 16)
                sp_.dma_start(split(w2_sb[:, bass.ds(e * (KF * D), KF * D)], KF),
                              w2_t[bass.ds(e, 1)].rearrange("o (k p) d -> p (o k) d", p=P)).then_inc(S["ld_w2"], 16)

            def next_ct(g):
                sp_.wait_ge(S["b_scores"], g + 1)
                sp_.dma_start(split(cT_sb, GB), ctv[:, bass.ds((g + 1) * GB, GB), :]).then_inc(S["ld_ct"], 16)

            def next_c(g):
                sp_.wait_ge(S["b_g_done"], g + 1)
                sp_.dma_start(c_sb, cv[:, bass.ds((g + 1) * GB, GB), :]).then_inc(S["ld_c"], 16)

            def rows_out(g):
                sp_.wait_ge(S["b_xhat"], GB * g + GB)
                sp_.wait_ge(S["b_base"], GB * g + GB)
                sp_.dma_start(rows_dram.rearrange("(b t) w -> t b w", t=T)[:, bass.ds(g * GB, GB), :],
                              B["row"].rearrange("p (j w) -> p j w", j=GB)).then_inc(S["b_rows_out"], 16)

            next_ct(0)
            sp_.wait_ge(S["a_resid"], 2 * G)
            next_ct(1)
            next_c(0)
            expert_weights(0)
            with sp_.Fori(1, G - 2) as g:
                next_ct(g + 1)
                next_c(g)
                rows_out(g - 1)
                expert_weights(g)
            next_c(G - 2)
            rows_out(G - 3)
            expert_weights(G - 2)
            rows_out(G - 2)
            expert_weights(G - 1)
            rows_out(G - 1)

            sp_.wait_ge(S["c_map"], 1)
            sp_.dma_start(b2_sb, b2.rearrange("(o e) d -> o e d", o=1).broadcast_to([P, E, D])).then_inc(S["ld_b2"], 16)

        @block.gpsimd
        def _(pool):
            nc.gpsimd.memset(dtw_raw, 0.0).then_inc(S["dt_zeroed"], 1)
            nc.gpsimd.memset(mhalf, -0.5).then_inc(S["fills_set"], 1)
            nc.gpsimd.memset(ones[:, :], 1.0).then_inc(S["fills_set"], 1)
            nc.gpsimd.memset(b_stack.bitcast(F32), 0.0).then_inc(S["fills_set"], 1)
            pool.wait_ge(S["fills_set"], 3)
            nc.gpsimd.affine_select(out=ident[:, :], in_=ones[:, :], compare_op=ALU.is_equal, fill=0.0, base=0,
                                    pattern=[[-1, P]], channel_multiplier=1).then_inc(S["ident_set"], 1)
            nc.gpsimd.affine_select(out=before[:, :], in_=ones[:, :], compare_op=ALU.is_gt, fill=0.0, base=0,
                                    pattern=[[1, P]], channel_multiplier=-1).then_inc(S["ident_set"], 1)
            nc.gpsimd.memset(b_stack[0:NS + 1, :].bitcast(F32), 1.0).then_inc(S["fills_set"], 1)
            pool.wait_ge(S["ident_set"], 2)
            pool.wait_ge(S["fills_set"], 4)
            nc.gpsimd.memset(b_stack[64:64 + NS + 1, :].bitcast(F32), 1.0).then_inc(S["fills_set"], 1)

            pool.wait_ge(S["fills_set"], 5)

            def gated(g, par):
                for c in range(KI):
                    pool.wait_ge(S["a_y"], KI * g + c + 1)
                    nc.gpsimd.tensor_tensor(yv[:, c, :], yv[:, c, :], gz[par][:, c, :], ALU.mult) \
                        .then_inc(S["a_gated"], 1)

            ln_rstd(pool, 0, 0)
            ln_rstd(pool, 0, 1)
            for name, base, step, per_lane in (("e8", -E, 1, 0), ("k128", 0, P, 0), ("lane", 0, 1, 0),
                                               ("slot", 0, 1, 0), ("tok", 1, P, 1)):
                nc.gpsimd.iota(Im[name], pattern=[[step, Im[name].shape[1]]], base=base, channel_multiplier=per_lane,
                               allow_small_or_imprecise_dtypes=True).then_inc(S["consts_set"], 1)
            ln_rstd(pool, 0, 2)
            gated(0, 0)
            with pool.Fori(0, (G - 4) // 2) as it:
                for k in range(2):
                    ln_rstd(pool, 0, 2 * it + k + 3)
                    gated(2 * it + k + 1, (k + 1) % 2)
            ln_rstd(pool, 0, G - 1)
            gated(G - 3, 1)
            gated(G - 2, 0)
            ln_rstd(pool, 1, 0)
            pool.wait_ge(lns[1]["out"], GB)
            ln_rstd(pool, 1, 1)
            gated(G - 1, 1)

            def add_bv(g):
                pool.wait_ge(lns[1]["out"], GB * g + GB)
                pool.nop(nofuse=True)
                for j in range(GB):
                    nc.gpsimd.tensor_tensor(x_tile(g, j), x_tile(g, j), B["bv"], ALU.add).then_inc(S["b_xbv"], 1)

            def base_rows(g):
                if not isinstance(g, int) or g > 0:
                    pool.wait_ge(S["b_rows_out"], 16 * g)
                for j in range(GB):
                    pool.wait_ge(lns[2]["out"], GB * g + j + 1)
                    pool.nop(nofuse=True)
                    nc.gpsimd.tensor_tensor(row[:, j, 1, :], x_tile(g, j), xlB[:, j, :], ALU.add) \
                        .then_inc(S["b_base"], 1)

            def rstd_b(g):
                pool.wait_ge(lns[1]["out"], GB * g)
                ln_rstd(pool, 1, g)

            pool.wait_ge(S["ld_wb"], 16 * 4)
            add_bv(0)
            rstd_b(2)

            def step_b(i, has_next, has_stats):
                if has_stats:
                    rstd_b(i + 3)
                if has_next:
                    add_bv(i + 1)
                if not isinstance(i, int) or i > 0:
                    pool.wait_ge(S["b_xhat"], GB * i)
                ln_rstd(pool, 2, i)
                base_rows(i)

            step_b(0, True, True)
            with pool.Fori(1, G - 3) as i:
                step_b(i, True, True)
            step_b(G - 3, True, False)
            step_b(G - 2, True, False)
            step_b(G - 1, False, False)

            for g in range(G):
                tiles = slice(g * GB, (g + 1) * GB)
                pool.wait_ge(S["c_hi_hot"], g + 1)
                nc.gpsimd.tensor_tensor(split(Cm["hi_val"], TILES)[:, tiles, SP_:2 * SP_],
                                        split(Cm["hi_hot"], TILES)[:, tiles],
                                        Rm["max"][:, tiles].rearrange("p (t o) -> p t o", o=1).broadcast_to([P, GB, SP_]),
                                        ALU.mult).then_inc(S["c_hi_alpha"], 1)

            def gather(s, k, after=None):
                if after is not None:
                    pool.wait_ge(S["d_xT_done"], after + 1)
                    pool.nop(nofuse=True)
                nc.gpsimd.tensor_copy(gather_col[k], gather_i[:, bass.ds(s, 1)]).then_inc(S["d_gather_col"], 1)
                if after is not None:
                    pool.wait_ge(S["d_o_ready"], after + 1)
                pool.wait_ge(S["d_gather_col"], s + 1)
                pool.nop(nofuse=True)
                nc.gpsimd.indirect_dma_start(
                    out=slot_rows[:, k, :], out_offset=None, in_=rows_dram,
                    in_offset=bass.IndirectOffsetOnAxis(ap=gather_col[k], axis=0)).then_inc(gath[k], 16)

            def scatter(s, k):
                pool.wait_ge(S["d_o_ready"], s + 1)
                pool.nop(nofuse=True)
                nc.gpsimd.tensor_copy(scatter_col[k], scatter_i[:, bass.ds(s, 1)]).then_inc(S["d_scatter_col"], 1)
                pool.wait_ge(S["d_scatter_col"], s + 1)
                pool.nop(nofuse=True)
                nc.gpsimd.indirect_dma_start(
                    out=out.rearrange("b t d -> (b t) d"), in_=o_d[:, k, :], in_offset=None,
                    out_offset=bass.IndirectOffsetOnAxis(ap=scatter_col[k], axis=0),
                    bounds_check=NB * T - 1, oob_is_err=False).then_inc(scat[k], 16)

            pool.wait_ge(S["b_rows_out"], 16 * G)
            pool.wait_ge(S["b_stage_copied"], G + 3)
            pool.wait_ge(S["c_map"], 1)
            for s in range(RING):
                gather(s, s)
            pool.wait_ge(S["c_map"], 2)

            def serve(s, k, more=True):
                if more:
                    gather(s + RING, k, after=s)
                scatter(s, k % 2)

            with pool.Fori(0, LOOP // RING - 1) as it:
                for k in range(RING):
                    serve(RING * it + k, k)
            for s in range(LOOP - RING, SLOTS):
                serve(s, s % RING, s + RING < SLOTS)
            pool.wait_ge(scat[0], 16 * ((SLOTS + 1) // 2))
            pool.wait_ge(scat[1], 16 * (SLOTS // 2))

        @block.tensor
        def _(pe):
            matmul = nc.tensor.matmul

            def keep_clock(n):
                for _ in range(n):
                    matmul(bank[3][:, 0:P], ident[:, :], ident[:, :], start=True, stop=True)

            def transpose_xn(g):
                pe.wait_ge(lns[0]["out"], GB * g + GB)
                for k in range(KD):
                    if not isinstance(g, int) or g > 0:
                        pe.wait_ge(S["a_gz"], KI * (g - 1) + k + 1)
                    for j in range(GB):
                        mm = nc.tensor.transpose(bank[k][:, j * P:(j + 1) * P], xnA[:, j, k * P:(k + 1) * P], ident[:, :])
                    mm.then_inc(S["a_transposed"], 1)

            def in_proj(g, c, first_col, to, done):
                lhs = [w[:, k, first_col + c * P:first_col + (c + 1) * P] for w in (inw_hi, inw_lo) for k in range(KD)]
                for k in range(2 * KD):
                    pe.wait_ge(S["a_xnT_hi"], KD * g + k % KD + 1)
                    matmul(to, lhs[k], xnT_hi[:, k % KD, :], start=(k == 0), stop=False)
                for k in range(KD):
                    pe.wait_ge(S["a_xnT_lo"], KD * g + k + 1)
                    mm = matmul(to, lhs[k], xnT_lo[:, k, :], start=False, stop=(k == KD - 1))
                mm.then_inc(done, 1)

            def x_part(g):
                for c in range(KI):
                    if not isinstance(g, int) or g > 0:
                        pe.wait_ge(S["a_abs"], GB * (g - 1) + c + 1)
                    in_proj(g, c, 0, bank[2 + c][:, :], S["a_x_done"])

            def z_part(g, resid_before=True):
                first = isinstance(g, int) and g == 0
                for c in range(KI):
                    if c >= 2 and not first:
                        pe.wait_ge(S["a_taps"], taps_done(g, c - 2))
                    elif resid_before and not first:
                        pe.wait_ge(S["a_resid"], 2 * (g - 2) + c + 1)
                    in_proj(g, c, DI, z_bank(g, c)[:, :], S["a_z_done"])

            def x_proj(g, par):
                if isinstance(g, int) and g == 0:
                    pe.wait_ge(S["a_gz"], KI)
                for c in range(KI):
                    pe.wait_ge(S["a_xs"], KI * g + c + 1)
                    mm = matmul(bank[6][0:NS, :], xpw_sb[:, c, :], xs[par][:, c, :], start=(c == 0), stop=(c == KI - 1))
                mm.then_inc(S["a_xp_done"], 1)

            def dt_proj(g):
                pe.wait_ge(S["a_b_hi"], 2 * g + 2)
                pe.wait_ge(S["a_b_lo"], g + 1)
                if isinstance(g, int) and g == 0:
                    pe.wait_ge(S["dt_split"], 1)
                    pe.wait_ge(S["ld_outw"], 16)
                for j in range(GB):
                    if j < 2:
                        pe.wait_ge(S["a_gz"], KI * g + j + 3)
                    tokens = b_stack[:, j * P:(j + 1) * P]
                    matmul(bank[2 + j][:, :], tokens, dtw_stack[:, 0:DI], start=True, stop=True).then_inc(S["a_dt_done"], 1)
                for j in range(GB):
                    mm = matmul(bank[6][:, 2 * j:2 * j + 2], b_stack[:, j * P:(j + 1) * P], dtw_stack[:, DI:DI + 2],
                                start=True, stop=True)
                mm.then_inc(S["a_dt_done"], 1)

            def alpha_rows(g):
                pe.wait_ge(S["a_alpha"], g + 1)
                for j in range(GB):
                    mm = matmul(bank[7][:, j * P:(j + 1) * P], alpha[:, j:j + 1].broadcast_to([P, P]), ident[:, :],
                                start=True, stop=True)
                mm.then_inc(S["a_alpha_rows"], 1)

            def out_proj(g):
                pe.wait_ge(S["a_gated"], KI * g + KI)
                for j in range(GB):
                    for c in range(KI):
                        mm = matmul(bank[j // 2][:, (j % 2) * D:(j % 2) * D + D],
                                    yv[:, c, j * P:(j + 1) * P], outw_sb[:, c, :], start=(c == 0), stop=(c == KI - 1))
                    mm.then_inc(S["a_out_done"], 1)

            def fold_wk():
                pe.wait_ge(S["ld_wb"], 16 * 4)
                pe.wait_ge(S["a_u"], KI * (G - 1))
                for k in range(KD):
                    for e in range(KD):
                        matmul(bank[7][:, k * C:(k + 1) * C], wq_sb[:, e, k * P:(k + 1) * P], wk_sb[:, e, :],
                               start=(e == 0), stop=(e == KD - 1))
                for e in range(KD):
                    matmul(bank[7][:, 2 * C:2 * C + 1], wk_sb[:, e, :], bq_sb[:, e:e + 1],
                           start=(e == 0), stop=(e == KD - 1))
                for k in range(KD):
                    for e in range(KD):
                        matmul(bank[7][:, 2 * C + 2 + k:2 * C + 3 + k], wq_sb[:, e, k * P:(k + 1) * P],
                               bk_sb[:, e:e + 1], start=(e == 0), stop=(e == KD - 1))
                for e in range(KD):
                    mm = matmul(bank[7][:, 2 * C + 4:2 * C + 5], bq_sb[:, e:e + 1].broadcast_to([P, P]),
                                bk_sb[:, e:e + 1], start=(e == 0), stop=(e == KD - 1))
                mm.then_inc(S["b_prep"], 1)

            def step_a(g, par, has_prev=True, has_next=True):
                x_proj(g, par)
                if has_next:
                    transpose_xn(g + 1)
                else:
                    fold_wk()
                dt_proj(g)
                if has_next:
                    x_part(g + 1)
                if has_prev:
                    out_proj(g - 1)
                if not has_next:
                    pe.wait_ge(S["b_prep_copied"], 1)
                alpha_rows(g)
                if has_next:
                    z_part(g + 1, has_prev)

            pe.wait_ge(S["ident_set"], 2)
            keep_clock(12)
            transpose_xn(0)
            pe.wait_ge(S["inw_hi_set"], 1)
            pe.wait_ge(S["inw_lo_set"], 1)
            x_part(0)
            z_part(0)
            step_a(0, 0, has_prev=False)
            with pe.Fori(0, (G - 4) // 2) as it:
                for k in range(2):
                    step_a(2 * it + k + 1, (k + 1) % 2)
            step_a(G - 3, 1)
            step_a(G - 2, 0)
            step_a(G - 1, 1, has_next=False)

            def transpose_b(src, done):
                for k in range(KD):
                    for j in range(GB):
                        mm = nc.tensor.transpose(bank[k][:, j * P:(j + 1) * P], src[:, j, k * P:(k + 1) * P], ident[:, :])
                    mm.then_inc(done, 1)

            def xn_t(n):
                pe.wait_ge(lns[1]["out"], GB * n + GB)
                transpose_b(xnB, S["b_transposed"])

            def xl_t(n, n_xn):
                pe.wait_ge(lns[2]["out"], GB * n + GB)
                pe.wait_ge(S["b_xnT_ready"], KD * n_xn)
                transpose_b(xlB, S["b_xl_transposed"])

            def q_part(n):
                pe.wait_ge(S["b_xnT_ready"], KD * n + KD)
                for k in range(KD):
                    mm = matmul(bank[4][:, :], wqk[:, k, :], xnTB[:, k, :], start=(k == 0), stop=(k == KD - 1))
                mm.then_inc(S["b_q_done"], 1)

            def scores(n):
                pe.wait_ge(S["b_q_ready"], n + 1)
                pe.wait_ge(S["ld_ct"], 16 * n + 16)
                for j in range(GB):
                    mm = matmul(bank[5][:, j * P:(j + 1) * P], B["q"][:, j * P:(j + 1) * P],
                                cT_sb[:, j * P:(j + 1) * P], start=True, stop=True)
                mm.then_inc(S["b_scores"], 1)

            def probs_t(i):
                pe.wait_ge(S["b_probs"], GB * i + GB)
                for j in range(GB):
                    mm = nc.tensor.transpose(bank[6][:, j * P:(j + 1) * P], pr[:, j, :], ident[:, :])
                mm.then_inc(S["b_prT_done"], 1)

            def g_part(i, stages):
                pe.wait_ge(S["b_prT_ready"], i + 1)
                pe.wait_ge(S["ld_c"], 16 * i + 16)
                pe.wait_ge(S["b_stage_copied"], stages)
                for j in range(GB):
                    mm = matmul(bank[7][:, j * P:(j + 1) * P], c_sb[:, j, :], B["prT"][:, j * P:(j + 1) * P],
                                start=True, stop=True)
                mm.then_inc(S["b_g_done"], 1)

            def v_part(i):
                pe.wait_ge(S["b_gT_ready"], i + 1)
                for j in range(GB):
                    if j % 2 == 0 and (not isinstance(i, int) or i > 0):
                        pe.wait_ge(S["b_x2"], GB * (i - 1) + j + 2)
                    matmul(bank[2 + j // 2][:, (j % 2) * D:(j % 2) * D + D], B["gT"][:, j * P:(j + 1) * P],
                           B["wv"], start=True, stop=True).then_inc(S["b_v_done"], 1)

            def stage(n, with_shift=True, with_aff=True):
                if with_shift:
                    pe.wait_ge(S["b_xnT_ready"], KD * n + KD)
                    for j in range(GB):
                        for k in range(KD):
                            mm = matmul(bank[7][:, GB * E + j:GB * E + j + 1], xnTB[:, k, j * P:(j + 1) * P],
                                        bk_proj[:, k:k + 1], start=(k == 0), stop=(k == KD - 1))
                if with_aff:
                    pe.wait_ge(S["b_xlT_ready"], KD * (n - 3) + KD)
                    for j in range(GB):
                        for k in range(KD):
                            mm = matmul(bank[7][:, j * E:(j + 1) * E], xlTB[:, k, j * P:(j + 1) * P],
                                        cent_sb[:, k, :], start=(k == 0), stop=(k == KD - 1))
                mm.then_inc(S["b_stage_done"], 1)

            pe.wait_ge(S["a_resid"], 2 * (G - 1))
            xn_t(0)
            q_part(0)
            pe.wait_ge(S["a_u"], KI * G)
            stage(0, with_aff=False)
            scores(0)
            xn_t(1)
            q_part(1)
            out_proj(G - 1)
            pe.wait_ge(S["b_stage_copied"], 1)
            stage(1, with_aff=False)
            pe.wait_ge(S["a_resid"], 2 * G)

            def step_b(i, has_prev=True, has_next=True, has_xn=True):
                probs_t(i)
                if has_next:
                    scores(i + 1)
                if has_xn:
                    xn_t(i + 2)
                g_part(i, i + 2)
                if has_prev and has_next:
                    xl_t(i - 1, i + 3 if has_xn else G)
                v_part(i)
                if has_prev and not has_next:
                    xl_t(i - 1, G)
                if has_xn:
                    q_part(i + 2)
                stage(i + 2, with_shift=has_xn, with_aff=has_prev)

            step_b(0, has_prev=False)
            with pe.Fori(1, G - 3) as i:
                step_b(i)
            step_b(G - 3)
            step_b(G - 2, has_xn=False)
            step_b(G - 1, has_next=False, has_xn=False)
            pe.wait_ge(S["b_xlT_ready"], KD * (G - 1))
            xl_t(G - 1, G)
            pe.wait_ge(S["b_stage_copied"], G + 2)
            stage(G + 2, with_shift=False)

            keep_clock(10)
            pe.wait_ge(S["c_step"], 5)
            matmul(bank[1][:, 0:TILES * E], ones[:, :], Rm["hot"], start=True, stop=True).then_inc(S["c_prefix"], 1)
            matmul(bank[0][:, 0:TILES * E], before[:, :], Rm["hot"], start=True, stop=True).then_inc(S["c_prefix"], 1)
            keep_clock(26)
            for j in range(TILES):
                pe.wait_ge(S["c_slots"], j // GB + 1)
                pe.wait_ge(S["c_hi_alpha"], j // GB + 1)
                mm = matmul(bank[2][:, 0:2 * SP_], split(Cm["lo_hot"], TILES)[:, j, :],
                            split(Cm["hi_val"], TILES)[:, j, :], start=(j == 0), stop=(j == TILES - 1))
            mm.then_inc(S["c_prefix"], 1)

            def xT(s, k, turn):
                pe.wait_ge(gath[k], 16 * turn + 16)
                for d in range(KD):
                    mm = nc.tensor.transpose(bank[0][:, d * P:(d + 1) * P], slot_rows[:, k, d * P:(d + 1) * P], ident[:, :])
                mm.then_inc(S["d_xT_done"], 1)

            def hidden(s, par):
                pe.wait_ge(S["d_w1_copied"], s + 1)
                pe.wait_ge(S["d_xT_ready"], KD * s + KD)
                for half in range(2):
                    for f in range(KF // 2):
                        at = (half * KF // 2 + f) * P
                        for k in range(KD):
                            mm = matmul(bank[2 + 2 * par + half][:, f * P:(f + 1) * P],
                                        w1_now[par][:, k * F + at:k * F + at + P], xT_d[:, k, :],
                                        start=(k == 0), stop=(k == KD - 1))
                    mm.then_inc(S["d_h_done"], 1)

            def y_part(s, par):
                if not isinstance(s, int) or s > 0:
                    pe.wait_ge(S["d_yb"], s)
                for half in range(2):
                    pe.wait_ge(S["d_hT_lo"], 2 * s + half + 1)
                    pe.wait_ge(S["d_w2_lo"], 2 * s + half + 1)
                    for f in range(half * KF // 2, (half + 1) * KF // 2):
                        matmul(bank[6][:, 0:D], hT_hi[par][:, f, :], w2_hi[:, f, :], start=(f == 0), stop=False)
                        matmul(bank[6][:, 0:D], hT_hi[par][:, f, :], w2_lo[:, f, :], start=False, stop=False)
                        mm = matmul(bank[6][:, 0:D], hT_lo[par][:, f, :], w2_hi[:, f, :], start=False, stop=(f == KF - 1))
                    mm.then_inc(S["d_y_half"] if half == 0 else S["d_y_done"], 1)

            def slot(s, k, turn, ahead=2):
                if ahead > 0:
                    hidden(s + 1, (k + 1) % 2)
                if ahead > 1:
                    xT(s + 2, (k + 2) % RING, turn)
                y_part(s, k % 2)

            keep_clock(28)
            pe.wait_ge(S["c_map"], 2)
            xT(0, 0, 0)
            keep_clock(4)
            hidden(0, 0)
            xT(1, 1, 0)
            for s in range(PEEL):
                slot(s, s, (s + 2) // RING)
            with pe.Fori(0, (LOOP - PEEL) // RING) as it:
                for k in range(RING):
                    slot(RING * it + k + PEEL, k, it + 1 + (k + 2) // RING)
            for s in range(LOOP, SLOTS):
                slot(s, s % RING, (s + 2) // RING, ahead=min(2, SLOTS - 1 - s))

        @block.scalar
        def _(act):
            act_ = nc.scalar.activation
            act.dma_start(inw_raw, in_w_t.rearrange("(k p) n -> p k n", p=P)).then_inc(S["ld_inw"], 16)

            def copy_xnT(g):
                for k in range(KD):
                    act.wait_ge(S["a_transposed"], KD * g + k + 1)
                    act_(xnT_hi[:, k, :], bank[k][:, :], ACT.Copy).then_inc(S["a_xnT_hi"], 1)

            def first_tap(g, chunks):
                for c in chunks:
                    act.wait_ge(S["a_x_done"], KI * g + c + 1)
                    act_(xc[:, c, :], bank[2 + c][:, :], ACT.Identity, bias=conv_b_sb[:, c:c + 1],
                         scale=conv_w_sb[:, c, 3:4]).then_inc(S["a_first_tap"], 1)

            def silu_x(g, par):
                for c in range(KI):
                    act.wait_ge(S["a_taps"], taps_done(g, c))
                    act_(xs[par][:, c, :], xc[:, c, :], ACT.Silu).then_inc(S["a_xs"], 1)

            def silu_z(g, par):
                for c in range(KI):
                    act.wait_ge(S["a_z_done"], KI * g + c + 1)
                    act_(gz[par][:, c, :], z_bank(g, c)[:, :], ACT.Silu).then_inc(S["a_gz"], 1)

            def copy_b(g):
                act.wait_ge(S["a_xp_done"], g + 1)
                act_(b_stack[0:NS, :], bank[6][0:NS, :], ACT.Copy).then_inc(S["a_b_hi"], 1)
                act.wait_ge(S["a_b_hi"], 2 * g + 1)
                act_(b_stack[64:64 + NS, :], b_stack[0:NS, :], ACT.Copy).then_inc(S["a_b_hi"], 1)

            def softplus_exp(g):
                for j in range(GB):
                    act.wait_ge(S["a_dt_done"], (GB + 1) * g + j + 1)
                    act_(sp[:, j, :], bank[2 + j][:, :], ACT.Abs, accum_out=abs_sum[:, j:j + 1]).then_inc(S["a_abs"], 1)
                for j in range(GB):
                    act.wait_ge(S["a_abs"], GB * g + j + 1)
                    act_(sp[:, j, :], sp[:, j, :], ACT.Exp, scale=-1.0).then_inc(S["a_exp"], 1)

            def softplus_ln(g):
                for j in range(GB):
                    act.wait_ge(S["a_exp"], GB * g + j + 1)
                    act_(sp[:, j, :], sp[:, j, :], ACT.Ln, bias=1.0, accum_out=ln_sum[:, j:j + 1]).then_inc(S["a_ln"], 1)

            def exp_alpha(g):
                act.wait_ge(S["a_sp_sum"], g + 1)
                act_(exp_a, sp_sum, ACT.Exp, scale=-1.0 / DI).then_inc(S["a_exp_a"], 1)

            def copy_alpha(g):
                act.wait_ge(S["a_alpha_rows"], g + 1)
                act_(alpha_all, bank[7][:, :], ACT.Copy).then_inc(S["a_alpha_copied"], 1)

            act.wait_ge(S["ld_inw"], 16)
            act_(inw_hi, inw_raw, ACT.Copy).then_inc(S["inw_hi_set"], 1)
            copy_xnT(0)
            act.wait_ge(S["ld_lane"], 16)
            first_tap(0, range(KI))
            silu_z(0, 0)
            silu_x(0, 0)
            act.wait_ge(S["fills_set"], 5)

            def copy_prep():
                act.wait_ge(S["b_prep"], 1)
                act_(B["wqk"], bank[7][:, 0:KD * C], ACT.Copy)
                act_(bk_proj, bank[7][:, 2 * C + 2:2 * C + 2 + KD], ACT.Copy)
                act_(bq_bk, bank[7][:, 2 * C + 4:2 * C + 5], ACT.Copy)
                act_(q_bias, bank[7][:, 2 * C:2 * C + 1], ACT.Copy).then_inc(S["b_prep_copied"], 1)

            def normalise(n):
                act.wait_ge(S["b_nbias"], n + 1)
                if not isinstance(n, int) or n > 0:
                    act.wait_ge(S["b_transposed"], KD * n)
                for j in range(GB):
                    act_(xnB[:, j, :], x_tile(n, j), ACT.Identity, bias=att_nbias[:, j:j + 1],
                         scale=ln_tmp[1][3][:, j:j + 1]).then_inc(lns[1]["out"], 1)

            def step_a(g, par, has_next=True):
                copy_b(g)
                if has_next:
                    copy_xnT(g + 1)
                softplus_exp(g)
                if not has_next:
                    copy_prep()
                if has_next:
                    first_tap(g + 1, (0, 1))
                softplus_ln(g)
                exp_alpha(g)
                if has_next:
                    first_tap(g + 1, (2, 3))
                else:
                    normalise(0)
                copy_alpha(g)
                if has_next:
                    silu_x(g + 1, 1 - par)
                    silu_z(g + 1, 1 - par)

            step_a(0, 0)
            with act.Fori(0, (G - 4) // 2) as it:
                for k in range(2):
                    step_a(2 * it + k + 1, (k + 1) % 2)
            step_a(G - 3, 1)
            step_a(G - 2, 0)
            step_a(G - 1, 1, has_next=False)

            def copy_xn_t(n):
                for k in range(KD):
                    act.wait_ge(S["b_transposed"], KD * n + k + 1)
                    act_(xnTB[:, k, :], bank[k][:, :], ACT.Copy).then_inc(S["b_xnT_ready"], 1)

            def copy_xl_t(n):
                for k in range(KD):
                    act.wait_ge(S["b_xl_transposed"], KD * n + k + 1)
                    act_(xlTB[:, k, :], bank[k][:, :], ACT.Copy).then_inc(S["b_xlT_ready"], 1)

            def copy_q(n):
                act.wait_ge(S["b_q_done"], n + 1)
                act_(B["q"], bank[4][:, :], ACT.Identity, bias=q_bias).then_inc(S["b_q_ready"], 1)

            def exp_scores(n):
                act.wait_ge(S["b_neg"], n + 1)
                for j in range(GB):
                    act_(pr[:, j, :], bank[5][:, j * P:(j + 1) * P], ACT.Exp, bias=att_neg[:, j:j + 1],
                         accum_out=att_sum[:, j:j + 1]).then_inc(S["b_probs"], 1)

            def xhat(i):
                act.wait_ge(S["b_xhat_nbias"], i + 1)
                if not isinstance(i, int) or i > 0:
                    act.wait_ge(S["b_rows_out"], 16 * i)
                for j in range(GB):
                    act_(row[:, j, 0, :], x_tile(i, j), ACT.Identity, bias=xhat_nbias[:, j:j + 1],
                         scale=ln_tmp[2][3][:, GB + j:GB + j + 1]).then_inc(S["b_xhat"], 1)

            def copy_prT(i):
                act.wait_ge(S["b_prT_done"], i + 1)
                act_(B["prT"], bank[6][:, :], ACT.Copy).then_inc(S["b_prT_ready"], 1)

            def copy_gT(i):
                act.wait_ge(S["b_g_done"], i + 1)
                act_(B["gT"], bank[7][:, :], ACT.Copy).then_inc(S["b_gT_ready"], 1)

            copy_xn_t(0)
            act.wait_ge(S["b_prep_copied"], 1)
            copy_q(0)
            normalise(1)
            copy_xn_t(1)
            copy_q(1)
            exp_scores(0)
            normalise(2)

            def step_b(i, has_prev=True, has_next=True, has_xn=True, has_stats=True):
                copy_prT(i)
                if has_xn:
                    copy_xn_t(i + 2)
                copy_gT(i)
                if has_next:
                    exp_scores(i + 1)
                if has_prev and has_next:
                    copy_xl_t(i - 1)
                    xhat(i - 1)
                elif has_prev:
                    xhat(i - 1)
                    copy_xl_t(i - 1)
                if has_stats:
                    normalise(i + 3)
                if has_xn:
                    copy_q(i + 2)

            step_b(0, has_prev=False)
            with act.Fori(1, G - 3) as i:
                step_b(i)
            step_b(G - 3, has_stats=False)
            step_b(G - 2, has_xn=False, has_stats=False)
            step_b(G - 1, has_next=False, has_xn=False, has_stats=False)
            copy_xl_t(G - 1)
            xhat(G - 1)

            act.wait_ge(S["c_step"], 1)
            act_(Rm["ealpha"], Rm["max"], ACT.Exp, scale=-1.0).then_inc(S["c_ealpha"], 1)

            def copy_w1(s, par, e):
                if not isinstance(s, int) or s > 1:
                    act.wait_ge(S["d_h_done"], 2 * (s - 2) + 2)
                act_(w1_now[par], w1_sb[:, bass.ds(e * (KD * F), KD * F)], ACT.Copy).then_inc(S["d_w1_copied"], 1)

            def relu_lo(s, par, e):
                act.wait_ge(S["d_h_done"], 2 * s + 1)
                if not isinstance(s, int) or s > 0:
                    act.wait_ge(S["d_hT_lo"], 2 * (s - 1) + 1)
                for f in range(4):
                    act_(hT_d[:, f, :], bank[2 + 2 * par][:, f * P:(f + 1) * P], ACT.Relu,
                         bias=L["b1"][:, bass.ds(e * KF + f, 1)]).then_inc(S["d_hT_act"], 1)

            def round_hT(s, par, half):
                act.wait_ge(S["d_hT_dve"] if half else S["d_hT_act"], 4 * s + 4)
                act_(hT_hi[par][:, 4 * half:4 * half + 4, :], hT_d[:, 4 * half:4 * half + 4, :], ACT.Copy) \
                    .then_inc(S["d_hT_hi"], 1)

            def round_w2(s, half, e):
                if not isinstance(s, int) or s > 0:
                    act.wait_ge(S["d_y_done"] if half else S["d_y_half"], s)
                act_(w2_hi[:, 4 * half:4 * half + 4, :], split(w2_sb[:, bass.ds(e * (KF * D) + half * 4 * D, 4 * D)], 4),
                     ACT.Copy).then_inc(S["d_w2_hi"], 1)

            def prepare(s, par, e, e_next=None):
                relu_lo(s, par, e)
                round_hT(s, par, 0)
                if e_next is not None:
                    copy_w1(s + 1, 1 - par, e_next)
                round_w2(s, 0, e)
                round_hT(s, par, 1)
                round_w2(s, 1, e)

            act.wait_ge(S["ld_w1"], 16 * E)
            act.wait_ge(S["c_map"], 1)
            act.wait_ge(S["c_experts"], 1)
            expert = Experts(act, 0)
            copy_w1(0, 0, expert(0))
            copy_w1(1, 1, expert(1))
            act.wait_ge(S["ld_w2"], 16 * E)
            act.wait_ge(S["b_rows_out"], 16 * G)
            round_w2(0, 0, expert(0))
            round_w2(0, 1, expert(0))
            relu_lo(0, 0, expert(0))
            round_hT(0, 0, 0)
            round_hT(0, 0, 1)
            for s in range(1, PEEL):
                prepare(s, s % 2, expert(s), expert(s + 1))
            with act.Fori(0, (LOOP - PEEL) // RING) as it:
                expert = Experts(act, RING * it + PEEL)
                for k in range(RING):
                    prepare(RING * it + k + PEEL, k % 2, expert(k), expert(k + 1))
            expert = Experts(act, LOOP)
            for s in range(LOOP, SLOTS):
                prepare(s, s % 2, expert(s - LOOP), expert(s + 1 - LOOP) if s + 1 < SLOTS else None)

        @block.vector
        def _(dve):
            v = nc.vector
            stt = nc.vector.scalar_tensor_tensor

            def ln_out(g):
                dve.wait_ge(lns[0]["rstd"], g + 1)
                ln_apply(dve, 0, g, ln_tmp[0][3], lambda j: x_tile(g, j), lambda j: xnA[:, j, :], lns[0]["out"])

            def xnT_rest(g):
                for k in range(KD):
                    dve.wait_ge(S["a_xnT_hi"], KD * g + k + 1)
                    v.tensor_tensor(xnT_lo[:, k, :], bank[k][:, :], xnT_hi[:, k, :], ALU.subtract) \
                        .then_inc(S["a_xnT_lo"], 1)

            def b_rest(g):
                dve.wait_ge(S["a_b_hi"], 2 * g + 1)
                v.tensor_tensor(b_stack[32:32 + NS, :], bank[6][0:NS, :], b_stack[0:NS, :], ALU.subtract) \
                    .then_inc(S["a_b_lo"], 1)

            def conv(g, chunks):
                for tap in (1, 2, 3):
                    for c in chunks:
                        if tap == 1:
                            dve.wait_ge(S["a_first_tap"], KI * g + c + 1)
                        else:
                            dve.wait_ge(S["a_taps"], taps_done(g, c, tap - 1))
                        late = split(xc[:, c, :], GB)[:, :, tap:T]
                        stt(late, split(bank[2 + c][:, :], GB)[:, :, 0:T - tap], conv_w_sb[:, c, 3 - tap:4 - tap], late,
                            ALU.mult, ALU.add).then_inc(S["a_taps"], 1)

            def relu_sums(g):
                dve.wait_ge(S["a_dt_done"], (GB + 1) * g + GB + 1)
                dve.wait_ge(S["a_abs"], GB * g + GB)
                v.tensor_tensor(twice_relu, abs_sum, bank[6][:, 0:2 * GB:2], ALU.add).then_inc(S["a_twice_relu"], 1)

            def alphas(g):
                dve.wait_ge(S["a_twice_relu"], g + 1)
                dve.wait_ge(S["a_ln"], GB * g + GB)
                stt(sp_sum, twice_relu, 0.5, ln_sum, ALU.mult, ALU.add).then_inc(S["a_sp_sum"], 1)
                dve.wait_ge(S["a_exp_a"], g + 1)
                v.tensor_scalar(exp_a1, exp_a, 1.0, None, ALU.add).then_inc(S["a_exp_a1"], 1)
                dve.wait_ge(S["a_exp_a1"], g + 1)
                v.reciprocal(alpha, exp_a1).then_inc(S["a_alpha"], 1)

            def scan_chunk(g, c):
                dve.wait_ge(S["a_u"], KI * g + c + 1)
                v.tensor_tensor_scan(uu[:, c, :], alpha_all, uu[:, c, :], 0.0, ALU.mult, ALU.add).then_inc(S["a_scan"], 1)

            def y_chunk(g, par, c):
                dve.wait_ge(S["a_scan"], KI * g + c + 1)
                stt(yv[:, c, :], uu[:, c, :], neg_d[:, c:c + 1], xs[par][:, c, :], ALU.mult, ALU.add) \
                    .then_inc(S["a_y"], 1)

            def recurrence(g, par):
                dve.wait_ge(S["a_alpha_copied"], g + 1)
                v.memset(split(alpha_all, GB)[:, :, 0:1], 0.0).then_inc(S["a_alpha_zeroed"], 1)
                for c in range(KI):
                    stt(uu[:, c, :], bank[7][:, :], 1.0, xs[par][:, c, :], ALU.subtract, ALU.mult).then_inc(S["a_u"], 1)
                if isinstance(g, int) and g == G - 1:
                    scale_and_bias(1)
                dve.wait_ge(S["a_alpha_zeroed"], g + 1)
                scan_chunk(g, 0)
                scan_chunk(g, 1)
                y_chunk(g, par, 0)
                scan_chunk(g, 2)
                y_chunk(g, par, 1)

            def recurrence_rest(g, par):
                scan_chunk(g, 3)
                y_chunk(g, par, 2)
                y_chunk(g, par, 3)

            def resid(g):
                for half in range(2):
                    dve.wait_ge(S["a_out_done"], GB * g + 2 * half + 2)
                    dst = x_flat[:, bass.ds(g * (GB * D) + half * 2 * D, 2 * D)]
                    v.tensor_tensor(dst, bank[half][:, :], dst, ALU.add).then_inc(S["a_resid"], 1)

            def scale_and_bias(n):
                dve.wait_ge(lns[1]["rstd"], n + 1)
                stt(att_nbias, ln_tmp[1][1][:, :, 0], -1.0, ln_tmp[1][3], ALU.mult, ALU.mult).then_inc(S["b_nbias"], 1)

            dve.wait_ge(S["ld_x0"], 16)
            ln_stats(dve, 0, 0)
            ln_out(0)
            dve.wait_ge(S["inw_hi_set"], 1)
            v.tensor_tensor(inw_lo, inw_raw, inw_hi, ALU.subtract).then_inc(S["inw_lo_set"], 1)
            xnT_rest(0)
            dve.wait_ge(S["ld_x1"], 16)
            ln_stats(dve, 0, 1)
            dve.wait_ge(S["ld_lane"], 16)
            v.tensor_scalar(neg_d, d_sb, -1.0, None, ALU.mult).then_inc(S["neg_d_set"], 1)
            conv(0, (0, 1))
            conv(0, (2, 3))
            ln_out(1)
            dve.wait_ge(S["ld_dt"], 16 * 6)
            v.tensor_reduce(dtw_raw[:, DI:DI + 1], dtw_raw[:, 0:DI], X, ALU.add).then_inc(S["dt_rowsum"], 1)
            dve.wait_ge(S["dt_rowsum"], 1)
            v.tensor_copy(dtw_raw[:, DI + 1:DI + 2], dtw_raw[:, DI:DI + 1]).then_inc(S["dt_rowsum"], 1)
            dve.wait_ge(S["dt_rowsum"], 2)
            v.tensor_copy(dtw_round, dtw_raw).then_inc(S["dt_rounded"], 1)
            dve.wait_ge(S["dt_rounded"], 1)
            v.tensor_copy(dtw_stack[0:64, :], dtw_raw[0:64, :])
            v.tensor_tensor(dtw_stack[64:P, :], dtw_raw[64:P, :], dtw_round[64:P, :], ALU.subtract) \
                .then_inc(S["dt_split"], 1)
            dve.wait_ge(S["ld_x"], 16)
            dve.wait_ge(S["ident_set"], 2)
            dve.wait_ge(S["neg_d_set"], 1)

            def step_a(g, par, has_prev=True, has_next=True, stats=0):
                b_rest(g)
                if has_next:
                    xnT_rest(g + 1)
                if has_prev:
                    recurrence_rest(g - 1, 1 - par)
                if stats is not None:
                    ln_stats(dve, stats, g + 2 if stats == 0 else 0)
                if stats == 0:
                    ln_out(g + 2)
                relu_sums(g)
                if stats == 1:
                    scale_and_bias(0)
                    dve.wait_ge(S["a_resid"], 2 * 2)
                    ln_stats(dve, 1, 1)
                if has_next:
                    conv(g + 1, (0, 1))
                alphas(g)
                if has_prev:
                    resid(g - 1)
                if has_next:
                    conv(g + 1, (2, 3))
                recurrence(g, par)

            step_a(0, 0, has_prev=False)
            with dve.Fori(0, (G - 4) // 2) as it:
                for k in range(2):
                    step_a(2 * it + k + 1, (k + 1) % 2)
            step_a(G - 3, 1)
            step_a(G - 2, 0, stats=None)
            dve.wait_ge(S["a_resid"], 2)
            step_a(G - 1, 1, has_next=False, stats=1)
            recurrence_rest(G - 1, 1)

            def sums_rcp(i):
                dve.wait_ge(S["b_probs"], GB * i + GB)
                v.reciprocal(att_rcp, att_sum).then_inc(S["b_rcp"], 1)

            def score_max(n):
                dve.wait_ge(S["b_stage_copied"], n + 1)
                dve.wait_ge(S["b_scores"], n + 1)
                v.tensor_reduce(att_max, split(bank[5][:, :], GB), X, ALU.max).then_inc(S["b_max"], 1)
                dve.wait_ge(S["b_max"], n + 1)
                v.tensor_tensor(att_top, att_max, shift, ALU.add).then_inc(S["b_top"], 1)
                dve.wait_ge(S["b_top"], n + 1)
                v.tensor_tensor(att_neg, shift, att_top, ALU.subtract).then_inc(S["b_neg"], 1)

            def add_attn(i):
                dve.wait_ge(S["b_rcp"], i + 1)
                dve.wait_ge(S["b_xbv"], GB * i + GB)
                for j in range(GB):
                    dve.wait_ge(S["b_v_done"], GB * i + 2 * (j // 2) + 2)
                    stt(x_tile(i, j), bank[2 + j // 2][:, (j % 2) * D:(j % 2) * D + D], att_rcp[:, j:j + 1],
                        x_tile(i, j), ALU.mult, ALU.add).then_inc(S["b_x2"], 1)

            def copy_stage(n, with_shift=True, with_aff=True):
                dve.wait_ge(S["b_stage_done"], n + 1)
                if with_shift:
                    if not isinstance(n, int) or n > 0:
                        dve.wait_ge(S["b_neg"], n)
                    ins = v.tensor_scalar(shift, bank[7][:, GB * E:GB * E + GB], bq_bk, None, ALU.add)
                if with_aff:
                    ins = v.tensor_copy(affs[:, bass.ds((n - 3) * GB, GB), :], split(bank[7][:, 0:GB * E], GB))
                ins.then_inc(S["b_stage_copied"], 1)

            def normalised_twice(i):
                rstd = ln_tmp[2][3]
                if not isinstance(i, int) or i > 0:
                    dve.wait_ge(S["b_xl_transposed"], KD * i)
                    dve.wait_ge(S["b_base"], GB * i)
                dve.wait_ge(lns[2]["rstd"], i + 1)
                ln_apply(dve, 2, i, rstd[:, 0:GB], lambda j: x_tile(i, j), lambda j: xlB[:, j, :], lns[2]["out"])
                stt(xhat_nbias, ln_tmp[2][1][:, :, 0], -1.0, rstd[:, GB:2 * GB], ALU.mult, ALU.mult) \
                    .then_inc(S["b_xhat_nbias"], 1)

            dve.wait_ge(S["a_resid"], 2 * 3)
            ln_stats(dve, 1, 2)
            copy_stage(0, with_aff=False)
            score_max(0)
            scale_and_bias(2)
            resid(G - 1)
            dve.wait_ge(S["a_resid"], 2 * G)
            copy_stage(1, with_aff=False)

            def step_b(i, has_prev=True, has_next=True, has_xn=True, has_stats=True):
                sums_rcp(i)
                if has_next:
                    score_max(i + 1)
                if has_stats:
                    ln_stats(dve, 1, i + 3)
                add_attn(i)
                if has_stats:
                    scale_and_bias(i + 3)
                dve.wait_ge(S["b_x2"], GB * i + GB)
                ln_stats(dve, 2, i)
                copy_stage(i + 2, with_shift=has_xn, with_aff=has_prev)
                normalised_twice(i)

            step_b(0, has_prev=False)
            with dve.Fori(1, G - 3) as i:
                step_b(i)
            step_b(G - 3, has_stats=False)
            sums_rcp(G - 2)
            score_max(G - 1)
            add_attn(G - 2)
            dve.wait_ge(S["b_x2"], GB * (G - 1))
            ln_stats(dve, 2, G - 2)
            copy_stage(G, with_shift=False)
            sums_rcp(G - 1)
            add_attn(G - 1)
            normalised_twice(G - 2)
            dve.wait_ge(S["b_x2"], GB * G)
            dve.wait_ge(S["b_xhat_nbias"], G - 1)
            ln_stats(dve, 2, G - 1)
            normalised_twice(G - 1)
            copy_stage(G + 1, with_shift=False)
            copy_stage(G + 2, with_shift=False)

            steps = [0]

            def step(ins):
                ins.then_inc(S["c_step"], 1)
                steps[0] += 1
                dve.wait_ge(S["c_step"], steps[0])

            hot, tot = split(Rm["hot"], TILES), split(bank[1][:, 0:TILES * E], TILES)

            def over_e(ap):
                return ap.rearrange("p (t o) -> p t o", o=1).broadcast_to([P, TILES, E])

            def over_t(ap, n=TILES):
                return ap.rearrange("p (o e) -> p o e", o=1).broadcast_to([P, n, ap.shape[1]])

            dve.wait_ge(S["b_stage_copied"], G + 3)
            dve.wait_ge(S["b_base"], GB * G)
            dve.wait_ge(S["consts_set"], 5)
            step(v.tensor_reduce(Rm["max"], affs, X, ALU.max))
            step(v.tensor_tensor(split(Rm["eq"], TILES), affs, over_e(Rm["max"]), ALU.is_ge))
            step(v.tensor_tensor(split(Rm["cand"], TILES), split(Rm["eq"], TILES), over_t(Im["e8"]), ALU.mult))
            step(v.tensor_reduce(Rm["first"], split(Rm["cand"], TILES), X, ALU.min))
            step(v.tensor_tensor(hot, over_t(Im["e8"]), over_e(Rm["first"]), ALU.is_equal))
            dve.wait_ge(S["c_ealpha"], 1)
            step(v.tensor_scalar(Rm["ealpha"], Rm["ealpha"], 1.0, None, ALU.add))
            step(v.reciprocal(Rm["max"], Rm["ealpha"]))
            dve.wait_ge(S["c_prefix"], 1)
            cum = split(Rm["eq"], TILES)
            for e in range(E):
                ins = v.tensor_tensor_scan(cum[:, :, e], ones[:, 0:TILES], tot[:, :, e], 0.0, ALU.mult, ALU.add)
            step(ins)
            count = cum[:, TILES - 1, :]
            per_e = Rm["cand"].rearrange("p (e k) -> p e k", e=E)
            step(v.tensor_tensor(per_e, count.rearrange("p (e o) -> p e o", o=1).broadcast_to([P, E, TILES]),
                                 over_t(Im["k128"], E), ALU.is_gt))
            n_slots, ends, starts = (routing_tmp[:, k * E:(k + 1) * E] for k in range(3))
            step(v.tensor_reduce(n_slots, per_e, X, ALU.add))
            step(v.tensor_tensor_scan(ends, ones[:, 0:E], n_slots, 0.0, ALU.mult, ALU.add))
            step(v.tensor_tensor(starts, ends, n_slots, ALU.subtract))
            dve.wait_ge(S["c_prefix"], 2)
            step(v.tensor_tensor(cum, cum, tot, ALU.subtract))
            step(v.tensor_tensor(Rm["eq"], Rm["eq"], bank[0][:, 0:TILES * E], ALU.add))
            step(stt(cum, over_t(starts), float(P), cum, ALU.mult, ALU.add))
            step(v.tensor_tensor(cum, cum, hot, ALU.mult))
            step(v.tensor_reduce(Rm["pos"], cum, X, ALU.add))
            step(v.tensor_copy(pos_i, Rm["pos"]))
            step(v.tensor_scalar(hi_i, pos_i, 7, None, ALU.logical_shift_right))
            step(v.tensor_copy(Rm["hi"], hi_i))
            step(stt(Rm["lo"], Rm["hi"], -float(P), Rm["pos"], ALU.mult, ALU.add))
            lo_hot, hi_hot = split(Cm["lo_hot"], TILES), split(Cm["hi_hot"], TILES)
            hi_val = split(Cm["hi_val"], TILES)

            def wide(ap, n):
                m = ap.shape[1]
                return ap.rearrange("p (t o) -> p t o", o=1).broadcast_to([P, m, n])

            dve.wait_ge(S["b_xhat"], GB * G)
            for g in range(G):
                tiles = slice(g * GB, (g + 1) * GB)
                v.tensor_tensor(hi_hot[:, tiles], wide(Rm["hi"][:, tiles], SP_), over_t(Im["slot"], GB), ALU.is_equal) \
                    .then_inc(S["c_hi_hot"], 1)
                v.tensor_tensor(lo_hot[:, tiles], wide(Rm["lo"][:, tiles], P), over_t(Im["lane"], GB), ALU.is_equal)
                dve.wait_ge(S["c_hi_hot"], g + 1)
                v.tensor_tensor(hi_val[:, tiles, 0:SP_], hi_hot[:, tiles], wide(Im["tok"][:, tiles], SP_), ALU.mult) \
                    .then_inc(S["c_slots"], 1)
            ge = Rm["hot"].rearrange("p (s e) -> p s e", e=E)
            slot_e = Rm["slot_e"]
            for half, n in ((0, TILES), (TILES, SP_ - TILES)):
                step(v.tensor_tensor(ge[:, 0:n], Im["slot"][:, half:half + n].rearrange("p (s o) -> p s o", o=1)
                                     .broadcast_to([P, n, E]), over_t(ends, n), ALU.is_ge))
                step(v.tensor_reduce(slot_e[:, half:half + n], ge[:, 0:n], X, ALU.add))
            v.tensor_scalar(expert_i, slot_e[:, 0:SP_], float(E - 1), None, ALU.min).then_inc(S["c_experts"], 1)
            dve.wait_ge(S["c_prefix"], 3)
            vmap = Rm["cand"][:, 0:SP_]
            v.tensor_scalar(gather_i, bank[2][:, 0:SP_], -1.0, 0.0, ALU.add, ALU.max).then_inc(S["c_map"], 1)
            none = Rm["cand"][:, SP_:2 * SP_]
            step(v.tensor_copy(vmap, bank[2][:, 0:SP_]))
            step(v.tensor_copy(slot_alpha, bank[2][:, SP_:2 * SP_]))
            step(v.tensor_scalar(none, vmap, 0.0, float(2 * NB * T), ALU.is_equal, ALU.mult))
            step(stt(none, vmap, -1.0, none, ALU.add, ALU.add))
            v.tensor_copy(scatter_i, none).then_inc(S["c_map"], 1)
            dve.wait_ge(S["c_map"], 2)
            dve.wait_ge(S["c_experts"], 1)

            lng_f, lnb_f, b1_f = L["ln_g"], L["ln_b"], L["b1"]

            def affine(s, e):
                dve.wait_ge(S["d_xT_done"], s + 1)
                if not isinstance(s, int) or s > 0:
                    dve.wait_ge(S["d_h_done"], 2 * s)
                for k in range(KD):
                    v.tensor_scalar(xT_d[:, k, :], bank[0][:, k * P:(k + 1) * P], lng_f[:, bass.ds(e + k * E, 1)],
                                    lnb_f[:, bass.ds(e + k * E, 1)], ALU.mult, ALU.add).then_inc(S["d_xT_ready"], 1)

            def relu_hi(s, par, e):
                dve.wait_ge(S["d_h_done"], 2 * s + 2)
                if not isinstance(s, int) or s > 0:
                    dve.wait_ge(S["d_hT_lo"], 2 * s)
                for f in range(4, 8):
                    v.tensor_scalar(hT_d[:, f, :], bank[3 + 2 * par][:, (f - 4) * P:(f - 3) * P],
                                    b1_f[:, bass.ds(e * KF + f, 1)], 0.0, ALU.add, ALU.max).then_inc(S["d_hT_dve"], 1)

            def hT_rest(s, par, half):
                fs = slice(4 * half, 4 * half + 4)
                dve.wait_ge(S["d_hT_hi"], 2 * s + half + 1)
                v.tensor_tensor(hT_lo[par][:, fs, :], hT_d[:, fs, :], hT_hi[par][:, fs, :], ALU.subtract) \
                    .then_inc(S["d_hT_lo"], 1)

            def w2_rest(s, half, e):
                fs = slice(4 * half, 4 * half + 4)
                dve.wait_ge(S["d_w2_hi"], 2 * s + half + 1)
                v.tensor_tensor(w2_lo[:, fs, :], split(w2_sb[:, bass.ds(e * (KF * D) + half * 4 * D, 4 * D)], 4),
                                w2_hi[:, fs, :], ALU.subtract).then_inc(S["d_w2_lo"], 1)

            def add_b2(s, k, turn, e):
                dve.wait_ge(S["d_y_done"], s + 1)
                if not isinstance(s, int) or s > 1:
                    dve.wait_ge(scat[k], 16 * turn)
                v.tensor_tensor(o_d[:, k, :], bank[6][:, 0:D], Dm["b2"][:, bass.ds(e * D, D)], ALU.add).then_inc(S["d_yb"], 1)

            def gate(s, place, k):
                dve.wait_ge(S["d_yb"], s + 1)
                stt(o_d[:, k, :], o_d[:, k, :], slot_alpha[:, bass.ds(s, 1)], slot_rows[:, place, D:2 * D],
                    ALU.mult, ALU.add).then_inc(S["d_o_ready"], 1)

            def prepare(s, par, add_b2_last, e, e_next=None):
                if e_next is not None:
                    affine(s + 1, e_next)
                relu_hi(s, par, e)
                hT_rest(s, par, 0)
                w2_rest(s, 0, e)
                hT_rest(s, par, 1)
                add_b2_last()
                w2_rest(s, 1, e)

            def slot(s, k, turn, expert, ahead=2):
                def add_b2_now():
                    add_b2(s, k % 2, turn, expert(k))

                if ahead > 0:
                    prepare(s + 1, (k + 1) % 2, add_b2_now, expert(k + 1), expert(k + 2) if ahead > 1 else None)
                else:
                    add_b2_now()
                gate(s, k, k % 2)

            expert = Experts(dve, 0)
            affine(0, expert(0))
            dve.wait_ge(S["ld_w2"], 16 * E)
            w2_rest(0, 0, expert(0))
            w2_rest(0, 1, expert(0))
            affine(1, expert(1))
            relu_hi(0, 0, expert(0))
            hT_rest(0, 0, 0)
            hT_rest(0, 0, 1)
            dve.wait_ge(S["ld_b2"], 16)
            for s in range(PEEL):
                slot(s, s, s // 2, expert)
            with dve.Fori(0, (LOOP - PEEL) // RING) as it:
                expert = Experts(dve, RING * it + PEEL)
                for k in range(RING):
                    slot(RING * it + k + PEEL, k, 2 * it + 2 + k // 2, expert)
            expert = Experts(dve, LOOP)
            for s in range(LOOP, SLOTS):
                slot(s, s % RING, s // 2, expert, ahead=min(2, SLOTS - 1 - s))


def kernel(**inputs):
    import numpy as np
    import concourse.bacc as bacc
    from concourse.bass_utils import run_bass_kernel_spmd

    def t(name, axes=None):
        a = np.asarray(inputs[name])
        return np.ascontiguousarray(a if axes is None else np.transpose(a, axes))

    def lanes(a):
        return a.reshape(a.shape[0] // P, P, -1).transpose(1, 0, 2).reshape(P, -1)

    b1 = t("L0_ffn_b1")
    lane_w = np.concatenate([
        lanes(t("L0_attn_conv_w")), lanes(t("L0_attn_conv_b")), lanes(t("L0_attn_D_param")),
        lanes(t("L0_attn_x_proj_w", (1, 0))[:, :t("L0_attn_dt_proj_w").shape[1]]),
        lanes(t("L0_xattn_bq")), lanes(t("L0_xattn_bk")), lanes(t("L0_ffn_centroids", (1, 0))),
        lanes(t("L0_ffn_ln_g", (1, 0))), lanes(t("L0_ffn_ln_b", (1, 0))),
        b1.reshape(b1.shape[0], -1, P).transpose(2, 0, 1).reshape(P, -1)], axis=1)
    arrays = [
        ("x", t("x")), ("ctx", t("ctx_512")), ("ctx_t", t("ctx_512", (0, 2, 1))),
        ("in_w_t", t("L0_attn_in_proj_w", (1, 0))), ("dt_w_t", t("L0_attn_dt_proj_w", (1, 0))),
        ("dt_b", t("L0_attn_dt_proj_b")), ("out_w_t", t("L0_attn_out_proj_w", (1, 0))),
        ("wq_t", t("L0_xattn_Wq", (1, 0))), ("wk_t", t("L0_xattn_Wk", (1, 0))),
        ("wv", t("L0_xattn_Wv")), ("bv", t("L0_xattn_bv")), ("lane_w", lane_w),
        ("w1_t", t("L0_ffn_w1", (0, 2, 1))), ("w2_t", t("L0_ffn_w2", (0, 2, 1))), ("b2", t("L0_ffn_b2")),
    ]
    nc = bacc.Bacc("TRN2", target_bir_lowering=False, num_devices=1)
    feeds, args = {}, []
    for name, a in arrays:
        feeds[f"in_{name}"] = a
        args.append(nc.dram_tensor(f"in_{name}", a.shape, mybir.dt.from_np(a.dtype), kind="ExternalInput").ap())
    shape = inputs["x"].shape
    args.append(nc.dram_tensor("layer_out", shape, F32, kind="ExternalOutput").ap())
    decoder_program(nc, *args)
    got = run_bass_kernel_spmd(nc, [feeds], core_ids=[0])
    return got.results[0]["layer_out"]
```
